# Optimizing a Trainium2 kernel written in Bass

```python
import numpy as np
import jax
import jax.numpy as jnp

def _softmax(x, axis=-1):
    return jax.nn.softmax(x, axis=axis)

def _gelu(x):
    return jax.nn.gelu(x, approximate=True)

def _silu(x):
    return jax.nn.silu(x)

def _sigmoid(x):
    return jax.nn.sigmoid(x)

def _layernorm(x, axis=-1, eps=1e-05):
    m = jnp.mean(x, axis=axis, keepdims=True)
    v = jnp.var(x, axis=axis, keepdims=True)
    return (x - m) / jnp.sqrt(v + eps)

def _scatter_add(tgt, idx, src, axis=0):
    return tgt.at[idx].add(src)

def _segment_sum(src, seg, n):
    return jax.ops.segment_sum(src, seg, n)
kernel_name = 'mk_decoder_preln_d1_seqx_r8_83ed62'

def setup_inputs(seed: int=0):
    np.random.seed(seed)
    _w = jnp.asarray

    def _rec_inputs():
        import jax
        import jax.numpy as jnp
        _rk = jax.random.key(seed)
        x = 7.22e-05 + 1 * jax.random.normal(jax.random.fold_in(_rk, 1), (32, 100, 256), jnp.float32)
        _lenS = 100 - jax.random.randint(jax.random.fold_in(_rk, 7), (32,), 0, max(1, 100 // 4) + 1, jnp.int32)
        _lenS2 = 1444 - jax.random.randint(jax.random.fold_in(_rk, 8), (32,), 0, max(1, 1444 // 4) + 1, jnp.int32)
        _ctx_512P = jax.random.normal(jax.random.fold_in(_rk, 11), (32, 16, 64), jnp.float32)
        _ctx_512c = jax.random.dirichlet(jax.random.fold_in(_rk, 511), 0.3 * jnp.ones((16,), jnp.float32), (32, 1444))
        _ctx_512t = jnp.einsum('bsk,bkd->bsd', _ctx_512c, _ctx_512P)
        _ctx_512t = _ctx_512t * jax.lax.rsqrt(jnp.mean(jnp.square(_ctx_512t)) + 1e-12) * 0.953939
        ctx_512 = -0.000514642 + 1.00011 * (_ctx_512t + 0.3 * jax.random.normal(jax.random.fold_in(_rk, 611), (32, 1444, 64), jnp.float32))
        return (x, ctx_512)
    x, ctx_512 = _rec_inputs()

    def _L0_attn_setup():
        import jax, jax.numpy as jnp
        import numpy as np
        import math
        B, T = (4, 128)
        D_MODEL = 256
        HEAD_DIM = 64
        N_HEADS = 32
        N_KV = 8
        Q_MULT = N_HEADS // N_KV
        SLIDING_WINDOW = 128
        CAUSAL = True
        SM_SCALE = 1.0 / math.sqrt(HEAD_DIM)
        ROPE_THETA = 150000.0
        SCALING = 32.0
        NTK_ALPHA = 1.0
        NTK_BETA = 32.0
        ICL = 128

        def _rope_cos_sin(t_len):
            d_half = HEAD_DIM // 2
            freq = ROPE_THETA ** (np.arange(0, HEAD_DIM, 2, dtype=np.float32) / HEAD_DIM)
            concentration = 0.1 * math.log(SCALING) + 1.0
            low = d_half * math.log(ICL / (NTK_BETA * 2 * math.pi)) / math.log(ROPE_THETA)
            high = d_half * math.log(ICL / (NTK_ALPHA * 2 * math.pi)) / math.log(ROPE_THETA)
            interpolation = 1.0 / (SCALING * freq)
            extrapolation = 1.0 / freq
            ramp = np.clip((np.arange(d_half, dtype=np.float32) - low) / (high - low), 0.0, 1.0)
            mask = 1.0 - ramp
            inv_freq = interpolation * (1.0 - mask) + extrapolation * mask
            freqs = np.outer(np.arange(t_len, dtype=np.float32), inv_freq)
            return (jnp.asarray(np.cos(freqs) * concentration, jnp.float32), jnp.asarray(np.sin(freqs) * concentration, jnp.float32))

        def _apply_rope(x, cos, sin):
            x1, x2 = jnp.split(x, 2, axis=-1)
            return jnp.concatenate([x1 * cos - x2 * sin, x2 * cos + x1 * sin], axis=-1)
        key = jax.random.key(seed)
        ks = jax.random.split(key, 6)
        qkv_dim = HEAD_DIM * (N_HEADS + 2 * N_KV)
        return {'x': jax.random.normal(ks[0], (B, T, D_MODEL), jnp.float32), 'qkv_w': jax.random.normal(ks[1], (qkv_dim, D_MODEL), jnp.float32) * 0.02, 'qkv_b': jax.random.normal(ks[2], (qkv_dim,), jnp.float32) * 0.02, 'out_w': jax.random.normal(ks[3], (D_MODEL, N_HEADS * HEAD_DIM), jnp.float32) * 0.02, 'out_b': jax.random.normal(ks[4], (D_MODEL,), jnp.float32) * 0.02, 'sinks': jax.random.normal(ks[5], (N_HEADS,), jnp.float32) * (1.0 / math.sqrt(HEAD_DIM))}
    _L0_attn_all = _L0_attn_setup()
    _L0_attn_in = {k: v for k, v in _L0_attn_all.items() if k in ('qkv_w', 'qkv_b', 'out_w', 'out_b', 'sinks')}
    del _L0_attn_all

    def _L0_xattn_setup():
        import jax, jax.numpy as jnp
        import numpy as np
        B, S, H, NH, L = (2, 256, 256, 16, 64)
        HD = H // NH
        key = jax.random.key(seed)
        k1, k2, k3, k4, k5 = jax.random.split(key, 5)
        scale = 0.02
        return {'q': jax.random.normal(k1, (B, S, H), dtype=jnp.float32), 'latent_kv': jax.random.normal(k2, (B, S, L), dtype=jnp.float32), 'Wq': jax.random.normal(k3, (H, H), dtype=jnp.float32) * scale, 'Wkv_expand': jax.random.normal(k4, (2 * H, L), dtype=jnp.float32) * scale, 'Wout': jax.random.normal(k5, (H, H), dtype=jnp.float32) * scale}
    _L0_xattn_all = _L0_xattn_setup()
    _L0_xattn_in = {k: v for k, v in _L0_xattn_all.items() if k in ('Wq', 'Wkv_expand', 'Wout')}
    del _L0_xattn_all

    def _L0_ffn_setup():
        import jax, jax.numpy as jnp
        import numpy as np
        FP8_MAX = 448.0
        GLOBAL_DIV = 448.0 * 6.0

        def _fp8(x):
            return x.astype(jnp.float8_e4m3fn).astype(jnp.float32)

        def _reorder_quantize_x(x, idx):
            scale = jnp.max(jnp.abs(x)) / GLOBAL_DIV
            xr = (x / scale)[:, idx]
            scale_x = jnp.max(jnp.abs(xr), axis=1, keepdims=True) / FP8_MAX
            qx = _fp8(xr / scale_x)
            return (qx, scale_x, scale)

        def _qlinear(qx, scale_x, scale, W, idx, out_idx=None):
            Wr = W[:, idx]
            w_scale = jnp.max(jnp.abs(Wr), axis=1, keepdims=True) / FP8_MAX
            qw = _fp8(Wr / w_scale)
            y = qx * scale_x @ (qw * w_scale).T * scale
            if out_idx is not None:
                y = y[:, out_idx]
            return y
        key = jax.random.key(seed)
        ks = jax.random.split(key, 6)
        B, S, H, I = (2, 128, 256, 704)
        return {'x': jax.random.normal(ks[0], (B, S, H), jnp.float32), 'w_gate': jax.random.normal(ks[1], (I, H), jnp.float32) * 0.02, 'w_up': jax.random.normal(ks[2], (I, H), jnp.float32) * 0.02, 'w_down': jax.random.normal(ks[3], (H, I), jnp.float32) * 0.02, 'up_reorder_index': jax.random.permutation(ks[4], jnp.arange(H, dtype=jnp.int64)), 'down_reorder_index': jax.random.permutation(ks[5], jnp.arange(I, dtype=jnp.int64))}
    _L0_ffn_all = _L0_ffn_setup()
    _L0_ffn_in = {k: v for k, v in _L0_ffn_all.items() if k in ('w_gate', 'w_up', 'w_down', 'up_reorder_index', 'down_reorder_index')}
    del _L0_ffn_all
    return {'x': x, 'ctx_512': ctx_512, 'L0_attn_qkv_w': _L0_attn_in['qkv_w'], 'L0_attn_qkv_b': _L0_attn_in['qkv_b'], 'L0_attn_out_w': _L0_attn_in['out_w'], 'L0_attn_out_b': _L0_attn_in['out_b'], 'L0_attn_sinks': _L0_attn_in['sinks'], 'L0_xattn_Wq': _L0_xattn_in['Wq'], 'L0_xattn_Wkv_expand': _L0_xattn_in['Wkv_expand'], 'L0_xattn_Wout': _L0_xattn_in['Wout'], 'L0_ffn_w_gate': _L0_ffn_in['w_gate'], 'L0_ffn_w_up': _L0_ffn_in['w_up'], 'L0_ffn_w_down': _L0_ffn_in['w_down'], 'L0_ffn_up_reorder_index': _L0_ffn_in['up_reorder_index'], 'L0_ffn_down_reorder_index': _L0_ffn_in['down_reorder_index']}

def reference(x, ctx_512, L0_attn_qkv_w, L0_attn_qkv_b, L0_attn_out_w, L0_attn_out_b, L0_attn_sinks, L0_xattn_Wq, L0_xattn_Wkv_expand, L0_xattn_Wout, L0_ffn_w_gate, L0_ffn_w_up, L0_ffn_w_down, L0_ffn_up_reorder_index, L0_ffn_down_reorder_index):
    import jax
    import jax.numpy as jnp

    def _L0_attn_ref(x, qkv_w, qkv_b, out_w, out_b, sinks):
        import jax, jax.numpy as jnp
        import numpy as np
        import math
        B, T = (4, 128)
        D_MODEL = 256
        HEAD_DIM = 64
        N_HEADS = 32
        N_KV = 8
        Q_MULT = N_HEADS // N_KV
        SLIDING_WINDOW = 128
        CAUSAL = True
        SM_SCALE = 1.0 / math.sqrt(HEAD_DIM)
        ROPE_THETA = 150000.0
        SCALING = 32.0
        NTK_ALPHA = 1.0
        NTK_BETA = 32.0
        ICL = 128

        def _rope_cos_sin(t_len):
            d_half = HEAD_DIM // 2
            freq = ROPE_THETA ** (np.arange(0, HEAD_DIM, 2, dtype=np.float32) / HEAD_DIM)
            concentration = 0.1 * math.log(SCALING) + 1.0
            low = d_half * math.log(ICL / (NTK_BETA * 2 * math.pi)) / math.log(ROPE_THETA)
            high = d_half * math.log(ICL / (NTK_ALPHA * 2 * math.pi)) / math.log(ROPE_THETA)
            interpolation = 1.0 / (SCALING * freq)
            extrapolation = 1.0 / freq
            ramp = np.clip((np.arange(d_half, dtype=np.float32) - low) / (high - low), 0.0, 1.0)
            mask = 1.0 - ramp
            inv_freq = interpolation * (1.0 - mask) + extrapolation * mask
            freqs = np.outer(np.arange(t_len, dtype=np.float32), inv_freq)
            return (jnp.asarray(np.cos(freqs) * concentration, jnp.float32), jnp.asarray(np.sin(freqs) * concentration, jnp.float32))

        def _apply_rope(x, cos, sin):
            x1, x2 = jnp.split(x, 2, axis=-1)
            return jnp.concatenate([x1 * cos - x2 * sin, x2 * cos + x1 * sin], axis=-1)
        Bv, Tv, _ = x.shape
        qkv = x @ qkv_w.T + qkv_b
        q = qkv[..., :N_HEADS * HEAD_DIM].reshape(Bv, Tv, N_KV, Q_MULT, HEAD_DIM)
        k = qkv[..., N_HEADS * HEAD_DIM:(N_HEADS + N_KV) * HEAD_DIM].reshape(Bv, Tv, N_KV, HEAD_DIM)
        v = qkv[..., (N_HEADS + N_KV) * HEAD_DIM:].reshape(Bv, Tv, N_KV, HEAD_DIM)
        cos, sin = _rope_cos_sin(Tv)
        q = _apply_rope(q, cos[:, None, None, :], sin[:, None, None, :])
        k = _apply_rope(k, cos[:, None, :], sin[:, None, :])
        logits = jnp.einsum('bqhmd,bkhd->bhmqk', q, k) * SM_SCALE
        i = jnp.arange(Tv)[:, None]
        j = jnp.arange(Tv)[None, :]
        mask = jnp.zeros((Tv, Tv), dtype=bool)
        if CAUSAL:
            mask = mask | (j > i)
        if SLIDING_WINDOW > 0:
            mask = mask | (j <= i - SLIDING_WINDOW)
        logits = jnp.where(mask, -jnp.inf, logits)
        m = jnp.max(logits, axis=-1, keepdims=True)
        e = jnp.exp(logits - m)
        s = sinks.reshape(N_KV, Q_MULT)[None, :, :, None, None]
        exp_sink = jnp.exp(s - m)
        w = e / (jnp.sum(e, axis=-1, keepdims=True) + exp_sink)
        out = jnp.einsum('bhmqk,bkhd->bqhmd', w, v).reshape(Bv, Tv, N_HEADS * HEAD_DIM)
        return out @ out_w.T + out_b

    def _L0_xattn_ref(q, latent_kv, Wq, Wkv_expand, Wout):
        import jax, jax.numpy as jnp
        import numpy as np
        B, S, H, NH, L = (2, 256, 256, 16, 64)
        HD = H // NH
        b, sq, _ = q.shape
        sk = latent_kv.shape[1]
        qp = q @ Wq.T
        kv = latent_kv @ Wkv_expand.T
        k, v = jnp.split(kv, 2, axis=-1)
        qh = qp.reshape(b, sq, NH, HD).transpose(0, 2, 1, 3)
        kh = k.reshape(b, sk, NH, HD).transpose(0, 2, 1, 3)
        vh = v.reshape(b, sk, NH, HD).transpose(0, 2, 1, 3)
        inv_sqrt_d = 1.0 / jnp.sqrt(jnp.float32(HD))
        scores = jnp.einsum('bhqd,bhkd->bhqk', qh, kh) * inv_sqrt_d
        causal = jnp.tril(jnp.ones((sq, sk), dtype=bool))
        scores = jnp.where(causal, scores, jnp.finfo(scores.dtype).min)
        attn = jax.nn.softmax(scores, axis=-1)
        out = jnp.einsum('bhqk,bhkd->bhqd', attn, vh)
        out = out.transpose(0, 2, 1, 3).reshape(b, sq, H)
        return out @ Wout.T

    def _L0_ffn_ref(x, w_gate, w_up, w_down, up_reorder_index, down_reorder_index):
        import jax, jax.numpy as jnp
        import numpy as np
        FP8_MAX = 448.0
        GLOBAL_DIV = 448.0 * 6.0

        def _fp8(x):
            return x.astype(jnp.float8_e4m3fn).astype(jnp.float32)

        def _reorder_quantize_x(x, idx):
            scale = jnp.max(jnp.abs(x)) / GLOBAL_DIV
            xr = (x / scale)[:, idx]
            scale_x = jnp.max(jnp.abs(xr), axis=1, keepdims=True) / FP8_MAX
            qx = _fp8(xr / scale_x)
            return (qx, scale_x, scale)

        def _qlinear(qx, scale_x, scale, W, idx, out_idx=None):
            Wr = W[:, idx]
            w_scale = jnp.max(jnp.abs(Wr), axis=1, keepdims=True) / FP8_MAX
            qw = _fp8(Wr / w_scale)
            y = qx * scale_x @ (qw * w_scale).T * scale
            if out_idx is not None:
                y = y[:, out_idx]
            return y
        B, S, H = x.shape
        xf = x.reshape(B * S, H)
        qx, sx, sc = _reorder_quantize_x(xf, up_reorder_index)
        g = _qlinear(qx, sx, sc, w_gate, up_reorder_index, out_idx=down_reorder_index)
        u = _qlinear(qx, sx, sc, w_up, up_reorder_index, out_idx=down_reorder_index)
        t = jax.nn.silu(g) * u
        qt, st, sct = _reorder_quantize_x(t, down_reorder_index)
        y = _qlinear(qt, st, sct, w_down, down_reorder_index)
        return y.reshape(B, S, H)
    x = x + _L0_attn_ref(_layernorm(x, axis=-1), L0_attn_qkv_w, L0_attn_qkv_b, L0_attn_out_w, L0_attn_out_b, L0_attn_sinks)
    x = x + _L0_xattn_ref(_layernorm(x, axis=-1), ctx_512, L0_xattn_Wq, L0_xattn_Wkv_expand, L0_xattn_Wout)
    x = x + _L0_ffn_ref(_layernorm(x, axis=-1), L0_ffn_w_gate, L0_ffn_w_up, L0_ffn_w_down, L0_ffn_up_reorder_index, L0_ffn_down_reorder_index)
    return x

_drawn_inputs = setup_inputs


def setup_inputs(seed=0):
    import zlib

    import numpy as np

    out = dict(_drawn_inputs(seed))
    spreads = {}
    factors = {'L0_attn_qkv_b': 3.631,
     'L0_attn_out_b': 2.909,
     'L0_attn_sinks': 44.153,
     'L0_xattn_Wq': 64.0}
    for name, (base, spread) in spreads.items():
        noise = np.random.default_rng([zlib.crc32(name.encode()), seed]).standard_normal(out[name].shape)
        drawn = base * np.exp(spread * noise) if base else spread * noise
        out[name] = jnp.asarray(drawn.astype(out[name].dtype))
    for name, factor in factors.items():
        out[name] = (out[name] * factor).astype(out[name].dtype)
    return out
```

```python
from contextlib import ExitStack
import math

import numpy as np
import concourse.bass as bass
from concourse import mybir

F32, F16, BF16, I32 = mybir.dt.float32, mybir.dt.float16, mybir.dt.bfloat16, mybir.dt.int32
ALU, ACT, AX = mybir.AluOpType, mybir.ActivationFunctionType, mybir.AxisListType

P = 128
B, T, D = 32, 100, 256
G = 2
NG = B // G
N = G * T
CD = D // P
NH, NKV, HD = 32, 8, 64
QUADS = (NH + NKV) // 4
XH, XD, L = 16, 16, 64
F = 704
FC = -(-F // P)
FL = F - (FC - 1) * P
FH = F // 2
W = 96
XS = XD + 1
XVW = (XH - 1) * XS + W
VS = HD + 1
WS = 64.0
EPS = 1e-5
FP8_MAX = 448.0
SUB = 1.5 * 2.0 ** 14
NEG = -1e30
WIDE, NARROW = 3, 2
SLOTS = WIDE + NARROW
STAGES = "ABCD"

KINDS = {"a": (NH, 1.0 / math.sqrt(HD)), "c": (XH, 1.0 / math.sqrt(XD))}


QUAD_ORDER = [8, 9] + list(range(8))
GAP = None

UNITS = {
    "A": [(("load",), 1), (GAP, 2), (("ln", 1), 1), (("nrm", 1), 1), (("xT", 1), 1), (("qk", 0), 2), (("qk", 1), 2)]
         + [x for n in range(2, QUADS) for x in ((("split", n - 2), 0.5), (("qk", n), 2))]
         + [(("v", 0), 1), (("split", QUADS - 2), 0.5), (("v", 1), 1), (("split", QUADS - 1), 0.5), (("qload", 0), 0.5)],
    "B": [(("qload", 1), 0)] + [(("M", "a", 0, j), 1) for j in range(4)] + [(("mT", "a", 0, 0), 1), (GAP, 3)]
         + [((w, "a", 0, j), 1) for w, j in (("S", 0), ("S", 1), ("V", 0), ("S", 2), ("V", 1), ("OT", 0), ("S", 3), ("V", 2),
                                             ("OT", 1))]
         + [(("M", "a", 1, 0), 1), (("M", "a", 1, 1), 1), (("V", "a", 0, 3), 1), (("OT", "a", 0, 2), 1), (("M", "a", 1, 2), 1),
            (("M", "a", 1, 3), 1), (("OT", "a", 0, 3), 1), (("mT", "a", 1, 0), 1), (("Y", "a", 0, 0), 5)]
         + [((w, "a", 1, j), 1) for w, j in (("S", 0), ("S", 1), ("V", 0), ("S", 2), ("V", 1), ("OT", 0), ("S", 3), ("V", 2),
                                             ("OT", 1), ("V", 3), ("OT", 2), ("OT", 3))] + [(("Y", "a", 1, 0), 5)],
    "C": [(("cload",), 0), (("ln", 2), 1), (("nrm", 2), 1), (("xT", 2), 1), (("ctxT",), 0.5), (("xq",), 2), (("xk",), 1),
          (("xload",), 0.5), (("xv", 0), 0.5), (("xv", 1), 0.5), (GAP, 4)]
         + [(("M", "c", 0, 0), 1), (("M", "c", 0, 1), 1), (("mT", "c", 0, 0), 1), (("M", "c", 1, 0), 1), (("M", "c", 1, 1), 1), (GAP, 3)]
         + [((w, "c", 0, j), 1) for w, j in (("S", 0), ("V", 0), ("S", 1), ("V", 1))]
         + [(("mT", "c", 1, 0), 1), (("OT", "c", 0, 0), 0.5), (("Y", "c", 0, 0), 1), (GAP, 3)]
         + [((w, "c", 1, j), 1) for w, j in (("S", 0), ("V", 0), ("S", 1), ("V", 1))]
         + [(("OT", "c", 1, 0), 0.5), (("Y", "c", 1, 0), 1)],
    "D": [(("ln", 3), 1), (("nrm", 3), 2), (("y", 0), 1), (("y", 1), 1), (GAP, 1)]
         + [x for b in range(2) for x in ((("qT", b), 1), (("G", b), 1), (("U", b), 1), (("h", b), 3), (GAP, 2), (("hk", b), 2),
                                          (("tq", b), 2), (GAP, 2), (("tT", b), 1), (("D", b), 1))],
}
NARROW_TILES = ("xT", "qk", "v", "mT", "OT", "Y", "ctxT", "xq", "xk", "xv", "qT", "tT", "D")
WIDE_TILES = ("M", "S", "V", "G", "U")


def body_units(stages):
    placed = []
    for st in stages:
        total = sum(w for _, w in UNITS[st])
        at = 0.0
        for unit, w in UNITS[st]:
            if unit is not GAP:
                placed.append(((at + w / 2) / total, st, unit))
            at += w
    return [(st, unit) for _, st, unit in sorted(placed, key=lambda x: x[0])]


def bodies():
    full = NG - len(STAGES) + 1
    loops = full // 2
    out = []
    n = 0
    while n < NG + len(STAGES) - 1:
        live = [st for i, st in enumerate(STAGES) if 0 <= n - i < NG]
        if n >= len(STAGES) and len(live) == len(STAGES) and not any(b[0] == "loop0" for b in out):
            out += [("loop0", n, live), ("loop1", n + 1, live)]
            n += 2 * loops
        else:
            out.append((f"body{n}", n, live))
            n += 1
    return out, loops


Q_Y = [1, 2]
Q_T = [3, 4]

PREP_V0 = 2 + FC + CD + 4
PREP_N = [11] * (2 * FC) + [12] * CD
VBASE = [PREP_V0 + sum(PREP_N[:n]) for n in range(len(PREP_N))]
PREP_VALL = PREP_V0 + sum(PREP_N)


def group_tiles():
    out = [("xT", 1)]
    out += [("qk", u) for u in QUAD_ORDER]
    out += [("v", b) for b in range(G)]
    out += attention_tiles("a")
    out += [("xT", 2), ("ctxT",), ("xq",), ("xk",)]
    out += [("xv", b) for b in range(G)]
    out += attention_tiles("c")
    out += ffn_tiles()
    return out


HI_TILES = {st: [u for u, _ in UNITS[st] if u and u[0] in ("xT", "OT", "ctxT", "xq", "xk")] for st in STAGES}
V_STEPS = {"A": 4, "B": 2 * G + 2 * G * NH // 8, "C": 4 + 2 * G + G * XH // 8, "D": 4 + G + 4 + G * (4 + 1 + 1)}
CONST_ALL = 16 * 15
N_FILLS = 2 + 2 + 3 + 3 * G + 2 + 2


def build(nc, io):
    order, loops = bodies()
    units = {name: body_units(live) for name, _, live in order}
    slot_of, before = {}, {}
    used = [0] * SLOTS
    turn = {"wide": 0, "narrow": 0}
    at_loop = None
    for name, _, _ in order:
        if name == "loop0":
            at_loop = list(used)
            turn = {"wide": 0, "narrow": 0}
        for st, unit in units[name]:
            if unit[0] in WIDE_TILES:
                s = turn["wide"] % WIDE
                turn["wide"] += 1
            elif unit[0] in NARROW_TILES:
                s = WIDE + turn["narrow"] % NARROW
                turn["narrow"] += 1
            else:
                continue
            slot_of[name, unit], before[name, unit] = s, used[s]
            used[s] += 1
        if name == "loop1":
            per_loop = [u - a for u, a in zip(used, at_loop)]
            used = [a + loops * p for a, p in zip(at_loop, per_loop)]

    with ExitStack() as ctx:
        def sb(name, shape, dt):
            return ctx.enter_context(nc.sbuf_tensor(name, shape, dt))

        def sem(name):
            return ctx.enter_context(nc.semaphore(name))

        slot = [ctx.enter_context(nc.psum_tensor(f"slot{s}", [P, 2 if s < WIDE else 1, 512], F32)) for s in range(SLOTS)]

        wqk = [sb(f"wqk_{k}", [P, CD, QUADS * 256], F16) for k in ("hi", "lo")]
        wv = [sb(f"wv_{k}", [P, CD, 512], F16) for k in ("hi", "lo")]
        wo = [sb(f"wo_{k}", [P, 16, D], F16) for k in ("hi", "lo")]
        wxq = [sb(f"wxq_{k}", [P, CD, D], F16) for k in ("hi", "lo")]
        wxo = [sb(f"wxo_{k}", [P, CD, D], F16) for k in ("hi", "lo")]
        wkv = [sb(f"wkv_{k}", [P, 512], F16) for k in ("hi", "lo")]
        wgT = sb("wgT", [P, CD, F], F16)
        wuT = sb("wuT", [P, CD, F], F16)
        wdT = sb("wdT", [P, FC, D], F16)
        sg_bc = sb("sg_bc", [P, F], F32)
        su_bc = sb("su_bc", [P, F], F32)
        sd_bc = sb("sd_bc", [P, D], F32)
        mask_u = sb("mask_u", [P, D], F32)
        cosT = sb("cosT", [P, N], F32)
        sinT = sb("sinT", [P, N], F32)
        bqk = sb("bqk", [P, 2 * QUADS], F32)
        bv_bc = sb("bv_bc", [T, 512], F32)
        bo_bc = sb("bo_bc", [T, D], F32)
        sink_bc = sb("sink_bc", [T, NH], F32)
        id32 = sb("id32", [P, P], F32)
        id16 = sb("id16", [P, P], F16)
        idb = sb("idb", [T + 3, T], BF16)
        maskM = sb("maskM", [T, 4 * T], BF16)
        half = sb("half", [T, G], F32)
        MB = {"a": [sb(f"maskT_m{i}", [T + 3, NH * T], BF16) for i in range(2)]}
        MB["c"] = [sb("maskT_mc", [T + 3, XH * T], BF16)] * 2

        X1 = [sb(f"X1_{i}", [T, G, D], F32) for i in range(2)]
        X2 = [sb(f"X2_{i}", [T, G, D], F32) for i in range(2)]
        X3 = [sb(f"X3_{i}", [T, G, D], F32) for i in range(2)]
        XN = {n: sb(f"XN{n}", [T, G, D], F32) for n in (1, 2, 3)}
        OUT = sb("OUT", [T, G, D], F32)
        xT = {n: [sb(f"xT{n}_{k}", [P, CD, N], F16) for k in ("hi", "lo")] for n in (1, 2)}
        ROT = sb("rope", [P, 2 * 2 * 2 * N], F32)
        SUM = sb("rope_sums", [P, 2 * 2 * N], F32)
        R = [sb(f"split{i}", [P, 4, N], F16) for i in range(2)]
        RX = [sb(f"xsplit{i}", [P, 4, N], F16) for i in range(2)]
        QA = [sb(f"QA{b}", [P, NH * T], F16) for b in range(G)]
        KA = [sb(f"KA{b}", [P, NKV, T], F16) for b in range(G)]
        KB = [sb(f"KB{b}", [P, NKV, T], F16) for b in range(G)]
        V = [sb(f"V{i}", [T, G, NKV * VS + W - VS], F32) for i in range(2)]
        PR = {"a": sb("probs", [T, 2, 8 * T], F32), "c": sb("xprobs", [T, 1, 8 * T], F32)}
        ON = {"a": sb("attn_out", [T, 2, 8 * HD], F32), "c": sb("xattn_out", [T, 1, D], F32)}
        OT = {"a": [sb(f"attn_outT_{k}", [P, 16, T], F16) for k in ("hi", "lo")],
              "c": [sb(f"xattn_outT_{k}", [P, CD, T], F16) for k in ("hi", "lo")]}
        XQs, XKs = sb("XQ", [P, XH * N], F16), sb("XK", [P, XH * N], F16)
        C0 = sb("ctx_rows", [T, G, L], F32)
        CT = sb("ctxT", [P, N], F16)
        XV = sb("XV", [T, G, XVW], F32)
        qT = sb("qT", [P, CD, T], F16)
        tT = sb("tT", [P, FC, T], F16)
        stats = {n: sb(f"stats{n}", [T, G, 6], F32) for n in (1, 2, 3)}
        mv = {n: sb(f"mv{n}", [T, G, 2], F32) for n in (1, 2, 3)}
        ve = {n: sb(f"var_eps{n}", [T, G], F32) for n in (1, 2, 3)}
        rstd = {n: sb(f"rstd{n}", [T, G], F32) for n in (1, 2, 3)}
        mx = {k: [sb(f"row_max_{k}{i}", [T, NH], F32) for i in range(2)] for k in "ac"}
        sm = [sb(f"sink_shift{i}", [T, NH], F32) for i in range(2)]
        es = [sb(f"sink_exp{i}", [T, NH], F32) for i in range(2)]
        MR = {k: [sb(f"neg_max_{k}{i}", [NH, 3, T], BF16) for i in range(2)] for k in "ac"}
        mr_rest = {k: sb(f"mr_rest_{k}", [NH, T], F32) for k in "ac"}
        den = sb("den", [T, 2, 8], F32)
        rden = {k: sb(f"rden_{k}", [T, 2, 8], F32) for k in "ac"}
        ry, rry, ky, kMy, sx = (sb(n, [T, G], F32) for n in ("ry", "rry", "ky", "kMy", "sx"))
        rt, rrt, kt, kMt, st_ = (sb(n, [T, G], F32) for n in ("rt", "rrt", "kt", "kMt", "st"))
        FB = sb("ffn", [P, 3 * F], F32)
        gs, us, th = (FB[0:T, i * F:(i + 1) * F] for i in range(3))
        tM, tS = th, gs
        YMS = sb("y_round", [T, 2 * D], F32)
        yM, yS = YMS[:, 0:D], YMS[:, D:2 * D]
        tq = sb("tq", [T, F], F16)
        yq = sb("yq", [T, G, D], F16)

        ab = ROT[:, 0:4 * N].rearrange("p (i k n) -> p i k n", i=2, k=2)
        abcos = ROT[:, 4 * N:8 * N].rearrange("p (i k n) -> p i k n", i=2, k=2)
        rsum = SUM[:].rearrange("p (i k n) -> p i k n", i=2, k=2)
        qa = [QA[b][:].rearrange("p (h t) -> p h t", h=NH) for b in range(G)]
        XQ = XQs[:].rearrange("p (h n) -> p h n", h=XH)
        XK = XKs[:].rearrange("p (h n) -> p h n", h=XH)
        stage = [QA[i][:].bitcast(F32)[:, 0:1024] for i in range(2)]
        wf = [x[:].bitcast(F32)[:, i * F:(i + 1) * F] for x in (XQs, XKs) for i in range(2)]
        wq = R[0][:].rearrange("p k n -> p (k n)")
        cnt4 = FB[:, 0:F]
        maskd = FB[:, F:2 * F]
        cnt4u = FB[:, 2 * F:2 * F + D]
        onehot = ROT[:].bitcast(BF16)[:, 0:F]
        iota = ROT[:, F:2 * F]
        ones_b = SUM[:].bitcast(BF16)[:, 0:P]
        idx_d = sb("idx_d", [P, FC], I32)
        idx_u = sb("idx_u", [P, CD], I32)
        idxf = sb("idxf", [P, FC + CD], F32)
        wr = sb("wr", [P, 4], F32)
        wsb = SUM[:, P:2 * P]

        const_ld = sem("const_ld")
        stage_ld = [sem(f"stage_ld{i}") for i in range(2)]
        hi_done, lo_done = sem("prep_hi_done"), sem("prep_lo_done")
        fills = sem("fills")
        prep_v = sem("prep_v")
        prep_p = sem("prep_p")
        prep_a = sem("prep_a")
        prep_abs = sem("prep_abs")
        wrow_ld = sem("wrow_ld")
        wdown_ld = sem("wdown_ld")
        full = [sem(f"slot_full{s}") for s in range(SLOTS)]
        free = [sem(f"slot_free{s}") for s in range(SLOTS)]
        x_ld, c_ld, out_st = sem("x_ld"), sem("ctx_ld"), sem("out_st")
        ln_var, ln_rstd, xn_rdy = ({n: sem(f"{w}{n}") for n in (1, 2, 3)} for w in ("ln_var", "ln_rstd", "xn_rdy"))
        hi_rdy = {st: sem(f"hi_rdy_{st}") for st in "ABC"}
        rope_rot, rope_sum, rope_hi, rope_lo = sem("rope_rot"), sem("rope_sum"), sem("rope_hi"), sem("rope_lo")
        sc_w = [sem(f"scratch_write{i}") for i in range(2)]
        xsc_w = sem("x_scratch_write")
        qa_ld = [sem(f"qa_ld{i}") for i in range(2)]
        xqk_ld = sem("xqk_ld")
        s_done = [sem(f"self_scores_done{b}") for b in range(G)]
        mr_rdy = {k: sem(f"mr_rdy_{k}") for k in "ac"}
        mb_ld = {k: [sem(f"mb_ld_{k}{i}") for i in range(2)] for k in "ac"}
        sm_rdy, es_rdy = sem("sm_rdy"), sem("es_rdy")
        xb_rdy = sem("xb_rdy")
        yk_rdy, tk_rdy = sem("yk_rdy"), sem("tk_rdy")
        abs_rdy, qs_rdy, q_rdy = sem("abs_rdy"), sem("qs_rdy"), sem("q_rdy")
        th_rdy, w_rdy, t_rdy = sem("th_rdy"), sem("w_rdy"), sem("t_rdy")
        out_rdy = sem("out_rdy")
        v_self = {st: sem(f"dve_step_{st}") for st in STAGES}
        stood = sem("stood")

        def wait_at(eng, semaphore, g, per_group, k):
            it, c = g
            if it is not None:
                assert c * per_group + k > 0
                eng.wait_ge(semaphore, it * (2 * per_group) + (c * per_group + k))
            elif c * per_group + k > 0:
                eng.wait_ge(semaphore, c * per_group + k)

        def index(g):
            return g[1] if g[0] is None else g[0] * 2 + g[1]

        def claim(at, *t):
            return free[slot_of[at[0], t]], at[1], slot_of[at[0], t], before[at[0], t] + 1

        def filled(at, *t):
            return full[slot_of[at[0], t]], at[1], slot_of[at[0], t], before[at[0], t] + 1

        def drained(at, *t):
            return free[slot_of[at[0], t]], at[1], slot_of[at[0], t], before[at[0], t] + 2

        def wait(eng, *positions):
            for i, (s, it, n, k) in enumerate(positions):
                if not any(s is s2 and (k2, j) > (k, i) for j, (s2, _, _, k2) in enumerate(positions) if j != i):
                    eng.wait_ge(s, k if it is None else it * per_loop[n] + k)

        def tile(at, *t):
            return slot[slot_of[at[0], t]]

        def full_sem(at, *t):
            return full[slot_of[at[0], t]]

        def free_sem(at, *t):
            return free[slot_of[at[0], t]]

        def run(eng, part):
            def body(name, n, it):
                for st, unit in units[name]:
                    c = n - STAGES.index(st)
                    part((name, it), (it, c), c % 2, unit)
            i = 0
            while i < len(order):
                if order[i][0] == "loop0":
                    with eng.Fori(0, loops) as it:
                        body("loop0", order[i][1], it)
                        body("loop1", order[i + 1][1], it)
                    i += 2
                else:
                    body(order[i][0], order[i][1], None)
                    i += 1

        def stand(eng):
            eng.sem_inc(stood, 1)

        consts = [(cosT[:], io["cosT"]), (sinT[:], io["sinT"]), (bqk[:], io["bqk"]), (bv_bc[:], io["bv"]),
                  (bo_bc[:], io["bo"]), (sink_bc[:], io["sinks"]), (id32[:], io["id32"]),
                  (iota, io["iota"]), (idx_d[:], io["idx_d"]), (idx_u[:], io["idx_u"])]
        splits = [(io["wqkT"][:, c, 1024 * i:min(1024 * i + 1024, 2560)],
                   wqk[0][:, c, 1024 * i:min(1024 * i + 1024, 2560)],
                   wqk[1][:, c, 1024 * i:min(1024 * i + 1024, 2560)], min(1024, 2560 - 1024 * i))
                  for c in range(CD) for i in range(3)]
        splits += [(io["wvT"][:, c, :], wv[0][:, c, :], wv[1][:, c, :], 512) for c in range(CD)]
        splits += [(io["woT"][:, 1024 * i:1024 * i + 1024], wo[0][:].rearrange("p c d -> p (c d)")[:, 1024 * i:1024 * i + 1024],
                    wo[1][:].rearrange("p c d -> p (c d)")[:, 1024 * i:1024 * i + 1024], 1024) for i in range(4)]
        splits += [(io["wxqT"], wxq[0][:].rearrange("p c d -> p (c d)"), wxq[1][:].rearrange("p c d -> p (c d)"), 512),
                   (io["wxoT"], wxo[0][:].rearrange("p c d -> p (c d)"), wxo[1][:].rearrange("p c d -> p (c d)"), 512),
                   (io["wkvT"], wkv[0][:], wkv[1][:], 512)]
        NS = len(splits)
        wrows = [(m, c, P if c < FC - 1 else FL, D) for m in ("g", "u") for c in range(FC)]
        wrows += [("d", c, P, F) for c in range(CD)]
        sc = io["scratch"]
        xsc = io["xscratch"]

        block = ctx.enter_context(nc.Block())

        @block.sync
        def _(sp):
            for dst, src in consts:
                sp.dma_start(dst, src).then_inc(const_ld, 16)
            for m in MB["a"] + MB["c"][:1]:
                sp.dma_start(m[0:T, :], io["maskT"][:, 0:m.shape[1]]).then_inc(const_ld, 16)
            sp.dma_start(maskM[:], io["maskM"]).then_inc(const_ld, 16)
            sp.dma_start(idb[:], io["idb"]).then_inc(const_ld, 16)
            for n, (src, _hi, _lo, cols) in enumerate(splits):
                if n >= 2:
                    sp.wait_ge(lo_done, n - 1)
                sp.dma_start(stage[n % 2][:, 0:cols], src).then_inc(stage_ld[n % 2], 16)
            for n in range(CD):
                sp.wait_ge(prep_v, VBASE[2 * FC + n - 1] + 1)
                sp.dma_start(wf[0], io["w_down"][P * n:P * n + P, :]).then_inc(wdown_ld, 16)

            sp.wait_ge(lo_done, NS + 1)
            sp.wait_ge(fills, N_FILLS)

            def part(at, g, i, unit):
                what = unit[0]
                if what == "load":
                    wait_at(sp, mr_rdy["a"], g, G, -G + 1)
                    stand(sp)
                    sp.dma_start(X1[i][:], io["x"][index(g)].rearrange("b t d -> t b d")).then_inc(x_ld, 16)
                elif what == "split":
                    n = unit[1]
                    wait_at(sp, rope_lo, g, QUADS, n + 1)
                    stand(sp)
                    sp.dma_start(sc[index(g), QUAD_ORDER[n]], R[n % 2][:]).then_inc(sc_w[n % 2], 16)
                elif what == "qload":
                    b = unit[1]
                    if b == 0:
                        for p in range(2):
                            wait_at(sp, sc_w[p], g, 8 * QUADS, 8 * QUADS)
                            stand(sp)
                    wait_at(sp, s_done[b], g, 1, 0)
                    stand(sp)
                    for k in range(4):
                        src = sc[index(g), 0:8, :, k, b * T:(b + 1) * T].rearrange("u (h f) t -> f (u h) t", h=4)
                        sp.dma_start(qa[b][32 * k:32 * k + 32], src).then_inc(qa_ld[b], 16)
                    for row, k, dst in ((0, 0, KA), (32, 1, KA), (64, 0, KA), (96, 1, KA), (0, 2, KB), (32, 3, KB)):
                        src = sc[index(g), 8:10, :, k, b * T:(b + 1) * T].rearrange("u (h f) t -> f (u h) t", h=4)
                        sp.dma_start(dst[b][row:row + 32], src).then_inc(qa_ld[b], 16)
                elif what == "mT":
                    _, kind, b, _ = unit
                    h = KINDS[kind][0]
                    wait_at(sp, mr_rdy[kind], g, G, b + 1)
                    stand(sp)
                    for k in range(3):
                        sp.dma_start(MB[kind][b][T + k:T + k + 1, 0:h * T], MR[kind][b][0:h, k, :]).then_inc(mb_ld[kind][b], 16)
                elif what == "cload":
                    sp.dma_start(C0[:], io["ctx"][index(g)].rearrange("b t d -> t b d")).then_inc(c_ld, 16)
                elif what == "xload":
                    for n, t in enumerate(("xq", "xk")):
                        wait(sp, drained(at, t))
                        stand(sp)
                        sp.dma_start(xsc[index(g), n].rearrange("k c p n -> p (k c) n"), RX[n][:]).then_inc(xsc_w, 16)
                    wait_at(sp, xsc_w, g, 32, 32)
                    stand(sp)
                    for n, dst in ((0, XQ), (1, XK)):
                        for row, k in enumerate((0, 1, 0) if n == 0 else (0, 0, 1)):
                            src = xsc[index(g), n, k].rearrange("c (h r) n -> r (c h) n", h=8)
                            sp.dma_start(dst[16 * row:16 * row + 16], src).then_inc(xqk_ld, 16)
                elif what == "D":
                    b = unit[1]
                    wait_at(sp, out_rdy, g, G, b + 1)
                    stand(sp)
                    sp.dma_start(io["out"][index(g), b], OUT[:, b, :]).then_inc(out_st, 16)

            run(sp, part)
            sp.wait_ge(out_st, 16 * B)

        @block.tensor
        def _(pe):
            for which, chunks, cols, o in (("d", FC, F, 0), ("u", CD, D, FC)):
                for c in range(chunks):
                    k = FL if which == "d" and c == FC - 1 else P
                    pe.wait_ge(prep_v, 3 + o + c)
                    for h in range(2):
                        w = cols // 2
                        last = pe.matmul(slot[0 if which == "d" else 1][:, h, 0:w], ones_b[0:k],
                                         onehot[0:k, h * w:(h + 1) * w], start=(c == 0), stop=(c == chunks - 1))
                    last.then_inc(prep_p, 1)
            for n, (m, c, rows, cols) in enumerate(wrows):
                pe.wait_ge(prep_a, n + 1)
                s = slot[2][:].bitcast(F16)
                if n:
                    pe.wait_ge(prep_v, VBASE[n])
                for k in range(-(-cols // P)):
                    kk = min(P, cols - k * P)
                    pe.transpose(s[0:kk, 0, k * P:k * P + rows], wq[0:rows, k * P:k * P + kk],
                                 id16[0:rows, 0:rows])
                pe.matmul(slot[WIDE][:, 0, 0:rows], wsb[0:rows], id32[0:rows, 0:rows],
                          start=True, stop=True).then_inc(prep_p, 1)
            pe.wait_ge(prep_v, PREP_VALL)
            pe.wait_ge(lo_done, NS + 1)

            def product(out, a, b, pairs, first=True, last=True):
                for i, (x, y) in enumerate(pairs):
                    ins = pe.matmul(out, a(x), b(y), start=(first and i == 0), stop=(last and i == len(pairs) - 1))
                return ins

            HL = ((0, 0), (0, 1), (1, 0))

            def columns(b):
                return slice(b * T, (b + 1) * T)

            def scores_for_max(at, g, kind, b, j):
                t = ("M", kind, b, j)
                wait(pe, claim(at, *t))
                if kind == "a" and j == 0:
                    wait_at(pe, qa_ld[b], g, 160, 160)
                if kind == "c" and j == 0 and b == 0:
                    wait_at(pe, xqk_ld, g, 96, 96)
                for k in range(2):
                    pe.matmul(tile(at, *t)[0:T, k, 0:4 * T], idb[0:T, :], maskM[:], start=True, stop=False)
                    for h in range(4):
                        head = 8 * j + 4 * k + h
                        if kind == "a":
                            q, key = qa[b][:, head, :], KA[b][:, head // 4, :]
                        else:
                            q, key = XQ[:, head, columns(b)], XK[:, head, columns(b)]
                        ins = pe.matmul(tile(at, *t)[0:T, k, h * T:(h + 1) * T], q, key, start=False, stop=(h == 3))
                ins.then_inc(full_sem(at, *t), 1)

            def scores(at, g, kind, b, j):
                t = ("S", kind, b, j)
                wait(pe, claim(at, *t))
                if j == 0:
                    wait_at(pe, mb_ld[kind][b], g, 48, 48)
                for k in range(2):
                    h0 = 8 * j + 4 * k
                    out = tile(at, *t)[0:T, k, 0:4 * T]
                    pe.matmul(out, idb[:], MB[kind][b][:, h0 * T:(h0 + 4) * T], start=True, stop=False)
                    if kind == "a":
                        q = qa[b][:, h0:h0 + 4, :]
                        pe.matmul(out, KA[b][:, h0 // 4, :], q, start=False, stop=False)
                        ins = pe.matmul(out, KB[b][:, h0 // 4, :], q, start=False, stop=True)
                    else:
                        for h in range(4):
                            ins = pe.matmul(tile(at, *t)[0:T, k, h * T:(h + 1) * T], XK[:, h0 + h, columns(b)],
                                            XQ[:, h0 + h, columns(b)], start=False, stop=(h == 3))
                ins.then_inc(full_sem(at, *t), 1)

            def values(at, g, i, kind, b, j):
                t = ("V", kind, b, j)
                last_tile = KINDS[kind][0] // 8 - 1
                needs = [claim(at, *t), drained(at, "S", kind, b, j)]
                if kind == "c":
                    needs.append(drained(at, "xv", b))
                wait(pe, *needs)
                for n in range(8):
                    head = 8 * j + n
                    if kind == "a":
                        v = V[i][:, b, head // 4 * VS:head // 4 * VS + W]
                    else:
                        v = XV[:, b, head * XS:head * XS + W]
                    p = j % 2 if kind == "a" else 0
                    ins = pe.matmul(tile(at, *t)[0:T, n // 4, (n % 4) * W:(n % 4) * W + W],
                                    PR[kind][:, p, n * T:(n + 1) * T], v, start=True, stop=True)
                    if n == 0 and kind == "a" and j == last_tile:
                        ins.then_inc(s_done[b], 1)
                ins.then_inc(full_sem(at, *t), 1)

            def outputs_to_columns(at, kind, b, j):
                t = ("OT", kind, b, j)
                n = 4 if kind == "a" else CD
                wait(pe, claim(at, *t),
                     drained(at, "V", kind, b, j if kind == "a" else 1))
                for c in range(n):
                    ins = pe.transpose(tile(at, *t)[:, 0, c * T:(c + 1) * T],
                                       ON[kind][:, j % 2, c * P:(c + 1) * P], id32[0:T, 0:T])
                ins.then_inc(full_sem(at, *t), 1)

            def project(at, kind, b):
                t = ("Y", kind, b, 0)
                n, w = (16, wo) if kind == "a" else (CD, wxo)
                wait(pe, claim(at, *t), *(drained(at, "OT", kind, b, j) for j in range(4 if kind == "a" else 1)))
                for c in range(n):
                    ins = product(tile(at, *t)[0:T, 0, 0:D], lambda i: OT[kind][i][:, c, :], lambda i: w[i][:, c, :],
                                  HL, c == 0, c == n - 1)
                ins.then_inc(full_sem(at, *t), 1)

            def part(at, g, i, unit):
                what = unit[0]
                if what in ("xT", "qk", "v", "ctxT", "xq", "xk", "xv", "qT", "G", "U", "tT", "D"):
                    ps, done = tile(at, *unit), full_sem(at, *unit)
                if what == "xT":
                    n = unit[1]
                    wait_at(pe, xn_rdy[n], g, 1, 1)
                    wait(pe, claim(at, *unit))
                    for c in range(CD):
                        for b in range(G):
                            ins = pe.transpose(ps[:, 0, c * N + b * T:c * N + (b + 1) * T], XN[n][:, b, c * P:(c + 1) * P],
                                               id32[0:T, 0:T])
                    ins.then_inc(done, 1)
                elif what == "qk":
                    wait(pe, claim(at, *unit), drained(at, "xT", 1))
                    for h in range(2):
                        col = QUAD_ORDER[unit[1]] * 256 + h * P
                        for c in range(CD):
                            ins = product(ps[:, 0, h * N:(h + 1) * N], lambda k: wqk[k][:, c, col:col + P],
                                          lambda k: xT[1][k][:, c, :], HL, c == 0, c == CD - 1)
                    ins.then_inc(done, 1)
                elif what == "v":
                    wait(pe, claim(at, *unit))
                    for c in range(CD):
                        ins = product(ps[0:T, 0, :], lambda k: xT[1][k][:, c, columns(unit[1])], lambda k: wv[k][:, c, :],
                                      HL, c == 0, c == CD - 1)
                    ins.then_inc(done, 1)
                elif what == "M":
                    scores_for_max(at, g, *unit[1:])
                elif what == "mT":
                    _, kind, b, _ = unit
                    h = KINDS[kind][0]
                    wait(pe, claim(at, *unit), drained(at, "M", kind, b, h // 8 - 1))
                    pe.transpose(tile(at, *unit)[0:h, 0, 0:T], mx[kind][b][:, 0:h], id32[0:T, 0:T]).then_inc(full_sem(at, *unit), 1)
                elif what == "S":
                    scores(at, g, *unit[1:])
                elif what == "V":
                    values(at, g, i, *unit[1:])
                elif what == "OT":
                    outputs_to_columns(at, *unit[1:])
                elif what == "Y":
                    project(at, *unit[1:3])
                elif what == "ctxT":
                    wait_at(pe, c_ld, g, 16, 16)
                    wait(pe, claim(at, *unit))
                    stand(pe)
                    for b in range(G):
                        ins = pe.transpose(ps[0:L, 0, columns(b)], C0[:, b, :], id32[0:T, 0:T])
                    ins.then_inc(done, 1)
                elif what == "xq":
                    wait(pe, claim(at, *unit), drained(at, "xT", 2))
                    for m in range(CD):
                        for c in range(CD):
                            ins = product(ps[:, 0, m * N:(m + 1) * N], lambda k: wxq[k][:, c, m * P:(m + 1) * P],
                                          lambda k: xT[2][k][:, c, :], HL, c == 0, c == CD - 1)
                    ins.then_inc(done, 1)
                elif what == "xk":
                    wait(pe, claim(at, *unit), drained(at, "ctxT"))
                    for m in range(CD):
                        ins = product(ps[:, 0, m * N:(m + 1) * N], lambda k: wkv[k][:, m * P:(m + 1) * P], lambda k: CT[:],
                                      ((0, 0), (1, 0)))
                    ins.then_inc(done, 1)
                elif what == "xv":
                    wait(pe, claim(at, *unit))
                    product(ps[0:T, 0, 0:D], lambda k: CT[:, columns(unit[1])], lambda k: wkv[k][:, D:2 * D],
                            ((0, 0), (0, 1))).then_inc(done, 1)
                elif what == "qT":
                    wait(pe, claim(at, *unit))
                    wait_at(pe, q_rdy, g, 2 * G, Q_Y[unit[1]])
                    for c in range(CD):
                        ins = pe.transpose(ps[:].bitcast(F16)[:, 0, c * T:(c + 1) * T], yq[:, unit[1], c * P:(c + 1) * P],
                                           id16[0:T, 0:T])
                    ins.then_inc(done, 1)
                elif what in ("G", "U"):
                    w = wgT if what == "G" else wuT
                    wait(pe, claim(at, *unit), drained(at, "qT", unit[1]))
                    for h in range(2):
                        for c in range(CD):
                            ins = pe.matmul(ps[0:T, h, 0:FH], qT[:, c, :], w[:, c, h * FH:(h + 1) * FH],
                                            start=(c == 0), stop=(c == CD - 1))
                    ins.then_inc(done, 1)
                elif what == "tT":
                    wait(pe, claim(at, *unit))
                    wait_at(pe, q_rdy, g, 2 * G, Q_T[unit[1]])
                    for c in range(FC):
                        k = P if c < FC - 1 else FL
                        ins = pe.transpose(ps[:].bitcast(F16)[0:k, 0, c * T:(c + 1) * T], tq[:, c * P:c * P + k], id16[0:T, 0:T])
                    ins.then_inc(done, 1)
                elif what == "D":
                    wait(pe, claim(at, *unit), drained(at, "tT", unit[1]))
                    for c in range(FC):
                        k = P if c < FC - 1 else FL
                        ins = pe.matmul(ps[0:T, 0, 0:D], tT[0:k, c, :], wdT[0:k, c, :], start=(c == 0), stop=(c == FC - 1))
                    ins.then_inc(done, 1)

            run(pe, part)

        @block.scalar
        def _(act):
            for n, (_src, hi, _lo, cols) in enumerate(splits):
                act.wait_ge(stage_ld[n % 2], 16 * (n // 2 + 1))
                act.activation(hi, stage[n % 2][:, 0:cols], ACT.Copy, scale=WS).then_inc(hi_done, 1)
            for n, (m, c, rows, cols) in enumerate(wrows):
                act.wait_ge(prep_v, VBASE[n] + 5)
                act.activation(wf[2][0:rows, 0:cols], wf[1][0:rows, 0:cols], ACT.Abs,
                               scale=wr[0:rows, 3:4]).then_inc(prep_abs, 1)
                act.wait_ge(prep_v, VBASE[n] + 9)
                act.activation(wsb[0:rows], id32[0:rows, :], ACT.Identity, bias=wr[0:rows, 0:1],
                               scale=0.0).then_inc(prep_a, 1)

            def part(at, g, i, unit):
                what = unit[0]
                if what in ("xT", "ctxT", "xq", "xk", "OT"):
                    ps = tile(at, *unit)
                    scale = 1.0
                    if what == "xT":
                        out, src, st = xT[unit[1]][0][:].rearrange("p c n -> p (c n)"), ps[:, 0, 0:CD * N], "AC"[unit[1] - 1]
                    elif what == "ctxT":
                        out, src, st = CT[0:L, :], ps[0:L, 0, 0:N], "C"
                    elif what == "OT":
                        _, kind, b, j = unit
                        n = 4 if kind == "a" else CD
                        out = OT[kind][0][:, n * j:n * (j + 1), :].rearrange("p c t -> p (c t)")
                        src, st = ps[:, 0, 0:n * T], "B" if kind == "a" else "C"
                    else:
                        wait_at(act, xsc_w, g, 32, 0)
                        out = RX[what == "xk"][:, 0:2, :].rearrange("p k n -> p (k n)")
                        src, st, scale = ps[:, 0, 0:2 * N], "C", 1.0 / WS
                    wait(act, filled(at, *unit))
                    act.activation(out, src, ACT.Copy, scale=scale).then_inc(hi_rdy[st], 1)
                elif what == "qk":
                    n = unit[1]
                    u = QUAD_ORDER[n]
                    wait(act, filled(at, *unit))
                    wait_at(act, rope_sum, g, QUADS, n - 1)
                    for h in range(2):
                        ins = act.activation(ab[:, n % 2, h, :], tile(at, *unit)[:, 0, h * N:(h + 1) * N], ACT.Identity,
                                             bias=bqk[:, 2 * u + h:2 * u + h + 1])
                    ins.then_inc(free_sem(at, *unit), 1)
                elif what == "split":
                    n = unit[1]
                    wait_at(act, rope_sum, g, QUADS, n + 1)
                    wait_at(act, sc_w[n % 2], g, 8 * QUADS, 16 * (n // 2))
                    act.activation(R[n % 2][:, 0:2, :], rsum[:, n % 2, :, :], ACT.Copy).then_inc(rope_hi, 1)
                elif what == "S":
                    _, kind, b, j = unit
                    wait(act, filled(at, *unit))
                    act.activation(PR[kind][:, j % 2 if kind == "a" else 0, :].rearrange("p (k n) -> p k n", k=2),
                                   tile(at, *unit)[0:T, :, 0:4 * T], ACT.Exp, scale=KINDS[kind][1]).then_inc(free_sem(at, *unit), 1)
                elif what == "mT" and unit[1] == "a":
                    b = unit[2]
                    wait_at(act, sm_rdy, g, G, b + 1)
                    act.activation(es[b][:], sm[b][:], ACT.Exp).then_inc(es_rdy, 1)
                elif what == "y":
                    b = unit[1]
                    if b == 0:
                        wait_at(act, yk_rdy, g, 1, 1)
                        wait_at(act, q_rdy, g, 2 * G, 0)
                    else:
                        wait_at(act, q_rdy, g, 2 * G, Q_Y[b - 1])
                    act.activation(yM, XN[3][:, b, :], ACT.Abs, scale=kMy[:, b:b + 1]).then_inc(abs_rdy, 1)
                elif what == "qT":
                    wait(act, filled(at, *unit))
                    act.activation(qT[:].rearrange("p c t -> p (c t)"), tile(at, *unit)[:].bitcast(F16)[:, 0, 0:CD * T],
                                   ACT.Copy).then_inc(free_sem(at, *unit), 1)
                elif what == "h":
                    wait(act, drained(at, "G", unit[1]))
                    act.activation(th, gs, ACT.Tanh, scale=0.5).then_inc(th_rdy, 1)
                elif what == "tq":
                    b = unit[1]
                    wait_at(act, tk_rdy, g, G, b + 1)
                    act.activation(tM, us, ACT.Abs, scale=kMt[:, b:b + 1]).then_inc(abs_rdy, 1)
                elif what == "tT":
                    s = tile(at, *unit)[:].bitcast(F16)
                    wait(act, filled(at, *unit))
                    act.activation(tT[:, 0:FC - 1, :].rearrange("p c t -> p (c t)"), s[:, 0, 0:(FC - 1) * T], ACT.Copy)
                    act.activation(tT[0:FL, FC - 1, :], s[0:FL, 0, (FC - 1) * T:FC * T], ACT.Copy).then_inc(free_sem(at, *unit), 1)

            run(act, part)

        @block.gpsimd
        def _(pool):
            pool.wait_ge(const_ld, CONST_ALL)
            for n, (m, c, rows, cols) in enumerate(wrows):
                if m == "d":
                    continue
                if n:
                    pool.wait_ge(prep_v, VBASE[n - 1] + 1)
                pool.indirect_dma_start(out=wf[0][0:rows, 0:D], out_offset=None, in_=io["w_gate" if m == "g" else "w_up"],
                                        in_offset=bass.IndirectOffsetOnAxis(ap=idx_d[0:rows, c:c + 1], axis=0)).then_inc(wrow_ld, 16)

            def part(at, g, i, unit):
                what = unit[0]
                if what == "ln":
                    n = unit[1]
                    wait_at(pool, ln_var[n], g, 1, 1)
                    pool.tensor_tensor(rstd[n][:], ve[n][:], half[:], ALU.pow).then_inc(ln_rstd[n], 1)
                elif what == "nrm" and unit[1] == 1:
                    wait_at(pool, xn_rdy[1], g, 1, 1)
                    pool.tensor_tensor(X1[i][:], X1[i][:], bo_bc[:].unsqueeze(1).broadcast_to([T, G, D]), ALU.add).then_inc(xb_rdy, 1)
                elif what == "qk":
                    n = unit[1]
                    k = n % 2
                    wait_at(pool, rope_rot, g, QUADS, n + 1)
                    wait_at(pool, rope_lo, g, QUADS, n - 1)
                    pool.tensor_tensor(rsum[:, k, 0, :], abcos[:, k, 0, :], ab[:, k, 1, :], ALU.subtract)
                    pool.tensor_tensor(rsum[:, k, 1, :], abcos[:, k, 1, :], ab[:, k, 0, :], ALU.add).then_inc(rope_sum, 1)
                elif what == "y":
                    b = unit[1]
                    wait_at(pool, qs_rdy, g, 2 * G, Q_Y[b])
                    pool.tensor_tensor(yq[:, b, :], yS, yM, ALU.subtract).then_inc(q_rdy, 1)
                elif what == "h":
                    wait_at(pool, w_rdy, g, G, unit[1] + 1)
                    pool.tensor_tensor(us, th, us, ALU.mult).then_inc(t_rdy, 1)
                elif what == "tq":
                    wait_at(pool, qs_rdy, g, 2 * G, Q_T[unit[1]])
                    pool.tensor_tensor(tq[:], tS, tM, ALU.subtract).then_inc(q_rdy, 1)

            run(pool, part)

        @block.vector
        def _(dve):
            n_fill = [0]

            def fill(ins):
                n_fill[0] += 1
                ins.then_inc(fills, 1)

            for s in range(SLOTS):
                dve.sem_inc(free[s], 1)
            fill(dve.memset(half[:], -0.5))
            fill(dve.memset(ones_b, 1.0))
            for i in range(2):
                fill(dve.memset(KB[i][HD:P, :, :], 0.0))
            fill(dve.memset(V[0][:], 0.0))
            fill(dve.memset(V[1][:], 0.0))
            fill(dve.memset(XV[:], 0.0))
            dve.wait_ge(fills, n_fill[0])
            for b in range(G):
                for i in range(2):
                    fill(dve.memset(V[i][:, b, 0:NKV * VS].rearrange("p (h w) -> p h w", w=VS)[:, :, HD:VS], 1.0))
                fill(dve.memset(XV[:, b, 0:XH * XS].rearrange("p (h w) -> p h w", w=XS)[:, :, XD:XS], 1.0))
            dve.wait_ge(const_ld, CONST_ALL)
            fill(dve.tensor_copy(id16[:], id32[:]))
            fill(dve.tensor_scalar(bqk[:], bqk[:], WS, None, ALU.mult))
            dve.wait_ge(fills, n_fill[0])

            nv = [0]

            def prep(ins):
                nv[0] += 1
                ins.then_inc(prep_v, 1)

            def prep_settled():
                dve.wait_ge(prep_v, nv[0])

            prep(dve.tensor_copy(idxf[:, 0:FC], idx_d[:]))
            prep(dve.tensor_copy(idxf[:, FC:FC + CD], idx_u[:]))
            prep_settled()
            for c in range(FC + CD):
                k = FL if c == FC - 1 else P
                w = F if c < FC else D
                if c:
                    dve.wait_ge(prep_p, c)
                prep(dve.tensor_scalar(onehot[0:k, 0:w], iota[0:k, 0:w], idxf[0:k, c:c + 1], None, ALU.is_equal))
            dve.wait_ge(prep_p, FC + CD)
            for s, w, cnt, mask in ((slot[0], F, cnt4, maskd), (slot[1], D, cnt4u, mask_u[:])):
                v = s[:, :, 0:w // 2]
                prep(dve.tensor_scalar(cnt.rearrange("p (k n) -> p k n", k=2), v, 0.25, None, ALU.mult))
                prep(dve.tensor_scalar(mask.rearrange("p (k n) -> p k n", k=2), v, 1.0, None, ALU.min))
            prep_settled()
            assert nv[0] == PREP_V0

            for n, (_src, hi, lo, cols) in enumerate(splits):
                dve.wait_ge(hi_done, n + 1)
                dve.scalar_tensor_tensor(out=lo, in0=stage[n % 2][:, 0:cols], scalar=WS, in1=hi, op0=ALU.mult,
                                         op1=ALU.subtract).then_inc(lo_done, 1)
            dve.wait_ge(lo_done, NS)
            dve.memset(wkv[1][L:P, :], 0.0).then_inc(lo_done, 1)

            for n, (m, c, rows, cols) in enumerate(wrows):
                r = slice(0, rows)
                w0, w1, w2, w3 = (wf[i][r, 0:cols] for i in range(4))
                mask, cnt = (maskd, cnt4) if m == "d" else (mask_u[:], cnt4u)
                assert nv[0] == VBASE[n]
                if m == "d":
                    dve.wait_ge(wdown_ld, 16 * (c + 1))
                else:
                    dve.wait_ge(wrow_ld, 16 * (n + 1))
                prep(dve.tensor_tensor(w1, w0, mask[r, :], ALU.mult))
                prep_settled()
                prep(dve.tensor_reduce(wr[r, 0:1], w1, AX.X, ALU.max, apply_absolute_value=True))
                prep_settled()
                prep(dve.reciprocal(wr[r, 1:2], wr[r, 0:1]))
                prep_settled()
                prep(dve.tensor_scalar(wr[r, 2:3], wr[r, 1:2], FP8_MAX, None, ALU.mult))
                prep(dve.tensor_scalar(wr[r, 3:4], wr[r, 1:2], FP8_MAX * 2.0 ** 20, None, ALU.mult))
                prep_settled()
                dve.wait_ge(prep_abs, n + 1)
                prep(dve.tensor_scalar(w2, w2, SUB, None, ALU.max))
                prep_settled()
                prep(dve.scalar_tensor_tensor(out=w3, in0=w1, scalar=wr[r, 2:3], in1=w2, op0=ALU.mult, op1=ALU.add))
                prep_settled()
                prep(dve.tensor_tensor(w3, w3, w2, ALU.subtract))
                prep_settled()
                prep(dve.tensor_tensor(wq[r, 0:cols], w3, cnt[r, :], ALU.mult))
                dve.wait_ge(prep_p, FC + CD + n + 1)
                s = slot[2][:].bitcast(F16)
                if m == "d":
                    prep(dve.tensor_copy(wdT[:, 0:FC - 1, c * P:(c + 1) * P],
                                         s[:, 0, 0:(FC - 1) * P].rearrange("p (k n) -> p k n", n=P)))
                    prep(dve.tensor_copy(wdT[0:FL, FC - 1, c * P:(c + 1) * P], s[0:FL, 0, (FC - 1) * P:FC * P]))
                else:
                    wT = wgT if m == "g" else wuT
                    prep(dve.tensor_copy(wT[:, :, c * P:c * P + rows],
                                         s[:, 0, 0:CD * P].rearrange("p (k n) -> p k n", n=P)[:, :, 0:rows]))
                out = {"g": sg_bc, "u": su_bc, "d": sd_bc}[m][:, c * P:c * P + rows]
                if m == "u":
                    prep(dve.scalar_tensor_tensor(out=out, in0=slot[WIDE][:, 0, 0:rows], scalar=4.0 / FP8_MAX,
                                                  in1=maskd[:, c * P:c * P + rows], op0=ALU.mult, op1=ALU.mult))
                else:
                    prep(dve.tensor_scalar(out, slot[WIDE][:, 0, 0:rows], (4.0 if m == "g" else 2.0) / FP8_MAX, None, ALU.mult))
                prep_settled()
            assert nv[0] == PREP_VALL

            fill(dve.memset(XQs[:].bitcast(F32), 0.0))
            fill(dve.memset(XKs[:].bitcast(F32), 0.0))
            assert n_fill[0] == N_FILLS, n_fill[0]

            count = {}

            def step(st, ins):
                count[st] += 1
                ins.then_inc(v_self[st], 1)

            def settled(st, g):
                wait_at(dve, v_self[st], g, V_STEPS[st], count[st])

            def lo_of(at, g, st, unit, out, src, hi, scale=None):
                wait_at(dve, hi_rdy[st], g, len(HI_TILES[st]), HI_TILES[st].index(unit) + 1)
                if scale is None:
                    dve.tensor_tensor(out, src, hi, ALU.subtract).then_inc(free_sem(at, *unit), 1)
                else:
                    dve.scalar_tensor_tensor(out=out, in0=src, scalar=scale, in1=hi, op0=ALU.mult,
                                             op1=ALU.subtract).then_inc(free_sem(at, *unit), 1)

            def round_rows(g, n_job, x, k, m, s):
                wait_at(dve, abs_rdy, g, 2 * G, n_job)
                step("D", dve.tensor_scalar(m, m, SUB, None, ALU.max))
                settled("D", g)
                dve.scalar_tensor_tensor(out=s, in0=x, scalar=k, in1=m, op0=ALU.mult, op1=ALU.add).then_inc(qs_rdy, 1)

            def part(at, g, i, unit):
                what = unit[0]
                st = {("ln", 1): "A", ("ln", 2): "C", ("ln", 3): "D"}.get(unit, None)
                ps = tile(at, *unit) if what in NARROW_TILES + WIDE_TILES else None
                if what == "ln":
                    n = unit[1]
                    x = (X1, X2, X3)[n - 1][i]
                    if n == 1:
                        wait_at(dve, x_ld, g, 16, 16)
                    for b in range(G):
                        step(st, dve.bn_stats(stats[n][:, b, :], x[:, b, :]))
                    settled(st, g)
                    stand(dve)
                    for b in range(G):
                        step(st, dve.bn_aggr(mv[n][:, b, :], stats[n][:, b, :]))
                    settled(st, g)
                    dve.tensor_scalar(ve[n][:], mv[n][:, :, 1], EPS, None, ALU.add).then_inc(ln_var[n], 1)
                elif what == "nrm":
                    n = unit[1]
                    x = (X1, X2, X3)[n - 1][i]
                    wait_at(dve, ln_rstd[n], g, 1, 1)
                    if n < 3:
                        for b in range(G):
                            ins = dve.tensor_scalar(XN[n][:, b, :], x[:, b, :], mv[n][:, b, 0:1], rstd[n][:, b:b + 1],
                                                    ALU.subtract, ALU.mult)
                        ins.then_inc(xn_rdy[n], 1)
                    else:
                        for b in range(G):
                            step("D", dve.scalar_tensor_tensor(out=XN[3][:, b, :], in0=x[:, b, :], scalar=mv[3][:, b, 0:1],
                                                               in1=mask_u[0:T, :], op0=ALU.subtract, op1=ALU.mult))
                        settled("D", g)
                        step("D", dve.tensor_reduce(ry[:], XN[3][:], AX.X, ALU.max, apply_absolute_value=True))
                        settled("D", g)
                        step("D", dve.reciprocal(rry[:], ry[:]))
                        settled("D", g)
                        step("D", dve.tensor_scalar(ky[:], rry[:], FP8_MAX, None, ALU.mult))
                        step("D", dve.scalar_tensor_tensor(out=sx[:], in0=ry[:], scalar=1.0 / FP8_MAX, in1=rstd[3][:],
                                                           op0=ALU.mult, op1=ALU.mult))
                        dve.tensor_scalar(kMy[:], rry[:], FP8_MAX * 2.0 ** 20, None, ALU.mult).then_inc(yk_rdy, 1)
                elif what == "xT":
                    n = unit[1]
                    hi, lo = (xT[n][k][:].rearrange("p c n -> p (c n)") for k in range(2))
                    lo_of(at, g, "AC"[n - 1], unit, lo, ps[:, 0, 0:CD * N], hi)
                elif what == "ctxT":
                    lo_of(at, g, "C", unit, CT[L:P, :], ps[0:L, 0, 0:N], CT[0:L, :])
                elif what in ("xq", "xk"):
                    r = RX[what == "xk"]
                    lo_of(at, g, "C", unit, r[:, 2:4, :].rearrange("p k n -> p (k n)"), ps[:, 0, 0:2 * N],
                          r[:, 0:2, :].rearrange("p k n -> p (k n)"), 1.0 / WS)
                elif what == "OT":
                    _, kind, b, j = unit
                    n = 4 if kind == "a" else CD
                    hi, lo = (OT[kind][k][:, n * j:n * (j + 1), :].rearrange("p c t -> p (c t)") for k in range(2))
                    lo_of(at, g, "B" if kind == "a" else "C", unit, lo, ps[:, 0, 0:n * T], hi)
                elif what == "qk":
                    n = unit[1]
                    k = n % 2
                    wait(dve, drained(at, *unit))
                    dve.tensor_tensor(abcos[:, k], ab[:, k], cosT[:].unsqueeze(1).broadcast_to([P, 2, N]), ALU.mult)
                    dve.tensor_tensor(ab[:, k], ab[:, k], sinT[:].unsqueeze(1).broadcast_to([P, 2, N]), ALU.mult).then_inc(rope_rot, 1)
                elif what == "split":
                    n = unit[1]
                    wait_at(dve, rope_hi, g, QUADS, n + 1)
                    dve.tensor_tensor(R[n % 2][:, 2:4, :], rsum[:, n % 2, :, :], R[n % 2][:, 0:2, :],
                                      ALU.subtract).then_inc(rope_lo, 1)
                elif what == "v":
                    wait(dve, filled(at, *unit))
                    dve.scalar_tensor_tensor(out=V[i][:, unit[1], 0:NKV * VS].rearrange("p (h w) -> p h w", w=VS)[:, :, 0:HD],
                                             in0=ps[0:T, 0, :].rearrange("p (h d) -> p h d", d=HD), scalar=1.0 / WS,
                                             in1=bv_bc[:].rearrange("p (h d) -> p h d", d=HD),
                                             op0=ALU.mult, op1=ALU.add).then_inc(free_sem(at, *unit), 1)
                elif what == "xv":
                    wait(dve, filled(at, *unit))
                    dve.tensor_scalar(XV[:, unit[1], 0:XH * XS].rearrange("p (h w) -> p h w", w=XS)[:, :, 0:XD],
                                      ps[0:T, 0, 0:D].rearrange("p (h d) -> p h d", d=XD),
                                      1.0 / WS, None, ALU.mult).then_inc(free_sem(at, *unit), 1)
                elif what == "M":
                    _, kind, b, j = unit
                    wait(dve, filled(at, *unit))
                    dve.tensor_reduce(mx[kind][b][:, 8 * j:8 * j + 8], ps[0:T, :, 0:4 * T].rearrange("p k (h n) -> p k h n", n=T),
                                      AX.X, ALU.max).then_inc(free_sem(at, *unit), 1)
                elif what == "mT":
                    _, kind, b, _ = unit
                    nh, scale = KINDS[kind]
                    st = "B" if kind == "a" else "C"
                    m, rest = MR[kind][b], mr_rest[kind][0:nh, :]
                    wait(dve, filled(at, *unit))
                    step(st, dve.tensor_scalar(m[0:nh, 0, :], ps[0:nh, 0, 0:T], -1.0, None, ALU.mult))
                    settled(st, g)
                    dve.scalar_tensor_tensor(out=rest, in0=ps[0:nh, 0, 0:T], scalar=-1.0, in1=m[0:nh, 0, :],
                                             op0=ALU.mult, op1=ALU.subtract).then_inc(free_sem(at, *unit), 1)
                    wait(dve, drained(at, *unit))
                    step(st, dve.tensor_copy(m[0:nh, 1, :], rest))
                    settled(st, g)
                    dve.tensor_tensor(m[0:nh, 2, :], rest, m[0:nh, 1, :], ALU.subtract).then_inc(mr_rdy[kind], 1)
                    if kind == "a":
                        dve.scalar_tensor_tensor(out=sm[b][:], in0=mx["a"][b][:], scalar=-scale, in1=sink_bc[:],
                                                 op0=ALU.mult, op1=ALU.add).then_inc(sm_rdy, 1)
                elif what == "V":
                    _, kind, b, j = unit
                    hd = HD if kind == "a" else XD
                    st = "B" if kind == "a" else "C"
                    wait(dve, filled(at, *unit))
                    v = ps[0:T, :, 0:4 * W].rearrange("p k (h w) -> p k h w", w=W)
                    r = rden[kind][:, j % 2].rearrange("p (k h) -> p k h", k=2)
                    if kind == "a":
                        wait_at(dve, es_rdy, g, G, b + 1)
                        step(st, dve.tensor_tensor(den[:, j % 2].rearrange("p (k h) -> p k h", k=2), v[:, :, :, hd],
                                                   es[b][:, 8 * j:8 * j + 8].rearrange("p (k h) -> p k h", k=2), ALU.add))
                        settled(st, g)
                        step(st, dve.reciprocal(rden[kind][:, j % 2], den[:, j % 2]))
                    else:
                        step(st, dve.reciprocal(r, v[:, :, :, hd]))
                    settled(st, g)
                    o = ON["a"][:, j % 2, :] if kind == "a" else ON["c"][:, 0, 8 * j * hd:8 * (j + 1) * hd]
                    dve.tensor_tensor(o.rearrange("p (k h d) -> p k h d", k=2, h=4),
                                      v[:, :, :, 0:hd], r.unsqueeze(3).broadcast_to([T, 2, 4, hd]),
                                      ALU.mult).then_inc(free_sem(at, *unit), 1)
                elif what == "Y":
                    _, kind, b, _ = unit
                    x, out = (X1, X2) if kind == "a" else (X2, X3)
                    wait(dve, filled(at, *unit))
                    if kind == "a" and b == 0:
                        wait_at(dve, xb_rdy, g, 1, 1)
                    dve.scalar_tensor_tensor(out=out[i][:, b, :], in0=ps[0:T, 0, 0:D], scalar=1.0 / WS, in1=x[i][:, b, :],
                                             op0=ALU.mult, op1=ALU.add).then_inc(free_sem(at, *unit), 1)
                    if b == G - 1:
                        wait(dve, drained(at, *unit))
                        stand(dve)
                elif what == "y":
                    b = unit[1]
                    round_rows(g, Q_Y[b], XN[3][:, b, :], ky[:, b:b + 1], yM, yS)
                elif what == "G":
                    b = unit[1]
                    wait(dve, filled(at, *unit))
                    dve.scalar_tensor_tensor(out=gs.rearrange("p (k n) -> p k n", k=2), in0=ps[0:T, :, 0:FH],
                                             scalar=sx[:, b:b + 1], in1=sg_bc[0:T, :].rearrange("p (k n) -> p k n", k=2),
                                             op0=ALU.mult, op1=ALU.mult).then_inc(free_sem(at, *unit), 1)
                elif what == "U":
                    wait(dve, filled(at, *unit))
                    dve.tensor_tensor(us.rearrange("p (k n) -> p k n", k=2), ps[0:T, :, 0:FH],
                                      su_bc[0:T, :].rearrange("p (k n) -> p k n", k=2), ALU.mult).then_inc(free_sem(at, *unit), 1)
                elif what == "h":
                    wait(dve, drained(at, "U", unit[1]))
                    wait_at(dve, th_rdy, g, G, unit[1] + 1)
                    dve.scalar_tensor_tensor(out=th, in0=th, scalar=1.0, in1=gs, op0=ALU.add,
                                             op1=ALU.mult).then_inc(w_rdy, 1)
                elif what == "hk":
                    b = unit[1]
                    c = slice(b, b + 1)
                    wait_at(dve, t_rdy, g, G, b + 1)
                    step("D", dve.tensor_reduce(rt[:, c], us, AX.X, ALU.max, apply_absolute_value=True))
                    settled("D", g)
                    step("D", dve.reciprocal(rrt[:, c], rt[:, c]))
                    settled("D", g)
                    step("D", dve.tensor_scalar(kt[:, c], rrt[:, c], FP8_MAX, None, ALU.mult))
                    step("D", dve.scalar_tensor_tensor(out=st_[:, c], in0=rt[:, c], scalar=1.0 / FP8_MAX,
                                                       in1=sx[:, c], op0=ALU.mult, op1=ALU.mult))
                    dve.tensor_scalar(kMt[:, c], rrt[:, c], FP8_MAX * 2.0 ** 20, None, ALU.mult).then_inc(tk_rdy, 1)
                elif what == "tq":
                    b = unit[1]
                    round_rows(g, Q_T[b], us, kt[:, b:b + 1], tM, tS)
                elif what == "D":
                    b = unit[1]
                    wait(dve, filled(at, *unit))
                    if b == 0:
                        wait_at(dve, out_st, g, 16 * G, 0)
                    dve.scalar_tensor_tensor(out=OUT[:, b, :], in0=ps[0:T, 0, 0:D], scalar=st_[:, b:b + 1],
                                             in1=sd_bc[0:T, :], op0=ALU.mult, op1=ALU.mult).then_inc(free_sem(at, *unit), 1)
                    wait(dve, drained(at, *unit))
                    dve.tensor_tensor(OUT[:, b, :], OUT[:, b, :], X3[i][:, b, :], ALU.add).then_inc(out_rdy, 1)

            def counted(at, g, i, unit):
                st = next(s for s in STAGES if any(u == unit for u, _ in UNITS[s]))
                if unit == next(u for u, _ in UNITS[st] if u):
                    count[st] = 0
                part(at, g, i, unit)
                if unit == UNITS[st][-1][0]:
                    assert count[st] == V_STEPS[st], (st, count[st])

            run(dve, counted)


def rope_tables():
    theta, scaling, ntk_alpha, ntk_beta, icl = 150000.0, 32.0, 1.0, 32.0, 128
    d_half = HD // 2
    freq = theta ** (np.arange(0, HD, 2, dtype=np.float32) / HD)
    concentration = 0.1 * math.log(scaling) + 1.0
    low = d_half * math.log(icl / (ntk_beta * 2 * math.pi)) / math.log(theta)
    high = d_half * math.log(icl / (ntk_alpha * 2 * math.pi)) / math.log(theta)
    interpolation = 1.0 / (scaling * freq)
    extrapolation = 1.0 / freq
    ramp = np.clip((np.arange(d_half, dtype=np.float32) - low) / (high - low), 0.0, 1.0)
    mask = 1.0 - ramp
    inv_freq = interpolation * (1.0 - mask) + extrapolation * mask
    freqs = np.outer(np.arange(T, dtype=np.float32), inv_freq)
    return (np.cos(freqs) * concentration).astype(np.float32).T, (np.sin(freqs) * concentration).astype(np.float32).T


def kernel(**inputs):
    import ml_dtypes
    import concourse.bacc as bacc
    from concourse.bass_utils import run_bass_kernel_spmd

    x = {k: np.asarray(v) for k, v in inputs.items()}

    def chunked(w):
        return w.T.reshape(-1, P, w.shape[0]).transpose(1, 0, 2)

    def rope_rows(w):
        return w.reshape(QUADS, 4, 2, HD // 2, -1).transpose(0, 2, 1, 3, 4).reshape(QUADS * 256, -1)

    def index_columns(idx, n):
        out = np.zeros(n * P, idx.dtype)
        out[:idx.size] = idx
        return out.reshape(n, P).T

    qk = (NH + NKV) * HD
    w, bias = x["L0_attn_qkv_w"], x["L0_attn_qkv_b"]
    cos, sin = rope_tables()
    causal = np.arange(T)[:, None] < np.arange(T)[None, :]
    mask = np.where(causal, np.float32(NEG), np.float32(0)).astype(ml_dtypes.bfloat16)
    arrays = {
        "x": x["x"].reshape(NG, G, T, D),
        "ctx": x["ctx_512"][:, :T].reshape(NG, G, T, L),
        "wqkT": chunked(rope_rows(w[:qk])),
        "wvT": chunked(w[qk:]),
        "woT": chunked(x["L0_attn_out_w"]).reshape(P, 16 * D),
        "wxqT": chunked(x["L0_xattn_Wq"]).reshape(P, CD * D),
        "wxoT": chunked(x["L0_xattn_Wout"]).reshape(P, CD * D),
        "wkvT": np.tile(x["L0_xattn_Wkv_expand"].T, (2, 1)),
        "w_gate": x["L0_ffn_w_gate"], "w_up": x["L0_ffn_w_up"], "w_down": x["L0_ffn_w_down"],
        "bqk": rope_rows(bias[:qk]).reshape(2 * QUADS, P).T,
        "bv": np.broadcast_to(bias[qk:], (T, 512)),
        "bo": np.broadcast_to(x["L0_attn_out_b"], (T, D)),
        "sinks": np.broadcast_to(x["L0_attn_sinks"], (T, NH)),
        "idx_d": index_columns(x["L0_ffn_down_reorder_index"], FC),
        "idx_u": index_columns(x["L0_ffn_up_reorder_index"], CD),
        "cosT": np.tile(cos / np.float32(WS), (4, G)), "sinT": np.tile(sin / np.float32(WS), (4, G)),
        "id32": np.eye(P, dtype=np.float32),
        "iota": np.tile(np.arange(F, dtype=np.float32), (P, 1)),
        "maskM": np.tile(mask, (1, 4)), "maskT": np.tile(mask.T, (1, NH)),
        "idb": np.concatenate([np.eye(T), np.ones((3, T))]).astype(ml_dtypes.bfloat16),
    }
    arrays = {k: np.ascontiguousarray(v) for k, v in arrays.items()}
    nc = bacc.Bacc("TRN2", target_bir_lowering=False, num_devices=1)
    io = {k: nc.dram_tensor(f"in_{k}", v.shape, mybir.dt.from_np(v.dtype), kind="ExternalInput").ap()
          for k, v in arrays.items()}
    io["scratch"] = nc.dram_tensor("rotated_qk", (NG, QUADS, P, 4, N), F16, kind="Internal").ap()
    io["xscratch"] = nc.dram_tensor("cross_qk", (NG, 2, 2, CD, P, N), F16, kind="Internal").ap()
    io["out"] = nc.dram_tensor("out", (NG, G, T, D), F32, kind="ExternalOutput").ap()
    build(nc, io)
    r = run_bass_kernel_spmd(nc, [{f"in_{k}": v for k, v in arrays.items()}], core_ids=[0])
    return r.results[0]["out"].reshape(B, T, D)
```

```python
from contextlib import ExitStack
import math

import numpy as np
import concourse.bass as bass
from concourse import mybir

F32, F16, BF16, I32 = mybir.dt.float32, mybir.dt.float16, mybir.dt.bfloat16, mybir.dt.int32
ALU, ACT, AX = mybir.AluOpType, mybir.ActivationFunctionType, mybir.AxisListType

P = 128
B, T, D = 32, 100, 256
G = 2
NG = B // G
N = G * T
CD = D // P
NH, NKV, HD = 32, 8, 64
QUADS = (NH + NKV) // 4
XH, XD, L = 16, 16, 64
F = 704
FC = -(-F // P)
FL = F - (FC - 1) * P
FH = F // 2
W = 96
XS = XD + 1
XVW = (XH - 1) * XS + W
VS = HD + 1
WS = 64.0
EPS = 1e-5
FP8_MAX = 448.0
SUB = 1.5 * 2.0 ** 14
NEG = -1e30
WIDE, NARROW = 3, 2
SLOTS = WIDE + NARROW

KINDS = {"a": (NH, 1.0 / math.sqrt(HD)), "c": (XH, 1.0 / math.sqrt(XD))}


QUAD_ORDER = [8, 9] + list(range(8))
GAP = None

ORDER = (
    (1, ('qk', 3)), (2, ('OT', 'a', 0, 1)), (2, ('S', 'a', 1, 0)), (3, ('mT', 'c', 0, 0)), (2, ('V', 'a', 0, 3)),
    (1, ('split', 2)), (2, ('OT', 'a', 0, 2)), (4, ('hk', 0)), (1, ('qk', 4)), (1, ('split', 3)), (2, ('cload',)),
    (2, ('S', 'a', 1, 1)), (1, ('qk', 5)), (2, ('OT', 'a', 0, 3)), (2, ('V', 'a', 1, 0)), (4, ('tq', 0)),
    (1, ('split', 4)), (2, ('S', 'a', 1, 2)), (1, ('qk', 6)), (1, ('split', 5)), (5, ('D', 1)), (3, ('S', 'c', 0, 0)),
    (3, ('M', 'c', 1, 0)), (1, ('qk', 7)), (3, ('M', 'c', 1, 1)), (3, ('V', 'c', 0, 0)), (4, ('tT', 0)),
    (1, ('split', 6)), (1, ('qk', 8)), (3, ('S', 'c', 0, 1)), (1, ('split', 7)), (1, ('qk', 9)),
    (3, ('mT', 'c', 1, 0)), (4, ('G', 1)), (1, ('split', 8)), (4, ('U', 1)), (1, ('split', 9)), (4, ('h', 1)),
    (2, ('V', 'a', 1, 1)), (2, ('Y', 'a', 0, 0)), (4, ('D', 0)), (3, ('V', 'c', 0, 1)), (2, ('OT', 'a', 1, 0)),
    (3, ('S', 'c', 1, 0)), (4, ('hk', 1)), (2, ('OT', 'a', 1, 1)), (1, ('qload', 0)), (2, ('S', 'a', 1, 3)),
    (2, ('V', 'a', 1, 2)), (2, ('ctxT',)), (3, ('OT', 'c', 0, 0)), (3, ('V', 'c', 1, 0)), (4, ('tq', 1)),
    (2, ('OT', 'a', 1, 2)), (3, ('S', 'c', 1, 1)), (2, ('V', 'a', 1, 3)), (3, ('V', 'c', 1, 1)), (2, ('xv', 1)),
    (3, ('Y', 'c', 0, 0)), (1, ('M', 'a', 0, 0)), (1, ('qload', 1)), (3, ('OT', 'c', 1, 0)), (1, ('M', 'a', 0, 1)),
    (2, ('OT', 'a', 1, 3)), (3, ('Y', 'c', 1, 0)), (1, ('M', 'a', 0, 2)), (3, ('ln', 3)), (1, ('M', 'a', 0, 3)),
    (2, ('xk',)), (3, ('nrm', 3)), (2, ('Y', 'a', 1, 0)), (0, ('load',)), (1, ('mT', 'a', 0, 0)), (2, ('ln', 2)),
    (1, ('v', 0)), (2, ('nrm', 2)), (1, ('v', 1)), (1, ('M', 'a', 1, 0)), (2, ('xT', 2)), (3, ('y', 0)),
    (0, ('ln', 1)), (1, ('M', 'a', 1, 1)), (2, ('xv', 0)), (1, ('S', 'a', 0, 0)), (2, ('xq',)), (3, ('y', 1)),
    (1, ('S', 'a', 0, 1)), (3, ('qT', 0)), (0, ('nrm', 1)), (1, ('V', 'a', 0, 0)), (4, ('tT', 1)), (3, ('G', 0)),
    (0, ('xT', 1)), (1, ('M', 'a', 1, 2)), (3, ('U', 0)), (1, ('M', 'a', 1, 3)), (0, ('qk', 0)), (3, ('h', 0)),
    (0, ('qk', 1)), (1, ('OT', 'a', 0, 0)), (2, ('xload',)), (1, ('S', 'a', 0, 2)), (1, ('mT', 'a', 1, 0)),
    (1, ('V', 'a', 0, 1)), (3, ('qT', 1)), (1, ('V', 'a', 0, 2)), (0, ('split', 0)), (0, ('qk', 2)),
    (0, ('split', 1)), (1, ('S', 'a', 0, 3)), (2, ('M', 'c', 0, 0)), (2, ('M', 'c', 0, 1)),
)
NARROW_TILES = ("xT", "qk", "v", "mT", "OT", "Y", "ctxT", "xq", "xk", "xv", "qT", "tT", "D")
WIDE_TILES = ("M", "S", "V", "G", "U")
HI_TILES = ("xT", "OT", "ctxT", "xq", "xk")


LAGS = max(lag for lag, _ in ORDER)


def body_units(n):
    return [(-lag, unit) for lag, unit in ORDER if 0 <= n - lag < NG]


def bodies():
    first = LAGS + 1
    loops = (NG - first) // 2
    out = [(f"body{n}", n) for n in range(first)] + [("loop0", first), ("loop1", first + 1)]
    out += [(f"body{n}", n) for n in range(first + 2 * loops, NG + LAGS)]
    return out, loops


Q_Y = [1, 2]
Q_T = [3, 4]

PREP_V0 = 2 + FC + CD + 4
PREP_N = [11] * (2 * FC) + [12] * CD
VBASE = [PREP_V0 + sum(PREP_N[:n]) for n in range(len(PREP_N))]
PREP_VALL = PREP_V0 + sum(PREP_N)


V_STEPS = 3 * 2 * G + 2 * G + 2 * G + 2 * G * NH // 8 + G * XH // 8 + (G + 4) + 2 * G + 4 * G
CONST_ALL = 16 * 15
N_FILLS = 2 + 2 + 3 + 3 * G + 2 + 2


def build(nc, io):
    order, loops = bodies()
    units = {name: body_units(n) for name, n in order}
    slot_of, before, hi_at = {}, {}, {}
    turn = {"wide": 0, "narrow": 0}
    for _, unit in ORDER:
        if unit[0] in WIDE_TILES:
            slot_of[unit] = turn["wide"] % WIDE
            turn["wide"] += 1
        elif unit[0] in NARROW_TILES:
            slot_of[unit] = WIDE + turn["narrow"] % NARROW
            turn["narrow"] += 1
    per_loop = [2 * sum(s == x for x in slot_of.values()) for s in range(SLOTS)]
    hi_per_loop = 2 * sum(unit[0] in HI_TILES for _, unit in ORDER)
    used, hi_used = [0] * SLOTS, 0
    for name, _ in order:
        for _, unit in units[name]:
            if unit in slot_of:
                before[name, unit] = used[slot_of[unit]]
                used[slot_of[unit]] += 1
            if unit[0] in HI_TILES:
                hi_at[name, unit] = hi_used
                hi_used += 1
        if name == "loop1":
            used = [u + (loops - 1) * p for u, p in zip(used, per_loop)]
            hi_used += (loops - 1) * hi_per_loop

    with ExitStack() as ctx:
        def sb(name, shape, dt):
            return ctx.enter_context(nc.sbuf_tensor(name, shape, dt))

        def sem(name):
            return ctx.enter_context(nc.semaphore(name))

        slot = [ctx.enter_context(nc.psum_tensor(f"slot{s}", [P, 2 if s < WIDE else 1, 512], F32)) for s in range(SLOTS)]

        wqk = [sb(f"wqk_{k}", [P, CD, QUADS * 256], F16) for k in ("hi", "lo")]
        wv = [sb(f"wv_{k}", [P, CD, 512], F16) for k in ("hi", "lo")]
        wo = [sb(f"wo_{k}", [P, 16, D], F16) for k in ("hi", "lo")]
        wxq = [sb(f"wxq_{k}", [P, CD, D], F16) for k in ("hi", "lo")]
        wxo = [sb(f"wxo_{k}", [P, CD, D], F16) for k in ("hi", "lo")]
        wkv = [sb(f"wkv_{k}", [P, 512], F16) for k in ("hi", "lo")]
        wgT = sb("wgT", [P, CD, F], F16)
        wuT = sb("wuT", [P, CD, F], F16)
        wdT = sb("wdT", [P, FC, D], F16)
        sg_bc = sb("sg_bc", [P, F], F32)
        su_bc = sb("su_bc", [P, F], F32)
        sd_bc = sb("sd_bc", [P, D], F32)
        mask_u = sb("mask_u", [P, D], F32)
        cosT = sb("cosT", [P, N], F32)
        sinT = sb("sinT", [P, N], F32)
        bqk = sb("bqk", [P, 2 * QUADS], F32)
        bv_bc = sb("bv_bc", [T, 512], F32)
        bo_bc = sb("bo_bc", [T, D], F32)
        sink_bc = sb("sink_bc", [T, NH], F32)
        id32 = sb("id32", [P, P], F32)
        id16 = sb("id16", [P, P], F16)
        idb = sb("idb", [T + 3, T], BF16)
        maskM = sb("maskM", [T, 4 * T], BF16)
        half = sb("half", [T, G], F32)
        MB = {"a": [sb(f"maskT_m{i}", [T + 3, NH * T], BF16) for i in range(2)]}
        MB["c"] = [sb("maskT_mc", [T + 3, XH * T], BF16)] * 2

        X1 = [sb(f"X1_{i}", [T, G, D], F32) for i in range(2)]
        X2 = [sb(f"X2_{i}", [T, G, D], F32) for i in range(2)]
        X3 = [sb(f"X3_{i}", [T, G, D], F32) for i in range(2)]
        XN = {n: sb(f"XN{n}", [T, G, D], F32) for n in (1, 2, 3)}
        OUT = sb("OUT", [T, G, D], F32)
        xT = {n: [sb(f"xT{n}_{k}", [P, CD, N], F16) for k in ("hi", "lo")] for n in (1, 2)}
        ROT = sb("rope", [P, 2 * 2 * 2 * N], F32)
        SUM = sb("rope_sums", [P, 2 * 2 * N], F32)
        R = [sb(f"split{i}", [P, 4, N], F16) for i in range(2)]
        RX = [sb(f"xsplit{i}", [P, 4, N], F16) for i in range(2)]
        QA = [sb(f"QA{b}", [P, NH * T], F16) for b in range(G)]
        KA = [sb(f"KA{b}", [P, NKV, T], F16) for b in range(G)]
        KB = [sb(f"KB{b}", [P, NKV, T], F16) for b in range(G)]
        V = [sb(f"V{i}", [T, G, NKV * VS + W - VS], F32) for i in range(2)]
        PR = {"a": sb("probs", [T, 2, 8 * T], F32), "c": sb("xprobs", [T, 1, 8 * T], F32)}
        ON = {"a": sb("attn_out", [T, 2, 8 * HD], F32), "c": sb("xattn_out", [T, 1, D], F32)}
        OT = {"a": [sb(f"attn_outT_{k}", [P, 16, T], F16) for k in ("hi", "lo")],
              "c": [sb(f"xattn_outT_{k}", [P, CD, T], F16) for k in ("hi", "lo")]}
        XQs, XKs = sb("XQ", [P, XH * N], F16), sb("XK", [P, XH * N], F16)
        C0 = sb("ctx_rows", [T, G, L], F32)
        CT = sb("ctxT", [P, N], F16)
        XV = sb("XV", [T, G, XVW], F32)
        qT = sb("qT", [P, CD, T], F16)
        tT = sb("tT", [P, FC, T], F16)
        stats = {n: sb(f"stats{n}", [T, G, 6], F32) for n in (1, 2, 3)}
        mv = {n: sb(f"mv{n}", [T, G, 2], F32) for n in (1, 2, 3)}
        ve = {n: sb(f"var_eps{n}", [T, G], F32) for n in (1, 2, 3)}
        rstd = {n: sb(f"rstd{n}", [T, G], F32) for n in (1, 2, 3)}
        mx = {k: [sb(f"row_max_{k}{i}", [T, NH], F32) for i in range(2)] for k in "ac"}
        sm = [sb(f"sink_shift{i}", [T, NH], F32) for i in range(2)]
        es = [sb(f"sink_exp{i}", [T, NH], F32) for i in range(2)]
        MR = {k: [sb(f"neg_max_{k}{i}", [NH, 3, T], BF16) for i in range(2)] for k in "ac"}
        mr_rest = {k: sb(f"mr_rest_{k}", [NH, T], F32) for k in "ac"}
        den = sb("den", [T, 2, 8], F32)
        rden = {k: sb(f"rden_{k}", [T, 2, 8], F32) for k in "ac"}
        ry, rry, ky, kMy, sx = (sb(n, [T, G], F32) for n in ("ry", "rry", "ky", "kMy", "sx"))
        rt, rrt, kt, kMt, st_ = (sb(n, [T, G], F32) for n in ("rt", "rrt", "kt", "kMt", "st"))
        FB = sb("ffn", [P, 3 * F], F32)
        gs, us, th = (FB[0:T, i * F:(i + 1) * F] for i in range(3))
        tM, tS = th, gs
        YMS = sb("y_round", [T, 2 * D], F32)
        yM, yS = YMS[:, 0:D], YMS[:, D:2 * D]
        tq = sb("tq", [T, F], F16)
        yq = sb("yq", [T, G, D], F16)

        ab = ROT[:, 0:4 * N].rearrange("p (i k n) -> p i k n", i=2, k=2)
        abcos = ROT[:, 4 * N:8 * N].rearrange("p (i k n) -> p i k n", i=2, k=2)
        rsum = SUM[:].rearrange("p (i k n) -> p i k n", i=2, k=2)
        qa = [QA[b][:].rearrange("p (h t) -> p h t", h=NH) for b in range(G)]
        XQ = XQs[:].rearrange("p (h n) -> p h n", h=XH)
        XK = XKs[:].rearrange("p (h n) -> p h n", h=XH)
        stage = [QA[i][:].bitcast(F32)[:, 0:1024] for i in range(2)]
        wf = [x[:].bitcast(F32)[:, i * F:(i + 1) * F] for x in (XQs, XKs) for i in range(2)]
        wq = R[0][:].rearrange("p k n -> p (k n)")
        cnt4 = FB[:, 0:F]
        maskd = FB[:, F:2 * F]
        cnt4u = FB[:, 2 * F:2 * F + D]
        onehot = ROT[:].bitcast(BF16)[:, 0:F]
        iota = ROT[:, F:2 * F]
        ones_b = SUM[:].bitcast(BF16)[:, 0:P]
        idx_d = sb("idx_d", [P, FC], I32)
        idx_u = sb("idx_u", [P, CD], I32)
        idxf = sb("idxf", [P, FC + CD], F32)
        wr = sb("wr", [P, 4], F32)
        wsb = SUM[:, P:2 * P]

        const_ld = sem("const_ld")
        stage_ld = [sem(f"stage_ld{i}") for i in range(2)]
        hi_done, lo_done = sem("prep_hi_done"), sem("prep_lo_done")
        fills = sem("fills")
        prep_v = sem("prep_v")
        prep_p = sem("prep_p")
        prep_a = sem("prep_a")
        prep_abs = sem("prep_abs")
        wrow_ld = sem("wrow_ld")
        wdown_ld = sem("wdown_ld")
        full = [sem(f"slot_full{s}") for s in range(SLOTS)]
        free = [sem(f"slot_free{s}") for s in range(SLOTS)]
        x_ld, c_ld, out_st = sem("x_ld"), sem("ctx_ld"), sem("out_st")
        ln_var, ln_rstd, xn_rdy = ({n: sem(f"{w}{n}") for n in (1, 2, 3)} for w in ("ln_var", "ln_rstd", "xn_rdy"))
        hi_rdy = sem("hi_rdy")
        rope_rot, rope_sum, rope_hi, rope_lo = sem("rope_rot"), sem("rope_sum"), sem("rope_hi"), sem("rope_lo")
        sc_w = [sem(f"scratch_write{i}") for i in range(2)]
        xsc_w = sem("x_scratch_write")
        qa_ld = [sem(f"qa_ld{i}") for i in range(2)]
        xqk_ld = sem("xqk_ld")
        s_done = [sem(f"self_scores_done{b}") for b in range(G)]
        mr_rdy = {k: sem(f"mr_rdy_{k}") for k in "ac"}
        mb_ld = {k: [sem(f"mb_ld_{k}{i}") for i in range(2)] for k in "ac"}
        sm_rdy, es_rdy = sem("sm_rdy"), sem("es_rdy")
        xb_rdy = sem("xb_rdy")
        yk_rdy, tk_rdy = sem("yk_rdy"), sem("tk_rdy")
        abs_rdy, qs_rdy, q_rdy = sem("abs_rdy"), sem("qs_rdy"), sem("q_rdy")
        th_rdy, w_rdy, t_rdy = sem("th_rdy"), sem("w_rdy"), sem("t_rdy")
        out_rdy = sem("out_rdy")
        v_self = sem("dve_step")
        stood = sem("stood")

        def wait_at(eng, semaphore, g, per_group, k):
            it, c = g
            if it is not None:
                assert c * per_group + k > 0
                eng.wait_ge(semaphore, it * (2 * per_group) + (c * per_group + k))
            elif c * per_group + k > 0:
                eng.wait_ge(semaphore, c * per_group + k)

        def index(g):
            return g[1] if g[0] is None else g[0] * 2 + g[1]

        def position(at, t, groups_back):
            name, it, unit = at
            bodies_back = groups_back + lag_of[unit] - lag_of[t]
            assert bodies_back in (0, 1), (unit, t)
            names = [n for n, _ in order]
            name = names[names.index(name) - bodies_back]
            late = (loops - 1) * per_loop[slot_of[t]] if bodies_back and name == "loop1" else 0
            return it, slot_of[t], before[name, t] + late

        def claim(at, *t):
            it, n, k = position(at, t, 0)
            return free[n], it, n, k + 1

        def filled(at, *t):
            it, n, k = position(at, t, 0)
            return full[n], it, n, k + 1

        def drained(at, *t, groups_back=0):
            it, n, k = position(at, t, groups_back)
            return free[n], it, n, k + 2

        def wait(eng, *positions):
            for i, (s, it, n, k) in enumerate(positions):
                if not any(s is s2 and (k2, j) > (k, i) for j, (s2, _, _, k2) in enumerate(positions) if j != i):
                    eng.wait_ge(s, k if it is None else it * per_loop[n] + k)

        def tile(at, *t):
            return slot[slot_of[t]]

        def full_sem(at, *t):
            return full[slot_of[t]]

        def free_sem(at, *t):
            return free[slot_of[t]]

        def run(eng, part, body_done=lambda name: None):
            def body(name, n, it):
                for lag, unit in units[name]:
                    c = n + lag
                    part((name, it, unit), (it, c), c % 2, unit)
            i = 0
            while i < len(order):
                if order[i][0] == "loop0":
                    with eng.Fori(0, loops) as it:
                        body("loop0", order[i][1], it)
                        body("loop1", order[i + 1][1], it)
                    body_done("loop1")
                    i += 2
                else:
                    body(order[i][0], order[i][1], None)
                    i += 1

        def stand(eng):
            eng.sem_inc(stood, 1)

        consts = [(cosT[:], io["cosT"]), (sinT[:], io["sinT"]), (bqk[:], io["bqk"]), (bv_bc[:], io["bv"]),
                  (bo_bc[:], io["bo"]), (sink_bc[:], io["sinks"]), (id32[:], io["id32"]),
                  (iota, io["iota"]), (idx_d[:], io["idx_d"]), (idx_u[:], io["idx_u"])]
        splits = [(io["wqkT"][:, c, 1024 * i:min(1024 * i + 1024, 2560)],
                   wqk[0][:, c, 1024 * i:min(1024 * i + 1024, 2560)],
                   wqk[1][:, c, 1024 * i:min(1024 * i + 1024, 2560)], min(1024, 2560 - 1024 * i))
                  for c in range(CD) for i in range(3)]
        splits += [(io["wvT"][:, c, :], wv[0][:, c, :], wv[1][:, c, :], 512) for c in range(CD)]
        splits += [(io["woT"][:, 1024 * i:1024 * i + 1024], wo[0][:].rearrange("p c d -> p (c d)")[:, 1024 * i:1024 * i + 1024],
                    wo[1][:].rearrange("p c d -> p (c d)")[:, 1024 * i:1024 * i + 1024], 1024) for i in range(4)]
        splits += [(io["wxqT"], wxq[0][:].rearrange("p c d -> p (c d)"), wxq[1][:].rearrange("p c d -> p (c d)"), 512),
                   (io["wxoT"], wxo[0][:].rearrange("p c d -> p (c d)"), wxo[1][:].rearrange("p c d -> p (c d)"), 512),
                   (io["wkvT"], wkv[0][:], wkv[1][:], 512)]
        NS = len(splits)
        wrows = [(m, c, P if c < FC - 1 else FL, D) for m in ("g", "u") for c in range(FC)]
        wrows += [("d", c, P, F) for c in range(CD)]
        sc = io["scratch"]
        xsc = io["xscratch"]

        lag_of = {unit: lag for lag, unit in ORDER}

        block = ctx.enter_context(nc.Block())

        @block.sync
        def _(sp):
            for dst, src in consts:
                sp.dma_start(dst, src).then_inc(const_ld, 16)
            for m in MB["a"] + MB["c"][:1]:
                sp.dma_start(m[0:T, :], io["maskT"][:, 0:m.shape[1]]).then_inc(const_ld, 16)
            sp.dma_start(maskM[:], io["maskM"]).then_inc(const_ld, 16)
            sp.dma_start(idb[:], io["idb"]).then_inc(const_ld, 16)
            for n, (src, _hi, _lo, cols) in enumerate(splits):
                if n >= 2:
                    sp.wait_ge(lo_done, n - 1)
                sp.dma_start(stage[n % 2][:, 0:cols], src).then_inc(stage_ld[n % 2], 16)
            for n in range(CD):
                sp.wait_ge(prep_v, VBASE[2 * FC + n - 1] + 1)
                sp.dma_start(wf[0], io["w_down"][P * n:P * n + P, :]).then_inc(wdown_ld, 16)

            sp.wait_ge(lo_done, NS + 1)
            sp.wait_ge(fills, N_FILLS)

            def part(at, g, i, unit):
                what = unit[0]
                if what == "load":
                    if g[1] >= 2:
                        wait(sp, drained(at, "Y", "a", G - 1, 0, groups_back=2))
                        stand(sp)
                    sp.dma_start(X1[i][:], io["x"][index(g)].rearrange("b t d -> t b d")).then_inc(x_ld, 16)
                elif what == "split":
                    n = unit[1]
                    wait_at(sp, rope_lo, g, QUADS, n + 1)
                    stand(sp)
                    sp.dma_start(sc[index(g), QUAD_ORDER[n]], R[n % 2][:]).then_inc(sc_w[n % 2], 16)
                elif what == "qload":
                    b = unit[1]
                    if b == 0:
                        for p in range(2):
                            wait_at(sp, sc_w[p], g, 8 * QUADS, 8 * QUADS)
                            stand(sp)
                    wait_at(sp, s_done[b], g, 1, 0)
                    stand(sp)
                    for k in range(4):
                        src = sc[index(g), 0:8, :, k, b * T:(b + 1) * T].rearrange("u (h f) t -> f (u h) t", h=4)
                        sp.dma_start(qa[b][32 * k:32 * k + 32], src).then_inc(qa_ld[b], 16)
                    for row, k, dst in ((0, 0, KA), (32, 1, KA), (64, 0, KA), (96, 1, KA), (0, 2, KB), (32, 3, KB)):
                        src = sc[index(g), 8:10, :, k, b * T:(b + 1) * T].rearrange("u (h f) t -> f (u h) t", h=4)
                        sp.dma_start(dst[b][row:row + 32], src).then_inc(qa_ld[b], 16)
                elif what == "mT":
                    _, kind, b, _ = unit
                    h = KINDS[kind][0]
                    wait_at(sp, mr_rdy[kind], g, G, b + 1)
                    stand(sp)
                    for k in range(3):
                        sp.dma_start(MB[kind][b][T + k:T + k + 1, 0:h * T], MR[kind][b][0:h, k, :]).then_inc(mb_ld[kind][b], 16)
                elif what == "cload":
                    if g[1] >= 1:
                        wait(sp, drained(at, "ctxT", groups_back=1))
                        stand(sp)
                    sp.dma_start(C0[:], io["ctx"][index(g)].rearrange("b t d -> t b d")).then_inc(c_ld, 16)
                elif what == "xload":
                    for n, t in enumerate(("xq", "xk")):
                        wait(sp, drained(at, t))
                        stand(sp)
                        sp.dma_start(xsc[index(g), n].rearrange("k c p n -> p (k c) n"), RX[n][:]).then_inc(xsc_w, 16)
                    wait_at(sp, xsc_w, g, 32, 32)
                    stand(sp)
                    for n, dst in ((0, XQ), (1, XK)):
                        for row, k in enumerate((0, 1, 0) if n == 0 else (0, 0, 1)):
                            src = xsc[index(g), n, k].rearrange("c (h r) n -> r (c h) n", h=8)
                            sp.dma_start(dst[16 * row:16 * row + 16], src).then_inc(xqk_ld, 16)
                elif what == "D":
                    b = unit[1]
                    wait_at(sp, out_rdy, g, G, b + 1)
                    stand(sp)
                    sp.dma_start(io["out"][index(g), b], OUT[:, b, :]).then_inc(out_st, 16)

            run(sp, part)
            sp.wait_ge(out_st, 16 * B)

        @block.tensor
        def _(pe):
            for which, chunks, cols, o in (("d", FC, F, 0), ("u", CD, D, FC)):
                for c in range(chunks):
                    k = FL if which == "d" and c == FC - 1 else P
                    pe.wait_ge(prep_v, 3 + o + c)
                    for h in range(2):
                        w = cols // 2
                        last = pe.matmul(slot[0 if which == "d" else 1][:, h, 0:w], ones_b[0:k],
                                         onehot[0:k, h * w:(h + 1) * w], start=(c == 0), stop=(c == chunks - 1))
                    last.then_inc(prep_p, 1)
            for n, (m, c, rows, cols) in enumerate(wrows):
                pe.wait_ge(prep_a, n + 1)
                s = slot[2][:].bitcast(F16)
                if n:
                    pe.wait_ge(prep_v, VBASE[n])
                for k in range(-(-cols // P)):
                    kk = min(P, cols - k * P)
                    pe.transpose(s[0:kk, 0, k * P:k * P + rows], wq[0:rows, k * P:k * P + kk],
                                 id16[0:rows, 0:rows])
                pe.matmul(slot[WIDE][:, 0, 0:rows], wsb[0:rows], id32[0:rows, 0:rows],
                          start=True, stop=True).then_inc(prep_p, 1)
            pe.wait_ge(prep_v, PREP_VALL)
            pe.wait_ge(lo_done, NS + 1)

            def product(out, a, b, pairs, first=True, last=True):
                for i, (x, y) in enumerate(pairs):
                    ins = pe.matmul(out, a(x), b(y), start=(first and i == 0), stop=(last and i == len(pairs) - 1))
                return ins

            HL = ((0, 0), (0, 1), (1, 0))

            def columns(b):
                return slice(b * T, (b + 1) * T)

            def scores_for_max(at, g, kind, b, j):
                t = ("M", kind, b, j)
                wait(pe, claim(at, *t))
                if kind == "a" and j == 0:
                    wait_at(pe, qa_ld[b], g, 160, 160)
                if kind == "c" and j == 0 and b == 0:
                    wait_at(pe, xqk_ld, g, 96, 96)
                for k in range(2):
                    pe.matmul(tile(at, *t)[0:T, k, 0:4 * T], idb[0:T, :], maskM[:], start=True, stop=False)
                    for h in range(4):
                        head = 8 * j + 4 * k + h
                        if kind == "a":
                            q, key = qa[b][:, head, :], KA[b][:, head // 4, :]
                        else:
                            q, key = XQ[:, head, columns(b)], XK[:, head, columns(b)]
                        ins = pe.matmul(tile(at, *t)[0:T, k, h * T:(h + 1) * T], q, key, start=False, stop=(h == 3))
                ins.then_inc(full_sem(at, *t), 1)

            def scores(at, g, kind, b, j):
                t = ("S", kind, b, j)
                wait(pe, claim(at, *t))
                if j == 0:
                    wait_at(pe, mb_ld[kind][b], g, 48, 48)
                for k in range(2):
                    h0 = 8 * j + 4 * k
                    out = tile(at, *t)[0:T, k, 0:4 * T]
                    pe.matmul(out, idb[:], MB[kind][b][:, h0 * T:(h0 + 4) * T], start=True, stop=False)
                    if kind == "a":
                        q = qa[b][:, h0:h0 + 4, :]
                        pe.matmul(out, KA[b][:, h0 // 4, :], q, start=False, stop=False)
                        ins = pe.matmul(out, KB[b][:, h0 // 4, :], q, start=False, stop=True)
                    else:
                        for h in range(4):
                            ins = pe.matmul(tile(at, *t)[0:T, k, h * T:(h + 1) * T], XK[:, h0 + h, columns(b)],
                                            XQ[:, h0 + h, columns(b)], start=False, stop=(h == 3))
                ins.then_inc(full_sem(at, *t), 1)

            def values(at, g, i, kind, b, j):
                t = ("V", kind, b, j)
                last_tile = KINDS[kind][0] // 8 - 1
                needs = [claim(at, *t), drained(at, "S", kind, b, j)]
                if kind == "c":
                    needs.append(drained(at, "xv", b))
                wait(pe, *needs)
                for n in range(8):
                    head = 8 * j + n
                    if kind == "a":
                        v = V[i][:, b, head // 4 * VS:head // 4 * VS + W]
                    else:
                        v = XV[:, b, head * XS:head * XS + W]
                    p = j % 2 if kind == "a" else 0
                    ins = pe.matmul(tile(at, *t)[0:T, n // 4, (n % 4) * W:(n % 4) * W + W],
                                    PR[kind][:, p, n * T:(n + 1) * T], v, start=True, stop=True)
                    if n == 0 and kind == "a" and j == last_tile:
                        ins.then_inc(s_done[b], 1)
                ins.then_inc(full_sem(at, *t), 1)

            def outputs_to_columns(at, kind, b, j):
                t = ("OT", kind, b, j)
                n = 4 if kind == "a" else CD
                wait(pe, claim(at, *t),
                     drained(at, "V", kind, b, j if kind == "a" else 1))
                for c in range(n):
                    ins = pe.transpose(tile(at, *t)[:, 0, c * T:(c + 1) * T],
                                       ON[kind][:, j % 2, c * P:(c + 1) * P], id32[0:T, 0:T])
                ins.then_inc(full_sem(at, *t), 1)

            def project(at, kind, b):
                t = ("Y", kind, b, 0)
                n, w = (16, wo) if kind == "a" else (CD, wxo)
                wait(pe, claim(at, *t), *(drained(at, "OT", kind, b, j) for j in range(4 if kind == "a" else 1)))
                for c in range(n):
                    ins = product(tile(at, *t)[0:T, 0, 0:D], lambda i: OT[kind][i][:, c, :], lambda i: w[i][:, c, :],
                                  HL, c == 0, c == n - 1)
                ins.then_inc(full_sem(at, *t), 1)

            def part(at, g, i, unit):
                what = unit[0]
                if what in ("xT", "qk", "v", "ctxT", "xq", "xk", "xv", "qT", "G", "U", "tT", "D"):
                    ps, done = tile(at, *unit), full_sem(at, *unit)
                if what == "xT":
                    n = unit[1]
                    wait_at(pe, xn_rdy[n], g, 1, 1)
                    wait(pe, claim(at, *unit))
                    for c in range(CD):
                        for b in range(G):
                            ins = pe.transpose(ps[:, 0, c * N + b * T:c * N + (b + 1) * T], XN[n][:, b, c * P:(c + 1) * P],
                                               id32[0:T, 0:T])
                    ins.then_inc(done, 1)
                elif what == "qk":
                    wait(pe, claim(at, *unit), drained(at, "xT", 1))
                    for h in range(2):
                        col = QUAD_ORDER[unit[1]] * 256 + h * P
                        for c in range(CD):
                            ins = product(ps[:, 0, h * N:(h + 1) * N], lambda k: wqk[k][:, c, col:col + P],
                                          lambda k: xT[1][k][:, c, :], HL, c == 0, c == CD - 1)
                    ins.then_inc(done, 1)
                elif what == "v":
                    wait(pe, claim(at, *unit))
                    for c in range(CD):
                        ins = product(ps[0:T, 0, :], lambda k: xT[1][k][:, c, columns(unit[1])], lambda k: wv[k][:, c, :],
                                      HL, c == 0, c == CD - 1)
                    ins.then_inc(done, 1)
                elif what == "M":
                    scores_for_max(at, g, *unit[1:])
                elif what == "mT":
                    _, kind, b, _ = unit
                    h = KINDS[kind][0]
                    wait(pe, claim(at, *unit), drained(at, "M", kind, b, h // 8 - 1))
                    pe.transpose(tile(at, *unit)[0:h, 0, 0:T], mx[kind][b][:, 0:h], id32[0:T, 0:T]).then_inc(full_sem(at, *unit), 1)
                elif what == "S":
                    scores(at, g, *unit[1:])
                elif what == "V":
                    values(at, g, i, *unit[1:])
                elif what == "OT":
                    outputs_to_columns(at, *unit[1:])
                elif what == "Y":
                    project(at, *unit[1:3])
                elif what == "ctxT":
                    wait_at(pe, c_ld, g, 16, 16)
                    wait(pe, claim(at, *unit))
                    stand(pe)
                    for b in range(G):
                        ins = pe.transpose(ps[0:L, 0, columns(b)], C0[:, b, :], id32[0:T, 0:T])
                    ins.then_inc(done, 1)
                elif what == "xq":
                    wait(pe, claim(at, *unit), drained(at, "xT", 2))
                    for m in range(CD):
                        for c in range(CD):
                            ins = product(ps[:, 0, m * N:(m + 1) * N], lambda k: wxq[k][:, c, m * P:(m + 1) * P],
                                          lambda k: xT[2][k][:, c, :], HL, c == 0, c == CD - 1)
                    ins.then_inc(done, 1)
                elif what == "xk":
                    wait(pe, claim(at, *unit), drained(at, "ctxT"))
                    for m in range(CD):
                        ins = product(ps[:, 0, m * N:(m + 1) * N], lambda k: wkv[k][:, m * P:(m + 1) * P], lambda k: CT[:],
                                      ((0, 0), (1, 0)))
                    ins.then_inc(done, 1)
                elif what == "xv":
                    wait(pe, claim(at, *unit))
                    product(ps[0:T, 0, 0:D], lambda k: CT[:, columns(unit[1])], lambda k: wkv[k][:, D:2 * D],
                            ((0, 0), (0, 1))).then_inc(done, 1)
                elif what == "qT":
                    wait(pe, claim(at, *unit))
                    wait_at(pe, q_rdy, g, 2 * G, Q_Y[unit[1]])
                    for c in range(CD):
                        ins = pe.transpose(ps[:].bitcast(F16)[:, 0, c * T:(c + 1) * T], yq[:, unit[1], c * P:(c + 1) * P],
                                           id16[0:T, 0:T])
                    ins.then_inc(done, 1)
                elif what in ("G", "U"):
                    w = wgT if what == "G" else wuT
                    wait(pe, claim(at, *unit), drained(at, "qT", unit[1]))
                    for h in range(2):
                        for c in range(CD):
                            ins = pe.matmul(ps[0:T, h, 0:FH], qT[:, c, :], w[:, c, h * FH:(h + 1) * FH],
                                            start=(c == 0), stop=(c == CD - 1))
                    ins.then_inc(done, 1)
                elif what == "tT":
                    wait(pe, claim(at, *unit))
                    wait_at(pe, q_rdy, g, 2 * G, Q_T[unit[1]])
                    for c in range(FC):
                        k = P if c < FC - 1 else FL
                        ins = pe.transpose(ps[:].bitcast(F16)[0:k, 0, c * T:(c + 1) * T], tq[:, c * P:c * P + k], id16[0:T, 0:T])
                    ins.then_inc(done, 1)
                elif what == "D":
                    wait(pe, claim(at, *unit), drained(at, "tT", unit[1]))
                    for c in range(FC):
                        k = P if c < FC - 1 else FL
                        ins = pe.matmul(ps[0:T, 0, 0:D], tT[0:k, c, :], wdT[0:k, c, :], start=(c == 0), stop=(c == FC - 1))
                    ins.then_inc(done, 1)

            run(pe, part)

        @block.scalar
        def _(act):
            for n, (_src, hi, _lo, cols) in enumerate(splits):
                act.wait_ge(stage_ld[n % 2], 16 * (n // 2 + 1))
                act.activation(hi, stage[n % 2][:, 0:cols], ACT.Copy, scale=WS).then_inc(hi_done, 1)
            for n, (m, c, rows, cols) in enumerate(wrows):
                act.wait_ge(prep_v, VBASE[n] + 5)
                act.activation(wf[2][0:rows, 0:cols], wf[1][0:rows, 0:cols], ACT.Abs,
                               scale=wr[0:rows, 3:4]).then_inc(prep_abs, 1)
                act.wait_ge(prep_v, VBASE[n] + 9)
                act.activation(wsb[0:rows], id32[0:rows, :], ACT.Identity, bias=wr[0:rows, 0:1],
                               scale=0.0).then_inc(prep_a, 1)

            def part(at, g, i, unit):
                what = unit[0]
                if what in ("xT", "ctxT", "xq", "xk", "OT"):
                    ps = tile(at, *unit)
                    scale = 1.0
                    if what == "xT":
                        out, src = xT[unit[1]][0][:].rearrange("p c n -> p (c n)"), ps[:, 0, 0:CD * N]
                    elif what == "ctxT":
                        out, src = CT[0:L, :], ps[0:L, 0, 0:N]
                    elif what == "OT":
                        _, kind, b, j = unit
                        n = 4 if kind == "a" else CD
                        out = OT[kind][0][:, n * j:n * (j + 1), :].rearrange("p c t -> p (c t)")
                        src = ps[:, 0, 0:n * T]
                    else:
                        wait_at(act, xsc_w, g, 32, 0)
                        out = RX[what == "xk"][:, 0:2, :].rearrange("p k n -> p (k n)")
                        src, scale = ps[:, 0, 0:2 * N], 1.0 / WS
                    wait(act, filled(at, *unit))
                    act.activation(out, src, ACT.Copy, scale=scale).then_inc(hi_rdy, 1)
                elif what == "qk":
                    n = unit[1]
                    u = QUAD_ORDER[n]
                    wait(act, filled(at, *unit))
                    wait_at(act, rope_sum, g, QUADS, n - 1)
                    for h in range(2):
                        ins = act.activation(ab[:, n % 2, h, :], tile(at, *unit)[:, 0, h * N:(h + 1) * N], ACT.Identity,
                                             bias=bqk[:, 2 * u + h:2 * u + h + 1])
                    ins.then_inc(free_sem(at, *unit), 1)
                elif what == "split":
                    n = unit[1]
                    wait_at(act, rope_sum, g, QUADS, n + 1)
                    wait_at(act, sc_w[n % 2], g, 8 * QUADS, 16 * (n // 2))
                    act.activation(R[n % 2][:, 0:2, :], rsum[:, n % 2, :, :], ACT.Copy).then_inc(rope_hi, 1)
                elif what == "S":
                    _, kind, b, j = unit
                    wait(act, filled(at, *unit))
                    act.activation(PR[kind][:, j % 2 if kind == "a" else 0, :].rearrange("p (k n) -> p k n", k=2),
                                   tile(at, *unit)[0:T, :, 0:4 * T], ACT.Exp, scale=KINDS[kind][1]).then_inc(free_sem(at, *unit), 1)
                elif what == "mT" and unit[1] == "a":
                    b = unit[2]
                    wait_at(act, sm_rdy, g, G, b + 1)
                    act.activation(es[b][:], sm[b][:], ACT.Exp).then_inc(es_rdy, 1)
                elif what == "y":
                    b = unit[1]
                    if b == 0:
                        wait_at(act, yk_rdy, g, 1, 1)
                        wait_at(act, q_rdy, g, 2 * G, 0)
                    else:
                        wait_at(act, q_rdy, g, 2 * G, Q_Y[b - 1])
                    act.activation(yM, XN[3][:, b, :], ACT.Abs, scale=kMy[:, b:b + 1]).then_inc(abs_rdy, 1)
                elif what == "qT":
                    wait(act, filled(at, *unit))
                    act.activation(qT[:].rearrange("p c t -> p (c t)"), tile(at, *unit)[:].bitcast(F16)[:, 0, 0:CD * T],
                                   ACT.Copy).then_inc(free_sem(at, *unit), 1)
                elif what == "h":
                    wait(act, drained(at, "G", unit[1]))
                    act.activation(th, gs, ACT.Tanh, scale=0.5).then_inc(th_rdy, 1)
                elif what == "tq":
                    b = unit[1]
                    wait_at(act, tk_rdy, g, G, b + 1)
                    act.activation(tM, us, ACT.Abs, scale=kMt[:, b:b + 1]).then_inc(abs_rdy, 1)
                elif what == "tT":
                    s = tile(at, *unit)[:].bitcast(F16)
                    wait(act, filled(at, *unit))
                    act.activation(tT[:, 0:FC - 1, :].rearrange("p c t -> p (c t)"), s[:, 0, 0:(FC - 1) * T], ACT.Copy)
                    act.activation(tT[0:FL, FC - 1, :], s[0:FL, 0, (FC - 1) * T:FC * T], ACT.Copy).then_inc(free_sem(at, *unit), 1)

            run(act, part)

        @block.gpsimd
        def _(pool):
            pool.wait_ge(const_ld, CONST_ALL)
            for n, (m, c, rows, cols) in enumerate(wrows):
                if m == "d":
                    continue
                if n:
                    pool.wait_ge(prep_v, VBASE[n - 1] + 1)
                pool.indirect_dma_start(out=wf[0][0:rows, 0:D], out_offset=None, in_=io["w_gate" if m == "g" else "w_up"],
                                        in_offset=bass.IndirectOffsetOnAxis(ap=idx_d[0:rows, c:c + 1], axis=0)).then_inc(wrow_ld, 16)

            def part(at, g, i, unit):
                what = unit[0]
                if what == "ln":
                    n = unit[1]
                    wait_at(pool, ln_var[n], g, 1, 1)
                    pool.tensor_tensor(rstd[n][:], ve[n][:], half[:], ALU.pow).then_inc(ln_rstd[n], 1)
                elif what == "nrm" and unit[1] == 1:
                    wait_at(pool, xn_rdy[1], g, 1, 1)
                    pool.tensor_tensor(X1[i][:], X1[i][:], bo_bc[:].unsqueeze(1).broadcast_to([T, G, D]), ALU.add).then_inc(xb_rdy, 1)
                elif what == "qk":
                    n = unit[1]
                    k = n % 2
                    wait_at(pool, rope_rot, g, QUADS, n + 1)
                    wait_at(pool, rope_lo, g, QUADS, n - 1)
                    pool.tensor_tensor(rsum[:, k, 0, :], abcos[:, k, 0, :], ab[:, k, 1, :], ALU.subtract)
                    pool.tensor_tensor(rsum[:, k, 1, :], abcos[:, k, 1, :], ab[:, k, 0, :], ALU.add).then_inc(rope_sum, 1)
                elif what == "y":
                    b = unit[1]
                    wait_at(pool, qs_rdy, g, 2 * G, Q_Y[b])
                    pool.tensor_tensor(yq[:, b, :], yS, yM, ALU.subtract).then_inc(q_rdy, 1)
                elif what == "h":
                    wait_at(pool, w_rdy, g, G, unit[1] + 1)
                    pool.tensor_tensor(us, th, us, ALU.mult).then_inc(t_rdy, 1)
                elif what == "tq":
                    wait_at(pool, qs_rdy, g, 2 * G, Q_T[unit[1]])
                    pool.tensor_tensor(tq[:], tS, tM, ALU.subtract).then_inc(q_rdy, 1)

            run(pool, part)

        @block.vector
        def _(dve):
            n_fill = [0]

            def fill(ins):
                n_fill[0] += 1
                ins.then_inc(fills, 1)

            for s in range(SLOTS):
                dve.sem_inc(free[s], 1)
            fill(dve.memset(half[:], -0.5))
            fill(dve.memset(ones_b, 1.0))
            for i in range(2):
                fill(dve.memset(KB[i][HD:P, :, :], 0.0))
            fill(dve.memset(V[0][:], 0.0))
            fill(dve.memset(V[1][:], 0.0))
            fill(dve.memset(XV[:], 0.0))
            dve.wait_ge(fills, n_fill[0])
            for b in range(G):
                for i in range(2):
                    fill(dve.memset(V[i][:, b, 0:NKV * VS].rearrange("p (h w) -> p h w", w=VS)[:, :, HD:VS], 1.0))
                fill(dve.memset(XV[:, b, 0:XH * XS].rearrange("p (h w) -> p h w", w=XS)[:, :, XD:XS], 1.0))
            dve.wait_ge(const_ld, CONST_ALL)
            fill(dve.tensor_copy(id16[:], id32[:]))
            fill(dve.tensor_scalar(bqk[:], bqk[:], WS, None, ALU.mult))
            dve.wait_ge(fills, n_fill[0])

            nv = [0]

            def prep(ins):
                nv[0] += 1
                ins.then_inc(prep_v, 1)

            def prep_settled():
                dve.wait_ge(prep_v, nv[0])

            prep(dve.tensor_copy(idxf[:, 0:FC], idx_d[:]))
            prep(dve.tensor_copy(idxf[:, FC:FC + CD], idx_u[:]))
            prep_settled()
            for c in range(FC + CD):
                k = FL if c == FC - 1 else P
                w = F if c < FC else D
                if c:
                    dve.wait_ge(prep_p, c)
                prep(dve.tensor_scalar(onehot[0:k, 0:w], iota[0:k, 0:w], idxf[0:k, c:c + 1], None, ALU.is_equal))
            dve.wait_ge(prep_p, FC + CD)
            for s, w, cnt, mask in ((slot[0], F, cnt4, maskd), (slot[1], D, cnt4u, mask_u[:])):
                v = s[:, :, 0:w // 2]
                prep(dve.tensor_scalar(cnt.rearrange("p (k n) -> p k n", k=2), v, 0.25, None, ALU.mult))
                prep(dve.tensor_scalar(mask.rearrange("p (k n) -> p k n", k=2), v, 1.0, None, ALU.min))
            prep_settled()
            assert nv[0] == PREP_V0

            for n, (_src, hi, lo, cols) in enumerate(splits):
                dve.wait_ge(hi_done, n + 1)
                dve.scalar_tensor_tensor(out=lo, in0=stage[n % 2][:, 0:cols], scalar=WS, in1=hi, op0=ALU.mult,
                                         op1=ALU.subtract).then_inc(lo_done, 1)
            dve.wait_ge(lo_done, NS)
            dve.memset(wkv[1][L:P, :], 0.0).then_inc(lo_done, 1)

            for n, (m, c, rows, cols) in enumerate(wrows):
                r = slice(0, rows)
                w0, w1, w2, w3 = (wf[i][r, 0:cols] for i in range(4))
                mask, cnt = (maskd, cnt4) if m == "d" else (mask_u[:], cnt4u)
                assert nv[0] == VBASE[n]
                if m == "d":
                    dve.wait_ge(wdown_ld, 16 * (c + 1))
                else:
                    dve.wait_ge(wrow_ld, 16 * (n + 1))
                prep(dve.tensor_tensor(w1, w0, mask[r, :], ALU.mult))
                prep_settled()
                prep(dve.tensor_reduce(wr[r, 0:1], w1, AX.X, ALU.max, apply_absolute_value=True))
                prep_settled()
                prep(dve.reciprocal(wr[r, 1:2], wr[r, 0:1]))
                prep_settled()
                prep(dve.tensor_scalar(wr[r, 2:3], wr[r, 1:2], FP8_MAX, None, ALU.mult))
                prep(dve.tensor_scalar(wr[r, 3:4], wr[r, 1:2], FP8_MAX * 2.0 ** 20, None, ALU.mult))
                prep_settled()
                dve.wait_ge(prep_abs, n + 1)
                prep(dve.tensor_scalar(w2, w2, SUB, None, ALU.max))
                prep_settled()
                prep(dve.scalar_tensor_tensor(out=w3, in0=w1, scalar=wr[r, 2:3], in1=w2, op0=ALU.mult, op1=ALU.add))
                prep_settled()
                prep(dve.tensor_tensor(w3, w3, w2, ALU.subtract))
                prep_settled()
                prep(dve.tensor_tensor(wq[r, 0:cols], w3, cnt[r, :], ALU.mult))
                dve.wait_ge(prep_p, FC + CD + n + 1)
                s = slot[2][:].bitcast(F16)
                if m == "d":
                    prep(dve.tensor_copy(wdT[:, 0:FC - 1, c * P:(c + 1) * P],
                                         s[:, 0, 0:(FC - 1) * P].rearrange("p (k n) -> p k n", n=P)))
                    prep(dve.tensor_copy(wdT[0:FL, FC - 1, c * P:(c + 1) * P], s[0:FL, 0, (FC - 1) * P:FC * P]))
                else:
                    wT = wgT if m == "g" else wuT
                    prep(dve.tensor_copy(wT[:, :, c * P:c * P + rows],
                                         s[:, 0, 0:CD * P].rearrange("p (k n) -> p k n", n=P)[:, :, 0:rows]))
                out = {"g": sg_bc, "u": su_bc, "d": sd_bc}[m][:, c * P:c * P + rows]
                if m == "u":
                    prep(dve.scalar_tensor_tensor(out=out, in0=slot[WIDE][:, 0, 0:rows], scalar=4.0 / FP8_MAX,
                                                  in1=maskd[:, c * P:c * P + rows], op0=ALU.mult, op1=ALU.mult))
                else:
                    prep(dve.tensor_scalar(out, slot[WIDE][:, 0, 0:rows], (4.0 if m == "g" else 2.0) / FP8_MAX, None, ALU.mult))
                prep_settled()
            assert nv[0] == PREP_VALL

            fill(dve.memset(XQs[:].bitcast(F32), 0.0))
            fill(dve.memset(XKs[:].bitcast(F32), 0.0))
            assert n_fill[0] == N_FILLS, n_fill[0]

            steps = [0]

            def step(ins):
                steps[0] += 1
                ins.then_inc(v_self, 1)

            def settled(g):
                dve.wait_ge(v_self, steps[0] if g[0] is None else g[0] * (2 * V_STEPS) + steps[0])

            def lo_of(at, unit, out, src, hi, scale=None):
                k = hi_at[at[0], unit] + 1
                dve.wait_ge(hi_rdy, k if at[1] is None else at[1] * hi_per_loop + k)
                if scale is None:
                    dve.tensor_tensor(out, src, hi, ALU.subtract).then_inc(free_sem(at, *unit), 1)
                else:
                    dve.scalar_tensor_tensor(out=out, in0=src, scalar=scale, in1=hi, op0=ALU.mult,
                                             op1=ALU.subtract).then_inc(free_sem(at, *unit), 1)

            def round_rows(g, n_job, x, k, m, s):
                wait_at(dve, abs_rdy, g, 2 * G, n_job)
                step(dve.tensor_scalar(m, m, SUB, None, ALU.max))
                settled(g)
                dve.scalar_tensor_tensor(out=s, in0=x, scalar=k, in1=m, op0=ALU.mult, op1=ALU.add).then_inc(qs_rdy, 1)

            def part(at, g, i, unit):
                what = unit[0]
                ps = tile(at, *unit) if what in NARROW_TILES + WIDE_TILES else None
                if what == "ln":
                    n = unit[1]
                    x = (X1, X2, X3)[n - 1][i]
                    if n == 1:
                        wait_at(dve, x_ld, g, 16, 16)
                    for b in range(G):
                        step(dve.bn_stats(stats[n][:, b, :], x[:, b, :]))
                    settled(g)
                    stand(dve)
                    for b in range(G):
                        step(dve.bn_aggr(mv[n][:, b, :], stats[n][:, b, :]))
                    settled(g)
                    dve.tensor_scalar(ve[n][:], mv[n][:, :, 1], EPS, None, ALU.add).then_inc(ln_var[n], 1)
                elif what == "nrm":
                    n = unit[1]
                    x = (X1, X2, X3)[n - 1][i]
                    wait_at(dve, ln_rstd[n], g, 1, 1)
                    if n < 3:
                        for b in range(G):
                            ins = dve.tensor_scalar(XN[n][:, b, :], x[:, b, :], mv[n][:, b, 0:1], rstd[n][:, b:b + 1],
                                                    ALU.subtract, ALU.mult)
                        ins.then_inc(xn_rdy[n], 1)
                    else:
                        for b in range(G):
                            step(dve.scalar_tensor_tensor(out=XN[3][:, b, :], in0=x[:, b, :], scalar=mv[3][:, b, 0:1],
                                                               in1=mask_u[0:T, :], op0=ALU.subtract, op1=ALU.mult))
                        settled(g)
                        step(dve.tensor_reduce(ry[:], XN[3][:], AX.X, ALU.max, apply_absolute_value=True))
                        settled(g)
                        step(dve.reciprocal(rry[:], ry[:]))
                        settled(g)
                        step(dve.tensor_scalar(ky[:], rry[:], FP8_MAX, None, ALU.mult))
                        step(dve.scalar_tensor_tensor(out=sx[:], in0=ry[:], scalar=1.0 / FP8_MAX, in1=rstd[3][:],
                                                           op0=ALU.mult, op1=ALU.mult))
                        dve.tensor_scalar(kMy[:], rry[:], FP8_MAX * 2.0 ** 20, None, ALU.mult).then_inc(yk_rdy, 1)
                elif what == "xT":
                    n = unit[1]
                    hi, lo = (xT[n][k][:].rearrange("p c n -> p (c n)") for k in range(2))
                    lo_of(at, unit, lo, ps[:, 0, 0:CD * N], hi)
                elif what == "ctxT":
                    lo_of(at, unit, CT[L:P, :], ps[0:L, 0, 0:N], CT[0:L, :])
                elif what in ("xq", "xk"):
                    r = RX[what == "xk"]
                    lo_of(at, unit, r[:, 2:4, :].rearrange("p k n -> p (k n)"), ps[:, 0, 0:2 * N],
                          r[:, 0:2, :].rearrange("p k n -> p (k n)"), 1.0 / WS)
                elif what == "OT":
                    _, kind, b, j = unit
                    n = 4 if kind == "a" else CD
                    hi, lo = (OT[kind][k][:, n * j:n * (j + 1), :].rearrange("p c t -> p (c t)") for k in range(2))
                    lo_of(at, unit, lo, ps[:, 0, 0:n * T], hi)
                elif what == "qk":
                    n = unit[1]
                    k = n % 2
                    wait(dve, drained(at, *unit))
                    dve.tensor_tensor(abcos[:, k], ab[:, k], cosT[:].unsqueeze(1).broadcast_to([P, 2, N]), ALU.mult)
                    dve.tensor_tensor(ab[:, k], ab[:, k], sinT[:].unsqueeze(1).broadcast_to([P, 2, N]), ALU.mult).then_inc(rope_rot, 1)
                elif what == "split":
                    n = unit[1]
                    wait_at(dve, rope_hi, g, QUADS, n + 1)
                    dve.tensor_tensor(R[n % 2][:, 2:4, :], rsum[:, n % 2, :, :], R[n % 2][:, 0:2, :],
                                      ALU.subtract).then_inc(rope_lo, 1)
                elif what == "v":
                    wait(dve, filled(at, *unit))
                    dve.scalar_tensor_tensor(out=V[i][:, unit[1], 0:NKV * VS].rearrange("p (h w) -> p h w", w=VS)[:, :, 0:HD],
                                             in0=ps[0:T, 0, :].rearrange("p (h d) -> p h d", d=HD), scalar=1.0 / WS,
                                             in1=bv_bc[:].rearrange("p (h d) -> p h d", d=HD),
                                             op0=ALU.mult, op1=ALU.add).then_inc(free_sem(at, *unit), 1)
                elif what == "xv":
                    wait(dve, filled(at, *unit))
                    dve.tensor_scalar(XV[:, unit[1], 0:XH * XS].rearrange("p (h w) -> p h w", w=XS)[:, :, 0:XD],
                                      ps[0:T, 0, 0:D].rearrange("p (h d) -> p h d", d=XD),
                                      1.0 / WS, None, ALU.mult).then_inc(free_sem(at, *unit), 1)
                elif what == "M":
                    _, kind, b, j = unit
                    wait(dve, filled(at, *unit))
                    dve.tensor_reduce(mx[kind][b][:, 8 * j:8 * j + 8], ps[0:T, :, 0:4 * T].rearrange("p k (h n) -> p k h n", n=T),
                                      AX.X, ALU.max).then_inc(free_sem(at, *unit), 1)
                elif what == "mT":
                    _, kind, b, _ = unit
                    nh, scale = KINDS[kind]
                    m, rest = MR[kind][b], mr_rest[kind][0:nh, :]
                    wait(dve, filled(at, *unit))
                    step(dve.tensor_scalar(m[0:nh, 0, :], ps[0:nh, 0, 0:T], -1.0, None, ALU.mult))
                    settled(g)
                    dve.scalar_tensor_tensor(out=rest, in0=ps[0:nh, 0, 0:T], scalar=-1.0, in1=m[0:nh, 0, :],
                                             op0=ALU.mult, op1=ALU.subtract).then_inc(free_sem(at, *unit), 1)
                    wait(dve, drained(at, *unit))
                    step(dve.tensor_copy(m[0:nh, 1, :], rest))
                    settled(g)
                    dve.tensor_tensor(m[0:nh, 2, :], rest, m[0:nh, 1, :], ALU.subtract).then_inc(mr_rdy[kind], 1)
                    if kind == "a":
                        dve.scalar_tensor_tensor(out=sm[b][:], in0=mx["a"][b][:], scalar=-scale, in1=sink_bc[:],
                                                 op0=ALU.mult, op1=ALU.add).then_inc(sm_rdy, 1)
                elif what == "V":
                    _, kind, b, j = unit
                    hd = HD if kind == "a" else XD
                    wait(dve, filled(at, *unit))
                    v = ps[0:T, :, 0:4 * W].rearrange("p k (h w) -> p k h w", w=W)
                    r = rden[kind][:, j % 2].rearrange("p (k h) -> p k h", k=2)
                    if kind == "a":
                        wait_at(dve, es_rdy, g, G, b + 1)
                        step(dve.tensor_tensor(den[:, j % 2].rearrange("p (k h) -> p k h", k=2), v[:, :, :, hd],
                                                   es[b][:, 8 * j:8 * j + 8].rearrange("p (k h) -> p k h", k=2), ALU.add))
                        settled(g)
                        step(dve.reciprocal(rden[kind][:, j % 2], den[:, j % 2]))
                    else:
                        step(dve.reciprocal(r, v[:, :, :, hd]))
                    settled(g)
                    o = ON["a"][:, j % 2, :] if kind == "a" else ON["c"][:, 0, 8 * j * hd:8 * (j + 1) * hd]
                    dve.tensor_tensor(o.rearrange("p (k h d) -> p k h d", k=2, h=4),
                                      v[:, :, :, 0:hd], r.unsqueeze(3).broadcast_to([T, 2, 4, hd]),
                                      ALU.mult).then_inc(free_sem(at, *unit), 1)
                elif what == "Y":
                    _, kind, b, _ = unit
                    x, out = (X1, X2) if kind == "a" else (X2, X3)
                    wait(dve, filled(at, *unit))
                    if kind == "a" and b == 0:
                        wait_at(dve, xb_rdy, g, 1, 1)
                    dve.scalar_tensor_tensor(out=out[i][:, b, :], in0=ps[0:T, 0, 0:D], scalar=1.0 / WS, in1=x[i][:, b, :],
                                             op0=ALU.mult, op1=ALU.add).then_inc(free_sem(at, *unit), 1)
                    if b == G - 1:
                        wait(dve, drained(at, *unit))
                        stand(dve)
                elif what == "y":
                    b = unit[1]
                    round_rows(g, Q_Y[b], XN[3][:, b, :], ky[:, b:b + 1], yM, yS)
                elif what == "G":
                    b = unit[1]
                    wait(dve, filled(at, *unit))
                    dve.scalar_tensor_tensor(out=gs.rearrange("p (k n) -> p k n", k=2), in0=ps[0:T, :, 0:FH],
                                             scalar=sx[:, b:b + 1], in1=sg_bc[0:T, :].rearrange("p (k n) -> p k n", k=2),
                                             op0=ALU.mult, op1=ALU.mult).then_inc(free_sem(at, *unit), 1)
                elif what == "U":
                    wait(dve, filled(at, *unit))
                    dve.tensor_tensor(us.rearrange("p (k n) -> p k n", k=2), ps[0:T, :, 0:FH],
                                      su_bc[0:T, :].rearrange("p (k n) -> p k n", k=2), ALU.mult).then_inc(free_sem(at, *unit), 1)
                elif what == "h":
                    wait(dve, drained(at, "U", unit[1]))
                    wait_at(dve, th_rdy, g, G, unit[1] + 1)
                    dve.scalar_tensor_tensor(out=th, in0=th, scalar=1.0, in1=gs, op0=ALU.add,
                                             op1=ALU.mult).then_inc(w_rdy, 1)
                elif what == "hk":
                    b = unit[1]
                    c = slice(b, b + 1)
                    wait_at(dve, t_rdy, g, G, b + 1)
                    step(dve.tensor_reduce(rt[:, c], us, AX.X, ALU.max, apply_absolute_value=True))
                    settled(g)
                    step(dve.reciprocal(rrt[:, c], rt[:, c]))
                    settled(g)
                    step(dve.tensor_scalar(kt[:, c], rrt[:, c], FP8_MAX, None, ALU.mult))
                    step(dve.scalar_tensor_tensor(out=st_[:, c], in0=rt[:, c], scalar=1.0 / FP8_MAX,
                                                       in1=sx[:, c], op0=ALU.mult, op1=ALU.mult))
                    dve.tensor_scalar(kMt[:, c], rrt[:, c], FP8_MAX * 2.0 ** 20, None, ALU.mult).then_inc(tk_rdy, 1)
                elif what == "tq":
                    b = unit[1]
                    round_rows(g, Q_T[b], us, kt[:, b:b + 1], tM, tS)
                elif what == "D":
                    b = unit[1]
                    wait(dve, filled(at, *unit))
                    if b == 0:
                        wait_at(dve, out_st, g, 16 * G, 0)
                    dve.scalar_tensor_tensor(out=OUT[:, b, :], in0=ps[0:T, 0, 0:D], scalar=st_[:, b:b + 1],
                                             in1=sd_bc[0:T, :], op0=ALU.mult, op1=ALU.mult).then_inc(free_sem(at, *unit), 1)
                    wait(dve, drained(at, *unit))
                    dve.tensor_tensor(OUT[:, b, :], OUT[:, b, :], X3[i][:, b, :], ALU.add).then_inc(out_rdy, 1)

            def body_done(n_body):
                if n_body == "loop1":
                    steps[0] += (loops - 1) * 2 * V_STEPS

            run(dve, part, body_done)


def rope_tables():
    theta, scaling, ntk_alpha, ntk_beta, icl = 150000.0, 32.0, 1.0, 32.0, 128
    d_half = HD // 2
    freq = theta ** (np.arange(0, HD, 2, dtype=np.float32) / HD)
    concentration = 0.1 * math.log(scaling) + 1.0
    low = d_half * math.log(icl / (ntk_beta * 2 * math.pi)) / math.log(theta)
    high = d_half * math.log(icl / (ntk_alpha * 2 * math.pi)) / math.log(theta)
    interpolation = 1.0 / (scaling * freq)
    extrapolation = 1.0 / freq
    ramp = np.clip((np.arange(d_half, dtype=np.float32) - low) / (high - low), 0.0, 1.0)
    mask = 1.0 - ramp
    inv_freq = interpolation * (1.0 - mask) + extrapolation * mask
    freqs = np.outer(np.arange(T, dtype=np.float32), inv_freq)
    return (np.cos(freqs) * concentration).astype(np.float32).T, (np.sin(freqs) * concentration).astype(np.float32).T


def kernel(**inputs):
    import ml_dtypes
    import concourse.bacc as bacc
    from concourse.bass_utils import run_bass_kernel_spmd

    x = {k: np.asarray(v) for k, v in inputs.items()}

    def chunked(w):
        return w.T.reshape(-1, P, w.shape[0]).transpose(1, 0, 2)

    def rope_rows(w):
        return w.reshape(QUADS, 4, 2, HD // 2, -1).transpose(0, 2, 1, 3, 4).reshape(QUADS * 256, -1)

    def index_columns(idx, n):
        out = np.zeros(n * P, idx.dtype)
        out[:idx.size] = idx
        return out.reshape(n, P).T

    qk = (NH + NKV) * HD
    w, bias = x["L0_attn_qkv_w"], x["L0_attn_qkv_b"]
    cos, sin = rope_tables()
    causal = np.arange(T)[:, None] < np.arange(T)[None, :]
    mask = np.where(causal, np.float32(NEG), np.float32(0)).astype(ml_dtypes.bfloat16)
    arrays = {
        "x": x["x"].reshape(NG, G, T, D),
        "ctx": x["ctx_512"][:, :T].reshape(NG, G, T, L),
        "wqkT": chunked(rope_rows(w[:qk])),
        "wvT": chunked(w[qk:]),
        "woT": chunked(x["L0_attn_out_w"]).reshape(P, 16 * D),
        "wxqT": chunked(x["L0_xattn_Wq"]).reshape(P, CD * D),
        "wxoT": chunked(x["L0_xattn_Wout"]).reshape(P, CD * D),
        "wkvT": np.tile(x["L0_xattn_Wkv_expand"].T, (2, 1)),
        "w_gate": x["L0_ffn_w_gate"], "w_up": x["L0_ffn_w_up"], "w_down": x["L0_ffn_w_down"],
        "bqk": rope_rows(bias[:qk]).reshape(2 * QUADS, P).T,
        "bv": np.broadcast_to(bias[qk:], (T, 512)),
        "bo": np.broadcast_to(x["L0_attn_out_b"], (T, D)),
        "sinks": np.broadcast_to(x["L0_attn_sinks"], (T, NH)),
        "idx_d": index_columns(x["L0_ffn_down_reorder_index"], FC),
        "idx_u": index_columns(x["L0_ffn_up_reorder_index"], CD),
        "cosT": np.tile(cos / np.float32(WS), (4, G)), "sinT": np.tile(sin / np.float32(WS), (4, G)),
        "id32": np.eye(P, dtype=np.float32),
        "iota": np.tile(np.arange(F, dtype=np.float32), (P, 1)),
        "maskM": np.tile(mask, (1, 4)), "maskT": np.tile(mask.T, (1, NH)),
        "idb": np.concatenate([np.eye(T), np.ones((3, T))]).astype(ml_dtypes.bfloat16),
    }
    arrays = {k: np.ascontiguousarray(v) for k, v in arrays.items()}
    nc = bacc.Bacc("TRN2", target_bir_lowering=False, num_devices=1)
    io = {k: nc.dram_tensor(f"in_{k}", v.shape, mybir.dt.from_np(v.dtype), kind="ExternalInput").ap()
          for k, v in arrays.items()}
    io["scratch"] = nc.dram_tensor("rotated_qk", (NG, QUADS, P, 4, N), F16, kind="Internal").ap()
    io["xscratch"] = nc.dram_tensor("cross_qk", (NG, 2, 2, CD, P, N), F16, kind="Internal").ap()
    io["out"] = nc.dram_tensor("out", (NG, G, T, D), F32, kind="ExternalOutput").ap()
    build(nc, io)
    r = run_bass_kernel_spmd(nc, [{f"in_{k}": v for k, v in arrays.items()}], core_ids=[0])
    return r.results[0]["out"].reshape(B, T, D)
```

```python
from contextlib import ExitStack
import math

import numpy as np
import concourse.bass as bass
from concourse import mybir

F32, F16, BF16, I32 = mybir.dt.float32, mybir.dt.float16, mybir.dt.bfloat16, mybir.dt.int32
ALU, ACT, AX = mybir.AluOpType, mybir.ActivationFunctionType, mybir.AxisListType

P = 128
B, T, D = 32, 100, 256
G = 2
NG = B // G
N = G * T
CD = D // P
NH, NKV, HD = 32, 8, 64
QUADS = (NH + NKV) // 4
XH, XD, L = 16, 16, 64
F = 704
FC = -(-F // P)
FL = F - (FC - 1) * P
FH = F // 2
W = 96
XS = XD + 1
XVW = (XH - 1) * XS + W
VS = HD + 1
WS = 64.0
EPS = 1e-5
FP8_MAX = 448.0
SUB = 1.5 * 2.0 ** 14
NEG = -1e30
WIDE, NARROW = 3, 2
SLOTS = WIDE + NARROW

KINDS = {"a": (NH, 1.0 / math.sqrt(HD)), "c": (XH, 1.0 / math.sqrt(XD))}
DVE_SPLITS = ("body0", "body1")
QUAD_ORDER = [8, 9] + list(range(8))

ORDER = (
    (2, ('V', 'a', 0, 2)), (2, ('OT', 'a', 0, 1)), (2, ('S', 'a', 1, 0)), (5, ('D', 0)), (5, ('hk', 1)),
    (1, ('split', 4)), (2, ('cload',)), (1, ('split', 5)), (2, ('V', 'a', 0, 3)), (1, ('qk', 6)), (1, ('qk', 7)),
    (5, ('tq', 1)), (2, ('S', 'a', 1, 1)), (2, ('OT', 'a', 0, 2)), (2, ('OT', 'a', 0, 3)), (3, ('M', 'c', 0, 0)),
    (3, ('M', 'c', 0, 1)), (2, ('V', 'a', 1, 0)), (1, ('split', 6)), (1, ('split', 7)), (1, ('qk', 8)),
    (1, ('qk', 9)), (2, ('S', 'a', 1, 2)), (1, ('split', 8)), (1, ('split', 9)), (3, ('mT', 'c', 0, 0)),
    (4, ('nrm', 3)), (2, ('Y', 'a', 0, 0)), (4, ('y', 0)), (3, ('M', 'c', 1, 0)), (2, ('ctxT',)),
    (3, ('M', 'c', 1, 1)), (5, ('tT', 1)), (1, ('qload', 0)), (2, ('V', 'a', 1, 1)), (4, ('y', 1)), (4, ('qT', 0)),
    (2, ('OT', 'a', 1, 0)), (2, ('S', 'a', 1, 3)), (2, ('V', 'a', 1, 2)), (2, ('OT', 'a', 1, 1)),
    (3, ('S', 'c', 0, 0)), (4, ('G', 0)), (4, ('U', 0)), (2, ('V', 'a', 1, 3)), (4, ('h', 0)), (3, ('V', 'c', 0, 0)),
    (2, ('OT', 'a', 1, 2)), (2, ('OT', 'a', 1, 3)), (3, ('S', 'c', 0, 1)), (1, ('qload', 1)), (1, ('M', 'a', 0, 0)),
    (3, ('mT', 'c', 1, 0)), (4, ('hk', 0)), (1, ('M', 'a', 0, 1)), (1, ('M', 'a', 0, 2)), (4, ('tq', 0)),
    (2, ('Y', 'a', 1, 0)), (0, ('load',)), (4, ('qT', 1)), (2, ('ln', 2)), (3, ('V', 'c', 0, 1)), (1, ('v', 0)),
    (5, ('D', 1)), (2, ('nrm', 2)), (0, ('ln', 1)), (3, ('S', 'c', 1, 0)), (1, ('v', 1)), (0, ('nrm', 1)),
    (2, ('xT', 2)), (1, ('M', 'a', 0, 3)), (3, ('OT', 'c', 0, 0)), (3, ('V', 'c', 1, 0)), (0, ('xT', 1)),
    (3, ('S', 'c', 1, 1)), (1, ('mT', 'a', 0, 0)), (1, ('M', 'a', 1, 0)), (1, ('M', 'a', 1, 1)), (0, ('qk', 0)),
    (0, ('qk', 1)), (2, ('xk',)), (1, ('M', 'a', 1, 2)), (2, ('xq',)), (3, ('V', 'c', 1, 1)), (0, ('split', 0)),
    (0, ('qk', 2)), (0, ('split', 1)), (1, ('M', 'a', 1, 3)), (0, ('qk', 3)), (4, ('tT', 0)), (4, ('G', 1)),
    (1, ('S', 'a', 0, 0)), (3, ('Y', 'c', 0, 0)), (3, ('OT', 'c', 1, 0)), (4, ('U', 1)), (1, ('S', 'a', 0, 1)),
    (0, ('split', 2)), (1, ('mT', 'a', 1, 0)), (2, ('xv', 1)), (1, ('V', 'a', 0, 0)), (0, ('split', 3)),
    (2, ('xv', 0)), (2, ('xload',)), (1, ('V', 'a', 0, 1)), (4, ('h', 1)), (0, ('qk', 4)), (1, ('S', 'a', 0, 2)),
    (3, ('Y', 'c', 1, 0)), (3, ('ln', 3)), (1, ('S', 'a', 0, 3)), (1, ('OT', 'a', 0, 0)), (0, ('qk', 5)),
)
PREP_PLACES = (
    0, 2, 3, 4, 10, 14, 18, 22, 24, 24, 24, 24, 25, 25, 25, 27, 31, 47, 50, 65, 76, 78, 79, 81, 81, 87, 88, 90, 92,
    96, 96, 100, 104, 106, 123, 136, 139, 156, 162, 167, 173, 179,
)
NARROW_TILES = ("xT", "qk", "v", "mT", "OT", "Y", "ctxT", "xq", "xk", "xv", "qT", "tT", "D")
WIDE_TILES = ("M", "S", "V", "G", "U")
HI_TILES = ("xT", "OT", "ctxT", "xq", "xk")
LAGS = max(lag for lag, _ in ORDER)


PREP_UNITS = [(w, n) for n in range(2 * FC + CD) for w in ("scale rows", "round rows", "turn rows")]


def body_units(n):
    live = [[(-lag, unit) for lag, unit in ORDER if 0 <= m - lag < NG] for m in range(n + 1)]
    if n >= LAGS + 1:
        return live[n]
    start = sum(len(b) for b in live[:n])
    out = []
    for i, unit in enumerate(live[n]):
        out += [(0, u) for u, place in zip(PREP_UNITS, PREP_PLACES) if place == start + i]
        out.append(unit)
    return out


def bodies():
    first = LAGS + 1
    loops = (NG - first) // 2
    out = [(f"body{n}", n) for n in range(first)] + [("loop0", first), ("loop1", first + 1)]
    out += [(f"body{n}", n) for n in range(first + 2 * loops, NG + LAGS)]
    return out, loops


Q_Y = [1, 2]
Q_T = [3, 4]

PREP_V0 = 2 + FC + CD + 4
PREP_N = [11] * (2 * FC) + [12] * CD
VBASE = [PREP_V0 + sum(PREP_N[:n]) for n in range(len(PREP_N))]

V_STEPS = 3 * 2 * G + 2 * G + 2 * G + 2 * G * NH // 8 + G * XH // 8 + (G + 4) + 2 * G + 4 * G


def build(nc, io):
    order, loops = bodies()
    units = {name: body_units(n) for name, n in order}
    slot_of, before, hi_at = {}, {}, {}
    turn = {"wide": 0, "narrow": 0}
    for _, unit in ORDER:
        if unit[0] in WIDE_TILES:
            slot_of[unit] = turn["wide"] % WIDE
            turn["wide"] += 1
        elif unit[0] in NARROW_TILES:
            slot_of[unit] = WIDE + turn["narrow"] % NARROW
            turn["narrow"] += 1
    for n in range(2 * FC + CD):
        slot_of["turn rows", n] = WIDE + n % NARROW
    per_loop = [2 * sum(s == slot_of.get(unit) for _, unit in ORDER) for s in range(SLOTS)]
    hi_per_loop = 2 * sum(unit[0] in HI_TILES for _, unit in ORDER)
    used, hi_used = [0] * SLOTS, 0
    for name, _ in order:
        for _, unit in units[name]:
            if unit in slot_of:
                before[name, unit] = used[slot_of[unit]]
                used[slot_of[unit]] += 1
            if unit[0] in HI_TILES:
                hi_at[name, unit] = hi_used
                hi_used += 1
        if name == "loop1":
            used = [u + (loops - 1) * p for u, p in zip(used, per_loop)]
            hi_used += (loops - 1) * hi_per_loop

    with ExitStack() as ctx:
        def sb(name, shape, dt):
            return ctx.enter_context(nc.sbuf_tensor(name, shape, dt))

        def sem(name):
            return ctx.enter_context(nc.semaphore(name))

        slot = [ctx.enter_context(nc.psum_tensor(f"slot{s}", [P, 2 if s < WIDE else 1, 512], F32)) for s in range(SLOTS)]

        wqk = [sb(f"wqk_{k}", [P, CD, QUADS * 256], F16) for k in ("hi", "lo")]
        wv = [sb(f"wv_{k}", [P, CD, 512], F16) for k in ("hi", "lo")]
        wo = [sb(f"wo_{k}", [P, 16, D], F16) for k in ("hi", "lo")]
        wxq = [sb(f"wxq_{k}", [P, CD, D], F16) for k in ("hi", "lo")]
        wxo = [sb(f"wxo_{k}", [P, CD, D], F16) for k in ("hi", "lo")]
        wkv = [sb(f"wkv_{k}", [P, 512], F16) for k in ("hi", "lo")]
        wgT = sb("wgT", [P, CD, F], F16)
        wuT = sb("wuT", [P, CD, F], F16)
        wdT = sb("wdT", [P, FC, D], F16)
        sg_bc = sb("sg_bc", [P, F], F32)
        su_bc = sb("su_bc", [P, F], F32)
        sd_bc = sb("sd_bc", [P, D], F32)
        mask_u = sb("mask_u", [P, D], F32)
        cosT = sb("cosT", [P, N], F32)
        sinT = sb("sinT", [P, N], F32)
        bqk = sb("bqk", [P, 2 * QUADS], F32)
        bv_bc = sb("bv_bc", [T, 512], F32)
        bo_bc = sb("bo_bc", [T, D], F32)
        sink_bc = sb("sink_bc", [T, NH], F32)
        id32 = sb("id32", [P, P], F32)
        id16 = sb("id16", [P, P], F16)
        idb = sb("idb", [T + 3, T], BF16)
        maskM = sb("maskM", [T, 4 * T], BF16)
        half = sb("half", [T, G], F32)
        MB = {"a": [sb(f"maskT_m{i}", [T + 3, NH * T], BF16) for i in range(2)]}
        MB["c"] = [sb("maskT_mc", [T + 3, XH * T], BF16)] * 2

        X1 = [sb(f"X1_{i}", [T, G, D], F32) for i in range(2)]
        X2 = [sb(f"X2_{i}", [T, G, D], F32) for i in range(2)]
        XN = {n: sb(f"XN{n}", [T, G, D], F32) for n in (1, 2)}
        FS = sb("ffn_rows", [P, 3 * G * D + G * D // 2 + F // 2 + 2 * G * D], F32)
        at_col = [0]

        def part_of(cols):
            at_col[0] += cols
            return FS[0:T, at_col[0] - cols:at_col[0]]

        XN[3], OUT = (part_of(G * D).rearrange("p (b d) -> p b d", b=G) for i in range(2))
        YMS = part_of(2 * D)
        yq = part_of(G * D // 2).bitcast(F16).rearrange("p (b d) -> p b d", b=G)
        tq = part_of(F // 2).bitcast(F16)
        X3 = [part_of(G * D).rearrange("p (b d) -> p b d", b=G) for i in range(2)]
        xT = {n: [sb(f"xT{n}_{k}", [P, CD, N], F16) for k in ("hi", "lo")] for n in (1, 2)}
        ROT = sb("rope", [P, 2 * 2 * 2 * N], F32)
        SUM = sb("rope_sums", [P, 2 * 2 * N], F32)
        R = [sb(f"split{i}", [P, 4, N], F16) for i in range(2)]
        RX = [sb(f"xsplit{i}", [P, 4, N], F16) for i in range(2)]
        QA = [sb(f"QA{b}", [P, NH * T], F16) for b in range(G)]
        KA = [sb(f"KA{b}", [P, NKV, T], F16) for b in range(G)]
        KB = [sb(f"KB{b}", [P, NKV, T], F16) for b in range(G)]
        V = [sb(f"V{i}", [T, G, NKV * VS + W - VS], F32) for i in range(2)]
        PR = {"a": sb("probs", [T, 2, 8 * T], F32), "c": sb("xprobs", [T, 1, 8 * T], F32)}
        ON = {"a": sb("attn_out", [T, 2, 8 * HD], F32), "c": sb("xattn_out", [T, 1, D], F32)}
        OT = {"a": [sb(f"attn_outT_{k}", [P, 16, T], F16) for k in ("hi", "lo")],
              "c": [sb(f"xattn_outT_{k}", [P, CD, T], F16) for k in ("hi", "lo")]}
        XQs, XKs = sb("XQ", [P, XH * N], F16), sb("XK", [P, XH * N], F16)
        C0 = sb("ctx_rows", [T, G, L], F32)
        CT = sb("ctxT", [P, N], F16)
        XV = sb("XV", [T, G, XVW], F32)
        QTS = sb("qT_tT", [P, (CD + FC) * T], F16)
        qT = QTS[:, 0:CD * T].rearrange("p (c t) -> p c t", c=CD)
        tT = QTS[:, CD * T:].rearrange("p (c t) -> p c t", c=FC)
        stats = {n: sb(f"stats{n}", [T, G, 6], F32) for n in (1, 2, 3)}
        mv = {n: sb(f"mv{n}", [T, G, 2], F32) for n in (1, 2, 3)}
        ve = {n: sb(f"var_eps{n}", [T, G], F32) for n in (1, 2, 3)}
        rstd = {n: sb(f"rstd{n}", [T, G], F32) for n in (1, 2, 3)}
        mx = {k: [sb(f"row_max_{k}{i}", [T, NH], F32) for i in range(2)] for k in "ac"}
        sm = [sb(f"sink_shift{i}", [T, NH], F32) for i in range(2)]
        es = [sb(f"sink_exp{i}", [T, NH], F32) for i in range(2)]
        MR = {k: [sb(f"neg_max_{k}{i}", [NH, 3, T], BF16) for i in range(2)] for k in "ac"}
        mr_rest = {k: sb(f"mr_rest_{k}", [NH, T], F32) for k in "ac"}
        den = sb("den", [T, 2, 8], F32)
        rden = {k: sb(f"rden_{k}", [T, 2, 8], F32) for k in "ac"}
        ry, rry, ky, kMy, sx = (sb(n, [T, G], F32) for n in ("ry", "rry", "ky", "kMy", "sx"))
        rt, rrt, kt, kMt, st_ = (sb(n, [T, G], F32) for n in ("rt", "rrt", "kt", "kMt", "st"))
        FB = sb("ffn", [P, 3 * F], F32)
        gs, us, th = (FB[0:T, i * F:(i + 1) * F] for i in range(3))
        tM, tS = th, gs
        yM, yS = YMS[:, 0:D], YMS[:, D:2 * D]

        ab = ROT[:, 0:4 * N].rearrange("p (i k n) -> p i k n", i=2, k=2)
        abcos = ROT[:, 4 * N:8 * N].rearrange("p (i k n) -> p i k n", i=2, k=2)
        rsum = SUM[:].rearrange("p (i k n) -> p i k n", i=2, k=2)
        qa = [QA[b][:].rearrange("p (h t) -> p h t", h=NH) for b in range(G)]
        XQ = XQs[:].rearrange("p (h n) -> p h n", h=XH)
        XK = XKs[:].rearrange("p (h n) -> p h n", h=XH)
        stage = [x[:].bitcast(F32)[:, 0:1024] for x in (*QA, XQs, XKs)]
        wf = [FS[:, i * F:(i + 1) * F] for i in range(4)]
        wq = QTS
        cnt4 = FB[:, 0:F]
        maskd = FB[:, F:2 * F]
        cnt4u = FB[:, 2 * F:2 * F + D]
        onehot = ROT[:].bitcast(BF16)[:, 0:F]
        iota = ROT[:, F:2 * F]
        ones_b = SUM[:].bitcast(BF16)[:, 0:P]
        idx_d = sb("idx_d", [P, FC], I32)
        idx_u = sb("idx_u", [P, CD], I32)
        idxf = sb("idxf", [P, FC + CD], F32)
        wr = sb("wr", [P, 4], F32)
        wsb = FS[:, 4 * F:4 * F + P]

        const_ld, later_ld = sem("const_ld"), sem("later_ld")
        stage_ld = [sem(f"stage_ld{i}") for i in range(4)]
        hi_done, lo_done = sem("prep_hi_done"), sem("prep_lo_done")
        xqk_zero = sem("xqk_zero")
        fills = sem("fills")
        prep_v = sem("prep_v")
        prep_p = sem("prep_p")
        prep_a = sem("prep_a")
        prep_abs = sem("prep_abs")
        wrow_ld = sem("wrow_ld")
        wdown_ld = sem("wdown_ld")
        full = [sem(f"slot_full{s}") for s in range(SLOTS)]
        free = [sem(f"slot_free{s}") for s in range(SLOTS)]
        x_ld, c_ld, out_st = sem("x_ld"), sem("ctx_ld"), sem("out_st")
        ln_var, ln_rstd, xn_rdy = ({n: sem(f"{w}{n}") for n in (1, 2, 3)} for w in ("ln_var", "ln_rstd", "xn_rdy"))
        hi_rdy = sem("hi_rdy")
        rope_rot, rope_sum, rope_hi, rope_lo = sem("rope_rot"), sem("rope_sum"), sem("rope_hi"), sem("rope_lo")
        sc_w = [sem(f"scratch_write{i}") for i in range(2)]
        xsc_w = sem("x_scratch_write")
        qa_ld = [sem(f"qa_ld{i}") for i in range(2)]
        xqk_ld = sem("xqk_ld")
        s_done = [sem(f"self_scores_done{b}") for b in range(G)]
        mr_rdy = {k: sem(f"mr_rdy_{k}") for k in "ac"}
        mb_ld = {k: [sem(f"mb_ld_{k}{i}") for i in range(2)] for k in "ac"}
        sm_rdy, es_rdy = sem("sm_rdy"), sem("es_rdy")
        xb_rdy = sem("xb_rdy")
        yk_rdy, tk_rdy = sem("yk_rdy"), sem("tk_rdy")
        abs_rdy, qs_rdy, q_rdy = sem("abs_rdy"), sem("qs_rdy"), sem("q_rdy")
        th_rdy, w_rdy, t_rdy = sem("th_rdy"), sem("w_rdy"), sem("t_rdy")
        out_mul, out_rdy = sem("out_mul"), sem("out_rdy")
        v_self = sem("dve_step")
        stood = sem("stood")

        def wait_at(eng, semaphore, g, per_group, k):
            it, c = g
            if it is not None:
                assert c * per_group + k > 0
                eng.wait_ge(semaphore, it * (2 * per_group) + (c * per_group + k))
            elif c * per_group + k > 0:
                eng.wait_ge(semaphore, c * per_group + k)

        def index(g):
            return g[1] if g[0] is None else g[0] * 2 + g[1]

        def position(at, t, groups_back):
            name, it, unit = at
            bodies_back = 0 if unit == t else groups_back + lag_of[unit] - lag_of[t]
            assert bodies_back in (0, 1), (unit, t)
            names = [n for n, _ in order]
            name = names[names.index(name) - bodies_back]
            late = (loops - 1) * per_loop[slot_of[t]] if bodies_back and name == "loop1" else 0
            return it, slot_of[t], before[name, t] + late

        def claim(at, *t):
            it, n, k = position(at, t, 0)
            return free[n], it, n, k + 1

        def filled(at, *t):
            it, n, k = position(at, t, 0)
            return full[n], it, n, k + 1

        def drained(at, *t, groups_back=0):
            it, n, k = position(at, t, groups_back)
            return free[n], it, n, k + 2

        def wait(eng, *positions):
            for i, (s, it, n, k) in enumerate(positions):
                if not any(s is s2 and (k2, j) > (k, i) for j, (s2, _, _, k2) in enumerate(positions) if j != i):
                    eng.wait_ge(s, k if it is None else it * per_loop[n] + k)

        def tile(at, *t):
            return slot[slot_of[t]]

        def full_sem(at, *t):
            return full[slot_of[t]]

        def free_sem(at, *t):
            return free[slot_of[t]]

        def run(eng, part, body_done=lambda name: None):
            def body(name, n, it):
                for lag, unit in units[name]:
                    c = n + lag
                    part((name, it, unit), (it, c), c % 2, unit)
            i = 0
            while i < len(order):
                if order[i][0] == "loop0":
                    with eng.Fori(0, loops) as it:
                        body("loop0", order[i][1], it)
                        body("loop1", order[i + 1][1], it)
                    body_done("loop1")
                    i += 2
                else:
                    body(order[i][0], order[i][1], None)
                    i += 1

        def rope_lo_half(eng, g, n):
            wait_at(eng, rope_hi, g, QUADS, n + 1)
            eng.tensor_tensor(R[n % 2][:, 2:4, :], rsum[:, n % 2, :, :], R[n % 2][:, 0:2, :], ALU.subtract).then_inc(rope_lo, 1)

        def stand(eng):
            eng.sem_inc(stood, 1)

        consts = [(idx_d[:], io["idx_d"]), (idx_u[:], io["idx_u"]), (iota, io["iota"]), (id32[:], io["id32"]),
                  (bqk[:], io["bqk"])]
        later = [(cosT[:], io["cosT"]), (sinT[:], io["sinT"]), (bv_bc[:], io["bv"]), (bo_bc[:], io["bo"]),
                 (sink_bc[:], io["sinks"]), (maskM[:], io["maskM"]), (idb[:], io["idb"])]
        later += [(m[0:T, :], io["maskT"][:, 0:m.shape[1]]) for m in MB["a"] + MB["c"][:1]]
        splits = [(io["wqkT"][:, c, 1024 * i:min(1024 * i + 1024, 2560)],
                   wqk[0][:, c, 1024 * i:min(1024 * i + 1024, 2560)],
                   wqk[1][:, c, 1024 * i:min(1024 * i + 1024, 2560)], min(1024, 2560 - 1024 * i))
                  for c in range(CD) for i in range(3)]
        splits += [(io["wvT"][:, c, :], wv[0][:, c, :], wv[1][:, c, :], 512) for c in range(CD)]
        splits += [(io["woT"][:, 1024 * i:1024 * i + 1024], wo[0][:].rearrange("p c d -> p (c d)")[:, 1024 * i:1024 * i + 1024],
                    wo[1][:].rearrange("p c d -> p (c d)")[:, 1024 * i:1024 * i + 1024], 1024) for i in range(4)]
        splits += [(io["wxqT"], wxq[0][:].rearrange("p c d -> p (c d)"), wxq[1][:].rearrange("p c d -> p (c d)"), 512),
                   (io["wxoT"], wxo[0][:].rearrange("p c d -> p (c d)"), wxo[1][:].rearrange("p c d -> p (c d)"), 512),
                   (io["wkvT"], wkv[0][:], wkv[1][:], 512)]
        NS = len(splits)
        wrows = [(m, c, P if c < FC - 1 else FL, D) for m in ("g", "u") for c in range(FC)]
        wrows += [("d", c, P, F) for c in range(CD)]
        sc = io["scratch"]
        xsc = io["xscratch"]

        lag_of = {unit: lag for lag, unit in ORDER}

        block = ctx.enter_context(nc.Block())

        @block.sync
        def _(sp):
            for dst, src in consts:
                sp.dma_start(dst, src).then_inc(const_ld, 16)
            for n, (src, _hi, _lo, cols) in enumerate(splits):
                if n >= 4:
                    if n - 4 < len(later):
                        sp.dma_start(*later[n - 4]).then_inc(later_ld, 16)
                    sp.wait_ge(lo_done, n - 3)
                sp.dma_start(stage[n % 4][:, 0:cols], src).then_inc(stage_ld[n % 4], 16)
            for dst, src in later[NS - 4:]:
                sp.dma_start(dst, src).then_inc(later_ld, 16)
            def part(at, g, i, unit):
                what = unit[0]
                if what == "scale rows" and 2 * FC <= unit[1] + 1 < 2 * FC + CD:
                    n = unit[1]
                    sp.wait_ge(prep_v, VBASE[n] + 1)
                    sp.dma_start(wf[0], io["w_down"][P * (n + 1 - 2 * FC):P * (n + 2 - 2 * FC), :]).then_inc(wdown_ld, 16)
                elif what == "load":
                    if g[1] >= 2:
                        wait(sp, drained(at, "Y", "a", G - 1, 0, groups_back=2))
                        stand(sp)
                    sp.dma_start(X1[i][:], io["x"][index(g)].rearrange("b t d -> t b d")).then_inc(x_ld, 16)
                elif what == "split":
                    n = unit[1]
                    wait_at(sp, rope_lo, g, QUADS, n + 1)
                    stand(sp)
                    sp.dma_start(sc[index(g), QUAD_ORDER[n]], R[n % 2][:]).then_inc(sc_w[n % 2], 16)
                elif what == "qload":
                    b = unit[1]
                    if b == 0:
                        for p in range(2):
                            wait_at(sp, sc_w[p], g, 8 * QUADS, 8 * QUADS)
                            stand(sp)
                    wait_at(sp, s_done[b], g, 1, 0)
                    stand(sp)
                    for k in range(4):
                        src = sc[index(g), 0:8, :, k, b * T:(b + 1) * T].rearrange("u (h f) t -> f (u h) t", h=4)
                        sp.dma_start(qa[b][32 * k:32 * k + 32], src).then_inc(qa_ld[b], 16)
                    for row, k, dst in ((0, 0, KA), (32, 1, KA), (64, 0, KA), (96, 1, KA), (0, 2, KB), (32, 3, KB)):
                        src = sc[index(g), 8:10, :, k, b * T:(b + 1) * T].rearrange("u (h f) t -> f (u h) t", h=4)
                        sp.dma_start(dst[b][row:row + 32], src).then_inc(qa_ld[b], 16)
                elif what == "mT":
                    _, kind, b, _ = unit
                    h = KINDS[kind][0]
                    wait_at(sp, mr_rdy[kind], g, G, b + 1)
                    stand(sp)
                    for k in range(3):
                        sp.dma_start(MB[kind][b][T + k:T + k + 1, 0:h * T], MR[kind][b][0:h, k, :]).then_inc(mb_ld[kind][b], 16)
                elif what == "cload":
                    if g[1] >= 1:
                        wait(sp, drained(at, "ctxT", groups_back=1))
                        stand(sp)
                    sp.dma_start(C0[:], io["ctx"][index(g)].rearrange("b t d -> t b d")).then_inc(c_ld, 16)
                elif what == "xload":
                    if g[1] == 0:
                        sp.wait_ge(xqk_zero, 2)
                    for n, t in enumerate(("xq", "xk")):
                        wait(sp, drained(at, t))
                        stand(sp)
                        sp.dma_start(xsc[index(g), n].rearrange("k c p n -> p (k c) n"), RX[n][:]).then_inc(xsc_w, 16)
                    wait_at(sp, xsc_w, g, 32, 32)
                    stand(sp)
                    if g[1] >= 1:
                        wait(sp, drained(at, "S", "c", 1, 1, groups_back=1))
                        stand(sp)
                    for n, dst in ((0, XQ), (1, XK)):
                        for row, k in enumerate((0, 1, 0) if n == 0 else (0, 0, 1)):
                            src = xsc[index(g), n, k].rearrange("c (h r) n -> r (c h) n", h=8)
                            sp.dma_start(dst[16 * row:16 * row + 16], src).then_inc(xqk_ld, 16)
                elif what == "D":
                    b = unit[1]
                    wait_at(sp, out_rdy, g, G, b + 1)
                    stand(sp)
                    sp.dma_start(io["out"][index(g), b], OUT[:, b, :]).then_inc(out_st, 16)

            run(sp, part)
            sp.wait_ge(out_st, 16 * B)

        @block.tensor
        def _(pe):
            for which, chunks, cols, o in (("d", FC, F, 0), ("u", CD, D, FC)):
                for c in range(chunks):
                    k = FL if which == "d" and c == FC - 1 else P
                    pe.wait_ge(prep_v, 3 + o + c)
                    for h in range(2):
                        w = cols // 2
                        last = pe.matmul(slot[0 if which == "d" else 1][:, h, 0:w], ones_b[0:k],
                                         onehot[0:k, h * w:(h + 1) * w], start=(c == 0), stop=(c == chunks - 1))
                    last.then_inc(prep_p, 1)
            pe.wait_ge(lo_done, NS + 1)

            def product(out, a, b, pairs, first=True, last=True):
                for i, (x, y) in enumerate(pairs):
                    ins = pe.matmul(out, a(x), b(y), start=(first and i == 0), stop=(last and i == len(pairs) - 1))
                return ins

            HL = ((0, 0), (0, 1), (1, 0))

            def columns(b):
                return slice(b * T, (b + 1) * T)

            def scores_for_max(at, g, kind, b, j):
                t = ("M", kind, b, j)
                wait(pe, claim(at, *t))
                if kind == "a" and j == 0:
                    wait_at(pe, qa_ld[b], g, 160, 160)
                if kind == "c" and j == 0 and b == 0:
                    wait_at(pe, xqk_ld, g, 96, 96)
                for k in range(2):
                    pe.matmul(tile(at, *t)[0:T, k, 0:4 * T], idb[0:T, :], maskM[:], start=True, stop=False)
                    for h in range(4):
                        head = 8 * j + 4 * k + h
                        if kind == "a":
                            q, key = qa[b][:, head, :], KA[b][:, head // 4, :]
                        else:
                            q, key = XQ[:, head, columns(b)], XK[:, head, columns(b)]
                        ins = pe.matmul(tile(at, *t)[0:T, k, h * T:(h + 1) * T], q, key, start=False, stop=(h == 3))
                ins.then_inc(full_sem(at, *t), 1)

            def scores(at, g, kind, b, j):
                t = ("S", kind, b, j)
                wait(pe, claim(at, *t))
                if j == 0:
                    wait_at(pe, mb_ld[kind][b], g, 48, 48)
                for k in range(2):
                    h0 = 8 * j + 4 * k
                    out = tile(at, *t)[0:T, k, 0:4 * T]
                    pe.matmul(out, idb[:], MB[kind][b][:, h0 * T:(h0 + 4) * T], start=True, stop=False)
                    if kind == "a":
                        q = qa[b][:, h0:h0 + 4, :]
                        pe.matmul(out, KA[b][:, h0 // 4, :], q, start=False, stop=False)
                        ins = pe.matmul(out, KB[b][:, h0 // 4, :], q, start=False, stop=True)
                    else:
                        for h in range(4):
                            ins = pe.matmul(tile(at, *t)[0:T, k, h * T:(h + 1) * T], XK[:, h0 + h, columns(b)],
                                            XQ[:, h0 + h, columns(b)], start=False, stop=(h == 3))
                ins.then_inc(full_sem(at, *t), 1)

            def values(at, g, i, kind, b, j):
                t = ("V", kind, b, j)
                last_tile = KINDS[kind][0] // 8 - 1
                needs = [claim(at, *t), drained(at, "S", kind, b, j)]
                if kind == "c":
                    needs.append(drained(at, "xv", b))
                wait(pe, *needs)
                for n in range(8):
                    head = 8 * j + n
                    if kind == "a":
                        v = V[i][:, b, head // 4 * VS:head // 4 * VS + W]
                    else:
                        v = XV[:, b, head * XS:head * XS + W]
                    p = j % 2 if kind == "a" else 0
                    ins = pe.matmul(tile(at, *t)[0:T, n // 4, (n % 4) * W:(n % 4) * W + W],
                                    PR[kind][:, p, n * T:(n + 1) * T], v, start=True, stop=True)
                    if n == 0 and kind == "a" and j == last_tile:
                        ins.then_inc(s_done[b], 1)
                ins.then_inc(full_sem(at, *t), 1)

            def outputs_to_columns(at, kind, b, j):
                t = ("OT", kind, b, j)
                n = 4 if kind == "a" else CD
                wait(pe, claim(at, *t),
                     drained(at, "V", kind, b, j if kind == "a" else 1))
                for c in range(n):
                    ins = pe.transpose(tile(at, *t)[:, 0, c * T:(c + 1) * T],
                                       ON[kind][:, j % 2, c * P:(c + 1) * P], id32[0:T, 0:T])
                ins.then_inc(full_sem(at, *t), 1)

            def project(at, kind, b):
                t = ("Y", kind, b, 0)
                n, w = (16, wo) if kind == "a" else (CD, wxo)
                wait(pe, claim(at, *t), *(drained(at, "OT", kind, b, j) for j in range(4 if kind == "a" else 1)))
                for c in range(n):
                    ins = product(tile(at, *t)[0:T, 0, 0:D], lambda i: OT[kind][i][:, c, :], lambda i: w[i][:, c, :],
                                  HL, c == 0, c == n - 1)
                ins.then_inc(full_sem(at, *t), 1)

            def part(at, g, i, unit):
                what = unit[0]
                if what in ("xT", "qk", "v", "ctxT", "xq", "xk", "xv", "qT", "G", "U", "tT", "D"):
                    ps, done = tile(at, *unit), full_sem(at, *unit)
                if what == "turn rows":
                    n = unit[1]
                    _m, _c, rows, cols = wrows[n]
                    wait(pe, claim(at, *unit))
                    pe.wait_ge(prep_a, n + 1)
                    ps = tile(at, *unit)
                    for k in range(-(-cols // P)):
                        kk = min(P, cols - k * P)
                        pe.transpose(ps[:].bitcast(F16)[0:kk, 0, k * P:k * P + rows], wq[0:rows, k * P:k * P + kk],
                                     id16[0:rows, 0:rows])
                    pe.matmul(ps[:, 0, 512 - P:512 - P + rows], wsb[0:rows], id32[0:rows, 0:rows],
                              start=True, stop=True).then_inc(full_sem(at, *unit), 1)
                elif what == "xT":
                    n = unit[1]
                    wait_at(pe, xn_rdy[n], g, 1, 1)
                    wait(pe, claim(at, *unit))
                    for c in range(CD):
                        for b in range(G):
                            ins = pe.transpose(ps[:, 0, c * N + b * T:c * N + (b + 1) * T], XN[n][:, b, c * P:(c + 1) * P],
                                               id32[0:T, 0:T])
                    ins.then_inc(done, 1)
                elif what == "qk":
                    wait(pe, claim(at, *unit), drained(at, "xT", 1))
                    for h in range(2):
                        col = QUAD_ORDER[unit[1]] * 256 + h * P
                        for c in range(CD):
                            ins = product(ps[:, 0, h * N:(h + 1) * N], lambda k: wqk[k][:, c, col:col + P],
                                          lambda k: xT[1][k][:, c, :], HL, c == 0, c == CD - 1)
                    ins.then_inc(done, 1)
                elif what == "v":
                    wait(pe, claim(at, *unit))
                    for c in range(CD):
                        ins = product(ps[0:T, 0, :], lambda k: xT[1][k][:, c, columns(unit[1])], lambda k: wv[k][:, c, :],
                                      HL, c == 0, c == CD - 1)
                    ins.then_inc(done, 1)
                elif what == "M":
                    scores_for_max(at, g, *unit[1:])
                elif what == "mT":
                    _, kind, b, _ = unit
                    h = KINDS[kind][0]
                    wait(pe, claim(at, *unit), drained(at, "M", kind, b, h // 8 - 1))
                    pe.transpose(tile(at, *unit)[0:h, 0, 0:T], mx[kind][b][:, 0:h], id32[0:T, 0:T]).then_inc(full_sem(at, *unit), 1)
                elif what == "S":
                    scores(at, g, *unit[1:])
                elif what == "V":
                    values(at, g, i, *unit[1:])
                elif what == "OT":
                    outputs_to_columns(at, *unit[1:])
                elif what == "Y":
                    project(at, *unit[1:3])
                elif what == "ctxT":
                    wait_at(pe, c_ld, g, 16, 16)
                    wait(pe, claim(at, *unit))
                    stand(pe)
                    for b in range(G):
                        ins = pe.transpose(ps[0:L, 0, columns(b)], C0[:, b, :], id32[0:T, 0:T])
                    ins.then_inc(done, 1)
                elif what == "xq":
                    wait(pe, claim(at, *unit), drained(at, "xT", 2))
                    for m in range(CD):
                        for c in range(CD):
                            ins = product(ps[:, 0, m * N:(m + 1) * N], lambda k: wxq[k][:, c, m * P:(m + 1) * P],
                                          lambda k: xT[2][k][:, c, :], HL, c == 0, c == CD - 1)
                    ins.then_inc(done, 1)
                elif what == "xk":
                    wait(pe, claim(at, *unit), drained(at, "ctxT"))
                    for m in range(CD):
                        ins = product(ps[:, 0, m * N:(m + 1) * N], lambda k: wkv[k][:, m * P:(m + 1) * P], lambda k: CT[:],
                                      ((0, 0), (1, 0)))
                    ins.then_inc(done, 1)
                elif what == "xv":
                    wait(pe, claim(at, *unit))
                    product(ps[0:T, 0, 0:D], lambda k: CT[:, columns(unit[1])], lambda k: wkv[k][:, D:2 * D],
                            ((0, 0), (0, 1))).then_inc(done, 1)
                elif what == "qT":
                    wait(pe, claim(at, *unit))
                    wait_at(pe, q_rdy, g, 2 * G, Q_Y[unit[1]])
                    for c in range(CD):
                        ins = pe.transpose(ps[:].bitcast(F16)[:, 0, c * T:(c + 1) * T], yq[:, unit[1], c * P:(c + 1) * P],
                                           id16[0:T, 0:T])
                    ins.then_inc(done, 1)
                elif what in ("G", "U"):
                    w = wgT if what == "G" else wuT
                    wait(pe, claim(at, *unit), drained(at, "qT", unit[1]))
                    for h in range(2):
                        for c in range(CD):
                            ins = pe.matmul(ps[0:T, h, 0:FH], qT[:, c, :], w[:, c, h * FH:(h + 1) * FH],
                                            start=(c == 0), stop=(c == CD - 1))
                    ins.then_inc(done, 1)
                elif what == "tT":
                    wait(pe, claim(at, *unit))
                    wait_at(pe, q_rdy, g, 2 * G, Q_T[unit[1]])
                    for c in range(FC):
                        k = P if c < FC - 1 else FL
                        ins = pe.transpose(ps[:].bitcast(F16)[0:k, 0, c * T:(c + 1) * T], tq[:, c * P:c * P + k], id16[0:T, 0:T])
                    ins.then_inc(done, 1)
                elif what == "D":
                    wait(pe, claim(at, *unit), drained(at, "tT", unit[1]))
                    for c in range(FC):
                        k = P if c < FC - 1 else FL
                        ins = pe.matmul(ps[0:T, 0, 0:D], tT[0:k, c, :], wdT[0:k, c, :], start=(c == 0), stop=(c == FC - 1))
                    ins.then_inc(done, 1)

            run(pe, part)

        @block.scalar
        def _(act):
            for n, (_src, hi, _lo, cols) in enumerate(splits):
                act.wait_ge(stage_ld[n % 4], 16 * (n // 4 + 1))
                act.activation(hi, stage[n % 4][:, 0:cols], ACT.Copy, scale=WS).then_inc(hi_done, 1)
            act.wait_ge(lo_done, NS + 1)

            def part(at, g, i, unit):
                what = unit[0]
                if what == "scale rows":
                    n = unit[1]
                    _m, _c, rows, cols = wrows[n]
                    act.wait_ge(prep_v, VBASE[n] + 5)
                    act.activation(wf[2][0:rows, 0:cols], wf[1][0:rows, 0:cols], ACT.Abs,
                                   scale=wr[0:rows, 3:4]).then_inc(prep_abs, 1)
                elif what == "round rows":
                    n = unit[1]
                    rows = wrows[n][2]
                    act.wait_ge(prep_v, VBASE[n] + 9)
                    act.activation(wsb[0:rows], id32[0:rows, :], ACT.Identity, bias=wr[0:rows, 0:1],
                                   scale=0.0).then_inc(prep_a, 1)
                elif what in ("xT", "ctxT", "xq", "xk", "OT"):
                    ps = tile(at, *unit)
                    scale = 1.0
                    if what == "xT":
                        out, src = xT[unit[1]][0][:].rearrange("p c n -> p (c n)"), ps[:, 0, 0:CD * N]
                    elif what == "ctxT":
                        out, src = CT[0:L, :], ps[0:L, 0, 0:N]
                    elif what == "OT":
                        _, kind, b, j = unit
                        n = 4 if kind == "a" else CD
                        out = OT[kind][0][:, n * j:n * (j + 1), :].rearrange("p c t -> p (c t)")
                        src = ps[:, 0, 0:n * T]
                    else:
                        wait_at(act, xsc_w, g, 32, 0)
                        out = RX[what == "xk"][:, 0:2, :].rearrange("p k n -> p (k n)")
                        src, scale = ps[:, 0, 0:2 * N], 1.0 / WS
                    wait(act, filled(at, *unit))
                    act.activation(out, src, ACT.Copy, scale=scale).then_inc(hi_rdy, 1)
                elif what == "qk":
                    n = unit[1]
                    u = QUAD_ORDER[n]
                    wait(act, filled(at, *unit))
                    wait_at(act, rope_sum, g, QUADS, n - 1)
                    for h in range(2):
                        ins = act.activation(ab[:, n % 2, h, :], tile(at, *unit)[:, 0, h * N:(h + 1) * N], ACT.Identity,
                                             bias=bqk[:, 2 * u + h:2 * u + h + 1])
                    ins.then_inc(free_sem(at, *unit), 1)
                elif what == "split":
                    n = unit[1]
                    wait_at(act, rope_sum, g, QUADS, n + 1)
                    wait_at(act, sc_w[n % 2], g, 8 * QUADS, 16 * (n // 2))
                    act.activation(R[n % 2][:, 0:2, :], rsum[:, n % 2, :, :], ACT.Copy).then_inc(rope_hi, 1)
                elif what == "S":
                    _, kind, b, j = unit
                    wait(act, filled(at, *unit))
                    act.activation(PR[kind][:, j % 2 if kind == "a" else 0, :].rearrange("p (k n) -> p k n", k=2),
                                   tile(at, *unit)[0:T, :, 0:4 * T], ACT.Exp, scale=KINDS[kind][1]).then_inc(free_sem(at, *unit), 1)
                elif what == "mT" and unit[1] == "a":
                    b = unit[2]
                    wait_at(act, sm_rdy, g, G, b + 1)
                    act.activation(es[b][:], sm[b][:], ACT.Exp).then_inc(es_rdy, 1)
                elif what == "y":
                    b = unit[1]
                    if b == 0:
                        wait_at(act, yk_rdy, g, 1, 1)
                        wait_at(act, q_rdy, g, 2 * G, 0)
                    else:
                        wait_at(act, q_rdy, g, 2 * G, Q_Y[b - 1])
                    act.activation(yM, XN[3][:, b, :], ACT.Abs, scale=kMy[:, b:b + 1]).then_inc(abs_rdy, 1)
                elif what == "qT":
                    wait(act, filled(at, *unit))
                    act.activation(qT.rearrange("p c t -> p (c t)"), tile(at, *unit)[:].bitcast(F16)[:, 0, 0:CD * T],
                                   ACT.Copy).then_inc(free_sem(at, *unit), 1)
                elif what == "h":
                    wait(act, drained(at, "G", unit[1]))
                    act.activation(th, gs, ACT.Tanh, scale=0.5).then_inc(th_rdy, 1)
                elif what == "tq":
                    b = unit[1]
                    wait_at(act, tk_rdy, g, G, b + 1)
                    act.activation(tM, us, ACT.Abs, scale=kMt[:, b:b + 1]).then_inc(abs_rdy, 1)
                elif what == "D":
                    b = unit[1]
                    wait(act, filled(at, *unit))
                    if b == 0:
                        wait_at(act, out_st, g, 16 * G, 0)
                    act.activation(OUT[:, b, :], tile(at, *unit)[0:T, 0, 0:D], ACT.Copy,
                                   scale=st_[:, b:b + 1]).then_inc(free_sem(at, *unit), 1)
                elif what == "tT":
                    s = tile(at, *unit)[:].bitcast(F16)
                    wait(act, filled(at, *unit))
                    act.activation(tT[:, 0:FC - 1, :].rearrange("p c t -> p (c t)"), s[:, 0, 0:(FC - 1) * T], ACT.Copy)
                    act.activation(tT[0:FL, FC - 1, :], s[0:FL, 0, (FC - 1) * T:FC * T], ACT.Copy).then_inc(free_sem(at, *unit), 1)

            run(act, part)

        @block.gpsimd
        def _(pool):
            pool.wait_ge(const_ld, 16 * len(consts))
            def gather(n):
                m, c, rows, _cols = wrows[n]
                pool.indirect_dma_start(out=wf[0][0:rows, 0:D], out_offset=None, in_=io["w_gate" if m == "g" else "w_up"],
                                        in_offset=bass.IndirectOffsetOnAxis(ap=idx_d[0:rows, c:c + 1], axis=0)).then_inc(wrow_ld, 16)

            gather(0)
            pool.wait_ge(lo_done, NS)
            pool.memset(XQs[:].bitcast(F32), 0.0).then_inc(xqk_zero, 1)
            pool.memset(XKs[:].bitcast(F32), 0.0).then_inc(xqk_zero, 1)

            def part(at, g, i, unit):
                what = unit[0]
                if what == "scale rows":
                    n = unit[1]
                    if n + 1 < 2 * FC:
                        pool.wait_ge(prep_v, VBASE[n] + 1)
                        gather(n + 1)
                elif what == "ln":
                    n = unit[1]
                    wait_at(pool, ln_var[n], g, 1, 1)
                    pool.tensor_tensor(rstd[n][:], ve[n][:], half[:], ALU.pow).then_inc(ln_rstd[n], 1)
                elif what == "nrm" and unit[1] == 1:
                    wait_at(pool, xn_rdy[1], g, 1, 1)
                    pool.tensor_tensor(X1[i][:], X1[i][:], bo_bc[:].unsqueeze(1).broadcast_to([T, G, D]), ALU.add).then_inc(xb_rdy, 1)
                elif what == "qk":
                    n = unit[1]
                    k = n % 2
                    wait_at(pool, rope_rot, g, QUADS, n + 1)
                    wait_at(pool, rope_lo, g, QUADS, n - 1)
                    pool.tensor_tensor(rsum[:, k, 0, :], abcos[:, k, 0, :], ab[:, k, 1, :], ALU.subtract)
                    pool.tensor_tensor(rsum[:, k, 1, :], abcos[:, k, 1, :], ab[:, k, 0, :], ALU.add).then_inc(rope_sum, 1)
                elif what == "split" and at[0] not in DVE_SPLITS:
                    rope_lo_half(pool, g, unit[1])
                elif what == "D":
                    b = unit[1]
                    wait(pool, drained(at, *unit))
                    pool.tensor_tensor(OUT[:, b, :], OUT[:, b, :], sd_bc[0:T, :], ALU.mult).then_inc(out_mul, 1)
                    wait_at(pool, out_mul, g, G, b + 1)
                    pool.tensor_tensor(OUT[:, b, :], OUT[:, b, :], X3[i][:, b, :], ALU.add).then_inc(out_rdy, 1)
                elif what == "y":
                    b = unit[1]
                    wait_at(pool, qs_rdy, g, 2 * G, Q_Y[b])
                    pool.tensor_tensor(yq[:, b, :], yS, yM, ALU.subtract).then_inc(q_rdy, 1)
                elif what == "h":
                    wait_at(pool, w_rdy, g, G, unit[1] + 1)
                    pool.tensor_tensor(us, th, us, ALU.mult).then_inc(t_rdy, 1)
                elif what == "tq":
                    wait_at(pool, qs_rdy, g, 2 * G, Q_T[unit[1]])
                    pool.tensor_tensor(tq, tS, tM, ALU.subtract).then_inc(q_rdy, 1)

            run(pool, part)

        @block.vector
        def _(dve):
            n_fill = [0]

            def fill(ins):
                n_fill[0] += 1
                ins.then_inc(fills, 1)

            for s in range(SLOTS):
                dve.sem_inc(free[s], 1)
            fill(dve.memset(half[:], -0.5))
            fill(dve.memset(ones_b, 1.0))
            for i in range(2):
                fill(dve.memset(KB[i][HD:P, :, :], 0.0))
            fill(dve.memset(V[0][:], 0.0))
            fill(dve.memset(V[1][:], 0.0))
            fill(dve.memset(XV[:], 0.0))
            dve.wait_ge(fills, n_fill[0])
            for b in range(G):
                for i in range(2):
                    fill(dve.memset(V[i][:, b, 0:NKV * VS].rearrange("p (h w) -> p h w", w=VS)[:, :, HD:VS], 1.0))
                fill(dve.memset(XV[:, b, 0:XH * XS].rearrange("p (h w) -> p h w", w=XS)[:, :, XD:XS], 1.0))
            dve.wait_ge(const_ld, 16 * len(consts))
            fill(dve.tensor_copy(id16[:], id32[:]))
            fill(dve.tensor_scalar(bqk[:], bqk[:], WS, None, ALU.mult))
            dve.wait_ge(fills, n_fill[0])

            nv = [0]

            def prep(ins):
                nv[0] += 1
                ins.then_inc(prep_v, 1)

            def prep_settled():
                dve.wait_ge(prep_v, nv[0])

            prep(dve.tensor_copy(idxf[:, 0:FC], idx_d[:]))
            prep(dve.tensor_copy(idxf[:, FC:FC + CD], idx_u[:]))
            prep_settled()
            def one_hot(c):
                k = FL if c == FC - 1 else P
                w = F if c < FC else D
                if c:
                    dve.wait_ge(prep_p, c)
                prep(dve.tensor_scalar(onehot[0:k, 0:w], iota[0:k, 0:w], idxf[0:k, c:c + 1], None, ALU.is_equal))

            for n, (_src, hi, lo, cols) in enumerate(splits):
                if n < FC + CD:
                    one_hot(n)
                dve.wait_ge(hi_done, n + 1)
                dve.scalar_tensor_tensor(out=lo, in0=stage[n % 4][:, 0:cols], scalar=WS, in1=hi, op0=ALU.mult,
                                         op1=ALU.subtract).then_inc(lo_done, 1)
            dve.wait_ge(prep_p, FC + CD)
            for s, w, cnt, mask in ((slot[0], F, cnt4, maskd), (slot[1], D, cnt4u, mask_u[:])):
                v = s[:, :, 0:w // 2]
                prep(dve.tensor_scalar(cnt.rearrange("p (k n) -> p k n", k=2), v, 0.25, None, ALU.mult))
                prep(dve.tensor_scalar(mask.rearrange("p (k n) -> p k n", k=2), v, 1.0, None, ALU.min))
            prep_settled()
            assert nv[0] == PREP_V0

            dve.wait_ge(lo_done, NS)
            dve.wait_ge(later_ld, 16 * len(later))
            dve.memset(wkv[1][L:P, :], 0.0).then_inc(lo_done, 1)

            def prepare_rows(at, what, unit):
                n = unit[1]
                m, c, rows, cols = wrows[n]
                r = slice(0, rows)
                w0, w1, w2, w3 = (wf[i][r, 0:cols] for i in range(4))
                mask, cnt = (maskd, cnt4) if m == "d" else (mask_u[:], cnt4u)
                if what == "scale rows":
                    assert nv[0] == VBASE[n]
                    if m == "d":
                        dve.wait_ge(wdown_ld, 16 * (c + 1))
                    else:
                        dve.wait_ge(wrow_ld, 16 * (n + 1))
                    prep(dve.tensor_tensor(w1, w0, mask[r, :], ALU.mult))
                    prep_settled()
                    prep(dve.tensor_reduce(wr[r, 0:1], w1, AX.X, ALU.max, apply_absolute_value=True))
                    prep_settled()
                    prep(dve.reciprocal(wr[r, 1:2], wr[r, 0:1]))
                    prep_settled()
                    prep(dve.tensor_scalar(wr[r, 2:3], wr[r, 1:2], FP8_MAX, None, ALU.mult))
                    prep(dve.tensor_scalar(wr[r, 3:4], wr[r, 1:2], FP8_MAX * 2.0 ** 20, None, ALU.mult))
                elif what == "round rows":
                    dve.wait_ge(prep_abs, n + 1)
                    prep(dve.tensor_scalar(w2, w2, SUB, None, ALU.max))
                    prep_settled()
                    prep(dve.scalar_tensor_tensor(out=w3, in0=w1, scalar=wr[r, 2:3], in1=w2, op0=ALU.mult, op1=ALU.add))
                    prep_settled()
                    prep(dve.tensor_tensor(w3, w3, w2, ALU.subtract))
                    prep_settled()
                    prep(dve.tensor_tensor(wq[r, 0:cols], w3, cnt[r, :], ALU.mult))
                else:
                    wait(dve, filled(at, *unit))
                    ps = tile(at, *unit)
                    s = ps[:].bitcast(F16)
                    if m == "d":
                        prep(dve.tensor_copy(wdT[:, 0:FC - 1, c * P:(c + 1) * P],
                                             s[:, 0, 0:(FC - 1) * P].rearrange("p (k n) -> p k n", n=P)))
                        prep(dve.tensor_copy(wdT[0:FL, FC - 1, c * P:(c + 1) * P], s[0:FL, 0, (FC - 1) * P:FC * P]))
                    else:
                        wT = wgT if m == "g" else wuT
                        prep(dve.tensor_copy(wT[:, :, c * P:c * P + rows],
                                             s[:, 0, 0:CD * P].rearrange("p (k n) -> p k n", n=P)[:, :, 0:rows]))
                    out = {"g": sg_bc, "u": su_bc, "d": sd_bc}[m][:, c * P:c * P + rows]
                    scales = ps[:, 0, 512 - P:512 - P + rows]
                    if m == "u":
                        prep(dve.scalar_tensor_tensor(out=out, in0=scales, scalar=4.0 / FP8_MAX,
                                                      in1=maskd[:, c * P:c * P + rows], op0=ALU.mult, op1=ALU.mult))
                    else:
                        prep(dve.tensor_scalar(out, scales, (4.0 if m == "g" else 2.0) / FP8_MAX, None, ALU.mult))
                    prep_settled()
                    dve.sem_inc(free_sem(at, *unit), 1)

            steps = [0]

            def step(ins):
                steps[0] += 1
                ins.then_inc(v_self, 1)

            def settled(g):
                dve.wait_ge(v_self, steps[0] if g[0] is None else g[0] * (2 * V_STEPS) + steps[0])

            def lo_of(at, unit, out, src, hi, scale=None):
                k = hi_at[at[0], unit] + 1
                dve.wait_ge(hi_rdy, k if at[1] is None else at[1] * hi_per_loop + k)
                if scale is None:
                    dve.tensor_tensor(out, src, hi, ALU.subtract).then_inc(free_sem(at, *unit), 1)
                else:
                    dve.scalar_tensor_tensor(out=out, in0=src, scalar=scale, in1=hi, op0=ALU.mult,
                                             op1=ALU.subtract).then_inc(free_sem(at, *unit), 1)

            def round_rows(g, n_job, x, k, m, s):
                wait_at(dve, abs_rdy, g, 2 * G, n_job)
                step(dve.tensor_scalar(m, m, SUB, None, ALU.max))
                settled(g)
                dve.scalar_tensor_tensor(out=s, in0=x, scalar=k, in1=m, op0=ALU.mult, op1=ALU.add).then_inc(qs_rdy, 1)

            def part(at, g, i, unit):
                what = unit[0]
                ps = tile(at, *unit) if what in NARROW_TILES + WIDE_TILES else None
                if what in ("scale rows", "round rows", "turn rows"):
                    prepare_rows(at, what, unit)
                elif what == "ln":
                    n = unit[1]
                    x = (X1, X2, X3)[n - 1][i]
                    if n == 1:
                        wait_at(dve, x_ld, g, 16, 16)
                    for b in range(G):
                        step(dve.bn_stats(stats[n][:, b, :], x[:, b, :]))
                    settled(g)
                    stand(dve)
                    for b in range(G):
                        step(dve.bn_aggr(mv[n][:, b, :], stats[n][:, b, :]))
                    settled(g)
                    dve.tensor_scalar(ve[n][:], mv[n][:, :, 1], EPS, None, ALU.add).then_inc(ln_var[n], 1)
                elif what == "nrm":
                    n = unit[1]
                    x = (X1, X2, X3)[n - 1][i]
                    wait_at(dve, ln_rstd[n], g, 1, 1)
                    if n < 3:
                        for b in range(G):
                            ins = dve.tensor_scalar(XN[n][:, b, :], x[:, b, :], mv[n][:, b, 0:1], rstd[n][:, b:b + 1],
                                                    ALU.subtract, ALU.mult)
                        ins.then_inc(xn_rdy[n], 1)
                    else:
                        for b in range(G):
                            step(dve.scalar_tensor_tensor(out=XN[3][:, b, :], in0=x[:, b, :], scalar=mv[3][:, b, 0:1],
                                                               in1=mask_u[0:T, :], op0=ALU.subtract, op1=ALU.mult))
                        settled(g)
                        step(dve.tensor_reduce(ry[:], XN[3], AX.X, ALU.max, apply_absolute_value=True))
                        settled(g)
                        step(dve.reciprocal(rry[:], ry[:]))
                        settled(g)
                        step(dve.tensor_scalar(ky[:], rry[:], FP8_MAX, None, ALU.mult))
                        step(dve.scalar_tensor_tensor(out=sx[:], in0=ry[:], scalar=1.0 / FP8_MAX, in1=rstd[3][:],
                                                           op0=ALU.mult, op1=ALU.mult))
                        dve.tensor_scalar(kMy[:], rry[:], FP8_MAX * 2.0 ** 20, None, ALU.mult).then_inc(yk_rdy, 1)
                elif what == "xT":
                    n = unit[1]
                    hi, lo = (xT[n][k][:].rearrange("p c n -> p (c n)") for k in range(2))
                    lo_of(at, unit, lo, ps[:, 0, 0:CD * N], hi)
                elif what == "ctxT":
                    lo_of(at, unit, CT[L:P, :], ps[0:L, 0, 0:N], CT[0:L, :])
                elif what in ("xq", "xk"):
                    r = RX[what == "xk"]
                    lo_of(at, unit, r[:, 2:4, :].rearrange("p k n -> p (k n)"), ps[:, 0, 0:2 * N],
                          r[:, 0:2, :].rearrange("p k n -> p (k n)"), 1.0 / WS)
                elif what == "OT":
                    _, kind, b, j = unit
                    n = 4 if kind == "a" else CD
                    hi, lo = (OT[kind][k][:, n * j:n * (j + 1), :].rearrange("p c t -> p (c t)") for k in range(2))
                    lo_of(at, unit, lo, ps[:, 0, 0:n * T], hi)
                elif what == "qk":
                    n = unit[1]
                    k = n % 2
                    wait(dve, drained(at, *unit))
                    dve.tensor_tensor(abcos[:, k], ab[:, k], cosT[:].unsqueeze(1).broadcast_to([P, 2, N]), ALU.mult)
                    dve.tensor_tensor(ab[:, k], ab[:, k], sinT[:].unsqueeze(1).broadcast_to([P, 2, N]), ALU.mult).then_inc(rope_rot, 1)
                elif what == "split" and at[0] in DVE_SPLITS:
                    rope_lo_half(dve, g, unit[1])
                elif what == "v":
                    wait(dve, filled(at, *unit))
                    dve.scalar_tensor_tensor(out=V[i][:, unit[1], 0:NKV * VS].rearrange("p (h w) -> p h w", w=VS)[:, :, 0:HD],
                                             in0=ps[0:T, 0, :].rearrange("p (h d) -> p h d", d=HD), scalar=1.0 / WS,
                                             in1=bv_bc[:].rearrange("p (h d) -> p h d", d=HD),
                                             op0=ALU.mult, op1=ALU.add).then_inc(free_sem(at, *unit), 1)
                elif what == "xv":
                    wait(dve, filled(at, *unit))
                    dve.tensor_scalar(XV[:, unit[1], 0:XH * XS].rearrange("p (h w) -> p h w", w=XS)[:, :, 0:XD],
                                      ps[0:T, 0, 0:D].rearrange("p (h d) -> p h d", d=XD),
                                      1.0 / WS, None, ALU.mult).then_inc(free_sem(at, *unit), 1)
                elif what == "M":
                    _, kind, b, j = unit
                    wait(dve, filled(at, *unit))
                    dve.tensor_reduce(mx[kind][b][:, 8 * j:8 * j + 8], ps[0:T, :, 0:4 * T].rearrange("p k (h n) -> p k h n", n=T),
                                      AX.X, ALU.max).then_inc(free_sem(at, *unit), 1)
                elif what == "mT":
                    _, kind, b, _ = unit
                    nh, scale = KINDS[kind]
                    m, rest = MR[kind][b], mr_rest[kind][0:nh, :]
                    wait(dve, filled(at, *unit))
                    step(dve.tensor_scalar(m[0:nh, 0, :], ps[0:nh, 0, 0:T], -1.0, None, ALU.mult))
                    settled(g)
                    dve.scalar_tensor_tensor(out=rest, in0=ps[0:nh, 0, 0:T], scalar=-1.0, in1=m[0:nh, 0, :],
                                             op0=ALU.mult, op1=ALU.subtract).then_inc(free_sem(at, *unit), 1)
                    wait(dve, drained(at, *unit))
                    step(dve.tensor_copy(m[0:nh, 1, :], rest))
                    settled(g)
                    dve.tensor_tensor(m[0:nh, 2, :], rest, m[0:nh, 1, :], ALU.subtract).then_inc(mr_rdy[kind], 1)
                    if kind == "a":
                        dve.scalar_tensor_tensor(out=sm[b][:], in0=mx["a"][b][:], scalar=-scale, in1=sink_bc[:],
                                                 op0=ALU.mult, op1=ALU.add).then_inc(sm_rdy, 1)
                elif what == "V":
                    _, kind, b, j = unit
                    hd = HD if kind == "a" else XD
                    wait(dve, filled(at, *unit))
                    v = ps[0:T, :, 0:4 * W].rearrange("p k (h w) -> p k h w", w=W)
                    r = rden[kind][:, j % 2].rearrange("p (k h) -> p k h", k=2)
                    if kind == "a":
                        wait_at(dve, es_rdy, g, G, b + 1)
                        step(dve.tensor_tensor(den[:, j % 2].rearrange("p (k h) -> p k h", k=2), v[:, :, :, hd],
                                                   es[b][:, 8 * j:8 * j + 8].rearrange("p (k h) -> p k h", k=2), ALU.add))
                        settled(g)
                        step(dve.reciprocal(rden[kind][:, j % 2], den[:, j % 2]))
                    else:
                        step(dve.reciprocal(r, v[:, :, :, hd]))
                    settled(g)
                    o = ON["a"][:, j % 2, :] if kind == "a" else ON["c"][:, 0, 8 * j * hd:8 * (j + 1) * hd]
                    dve.tensor_tensor(o.rearrange("p (k h d) -> p k h d", k=2, h=4),
                                      v[:, :, :, 0:hd], r.unsqueeze(3).broadcast_to([T, 2, 4, hd]),
                                      ALU.mult).then_inc(free_sem(at, *unit), 1)
                elif what == "Y":
                    _, kind, b, _ = unit
                    x, out = (X1, X2) if kind == "a" else (X2, X3)
                    wait(dve, filled(at, *unit))
                    if kind == "a" and b == 0:
                        wait_at(dve, xb_rdy, g, 1, 1)
                    if kind == "c":
                        wait_at(dve, out_rdy, g, G, b + 1 - 2 * G)
                    dve.scalar_tensor_tensor(out=out[i][:, b, :], in0=ps[0:T, 0, 0:D], scalar=1.0 / WS, in1=x[i][:, b, :],
                                             op0=ALU.mult, op1=ALU.add).then_inc(free_sem(at, *unit), 1)
                    if b == G - 1:
                        wait(dve, drained(at, *unit))
                        stand(dve)
                elif what == "y":
                    b = unit[1]
                    round_rows(g, Q_Y[b], XN[3][:, b, :], ky[:, b:b + 1], yM, yS)
                elif what == "G":
                    b = unit[1]
                    wait(dve, filled(at, *unit))
                    dve.scalar_tensor_tensor(out=gs.rearrange("p (k n) -> p k n", k=2), in0=ps[0:T, :, 0:FH],
                                             scalar=sx[:, b:b + 1], in1=sg_bc[0:T, :].rearrange("p (k n) -> p k n", k=2),
                                             op0=ALU.mult, op1=ALU.mult).then_inc(free_sem(at, *unit), 1)
                elif what == "U":
                    wait(dve, filled(at, *unit))
                    dve.tensor_tensor(us.rearrange("p (k n) -> p k n", k=2), ps[0:T, :, 0:FH],
                                      su_bc[0:T, :].rearrange("p (k n) -> p k n", k=2), ALU.mult).then_inc(free_sem(at, *unit), 1)
                elif what == "h":
                    wait(dve, drained(at, "U", unit[1]))
                    wait_at(dve, th_rdy, g, G, unit[1] + 1)
                    dve.scalar_tensor_tensor(out=th, in0=th, scalar=1.0, in1=gs, op0=ALU.add,
                                             op1=ALU.mult).then_inc(w_rdy, 1)
                elif what == "hk":
                    b = unit[1]
                    c = slice(b, b + 1)
                    wait_at(dve, t_rdy, g, G, b + 1)
                    step(dve.tensor_reduce(rt[:, c], us, AX.X, ALU.max, apply_absolute_value=True))
                    settled(g)
                    step(dve.reciprocal(rrt[:, c], rt[:, c]))
                    settled(g)
                    step(dve.tensor_scalar(kt[:, c], rrt[:, c], FP8_MAX, None, ALU.mult))
                    step(dve.scalar_tensor_tensor(out=st_[:, c], in0=rt[:, c], scalar=1.0 / FP8_MAX,
                                                       in1=sx[:, c], op0=ALU.mult, op1=ALU.mult))
                    dve.tensor_scalar(kMt[:, c], rrt[:, c], FP8_MAX * 2.0 ** 20, None, ALU.mult).then_inc(tk_rdy, 1)
                elif what == "tq":
                    b = unit[1]
                    round_rows(g, Q_T[b], us, kt[:, b:b + 1], tM, tS)

            def body_done(n_body):
                if n_body == "loop1":
                    steps[0] += (loops - 1) * 2 * V_STEPS

            run(dve, part, body_done)


def rope_tables():
    theta, scaling, ntk_alpha, ntk_beta, icl = 150000.0, 32.0, 1.0, 32.0, 128
    d_half = HD // 2
    freq = theta ** (np.arange(0, HD, 2, dtype=np.float32) / HD)
    concentration = 0.1 * math.log(scaling) + 1.0
    low = d_half * math.log(icl / (ntk_beta * 2 * math.pi)) / math.log(theta)
    high = d_half * math.log(icl / (ntk_alpha * 2 * math.pi)) / math.log(theta)
    interpolation = 1.0 / (scaling * freq)
    extrapolation = 1.0 / freq
    ramp = np.clip((np.arange(d_half, dtype=np.float32) - low) / (high - low), 0.0, 1.0)
    mask = 1.0 - ramp
    inv_freq = interpolation * (1.0 - mask) + extrapolation * mask
    freqs = np.outer(np.arange(T, dtype=np.float32), inv_freq)
    return (np.cos(freqs) * concentration).astype(np.float32).T, (np.sin(freqs) * concentration).astype(np.float32).T


def kernel(**inputs):
    import ml_dtypes
    import concourse.bacc as bacc
    from concourse.bass_utils import run_bass_kernel_spmd

    x = {k: np.asarray(v) for k, v in inputs.items()}

    def chunked(w):
        return w.T.reshape(-1, P, w.shape[0]).transpose(1, 0, 2)

    def rope_rows(w):
        return w.reshape(QUADS, 4, 2, HD // 2, -1).transpose(0, 2, 1, 3, 4).reshape(QUADS * 256, -1)

    def index_columns(idx, n):
        out = np.zeros(n * P, idx.dtype)
        out[:idx.size] = idx
        return out.reshape(n, P).T

    qk = (NH + NKV) * HD
    w, bias = x["L0_attn_qkv_w"], x["L0_attn_qkv_b"]
    cos, sin = rope_tables()
    causal = np.arange(T)[:, None] < np.arange(T)[None, :]
    mask = np.where(causal, np.float32(NEG), np.float32(0)).astype(ml_dtypes.bfloat16)
    arrays = {
        "x": x["x"].reshape(NG, G, T, D),
        "ctx": x["ctx_512"][:, :T].reshape(NG, G, T, L),
        "wqkT": chunked(rope_rows(w[:qk])),
        "wvT": chunked(w[qk:]),
        "woT": chunked(x["L0_attn_out_w"]).reshape(P, 16 * D),
        "wxqT": chunked(x["L0_xattn_Wq"]).reshape(P, CD * D),
        "wxoT": chunked(x["L0_xattn_Wout"]).reshape(P, CD * D),
        "wkvT": np.tile(x["L0_xattn_Wkv_expand"].T, (2, 1)),
        "w_gate": x["L0_ffn_w_gate"], "w_up": x["L0_ffn_w_up"], "w_down": x["L0_ffn_w_down"],
        "bqk": rope_rows(bias[:qk]).reshape(2 * QUADS, P).T,
        "bv": np.broadcast_to(bias[qk:], (T, 512)),
        "bo": np.broadcast_to(x["L0_attn_out_b"], (T, D)),
        "sinks": np.broadcast_to(x["L0_attn_sinks"], (T, NH)),
        "idx_d": index_columns(x["L0_ffn_down_reorder_index"], FC),
        "idx_u": index_columns(x["L0_ffn_up_reorder_index"], CD),
        "cosT": np.tile(cos / np.float32(WS), (4, G)), "sinT": np.tile(sin / np.float32(WS), (4, G)),
        "id32": np.eye(P, dtype=np.float32),
        "iota": np.tile(np.arange(F, dtype=np.float32), (P, 1)),
        "maskM": np.tile(mask, (1, 4)), "maskT": np.tile(mask.T, (1, NH)),
        "idb": np.concatenate([np.eye(T), np.ones((3, T))]).astype(ml_dtypes.bfloat16),
    }
    arrays = {k: np.ascontiguousarray(v) for k, v in arrays.items()}
    nc = bacc.Bacc("TRN2", target_bir_lowering=False, num_devices=1)
    io = {k: nc.dram_tensor(f"in_{k}", v.shape, mybir.dt.from_np(v.dtype), kind="ExternalInput").ap()
          for k, v in arrays.items()}
    io["scratch"] = nc.dram_tensor("rotated_qk", (NG, QUADS, P, 4, N), F16, kind="Internal").ap()
    io["xscratch"] = nc.dram_tensor("cross_qk", (NG, 2, 2, CD, P, N), F16, kind="Internal").ap()
    io["out"] = nc.dram_tensor("out", (NG, G, T, D), F32, kind="ExternalOutput").ap()
    build(nc, io)
    r = run_bass_kernel_spmd(nc, [{f"in_{k}": v for k, v in arrays.items()}], core_ids=[0])
    return r.results[0]["out"].reshape(B, T, D)
```
